# Optimizing a Trainium2 kernel written in Bass

```python
import numpy as np
import jax
import jax.numpy as jnp

def _softmax(x, axis=-1):
    return jax.nn.softmax(x, axis=axis)

def _gelu(x):
    return jax.nn.gelu(x, approximate=True)

def _silu(x):
    return jax.nn.silu(x)

def _sigmoid(x):
    return jax.nn.sigmoid(x)

def _layernorm(x, axis=-1, eps=1e-05):
    m = jnp.mean(x, axis=axis, keepdims=True)
    v = jnp.var(x, axis=axis, keepdims=True)
    return (x - m) / jnp.sqrt(v + eps)

def _scatter_add(tgt, idx, src, axis=0):
    return tgt.at[idx].add(src)

def _segment_sum(src, seg, n):
    return jax.ops.segment_sum(src, seg, n)
kernel_name = 'mk_perceiver_d1_seqx_r8_cb468e'

def setup_inputs(seed: int=0):
    np.random.seed(seed)
    _w = jnp.asarray

    def _rec_inputs():
        import jax
        import jax.numpy as jnp
        _rk = jax.random.key(seed)
        x = 7.22e-05 + 1 * jax.random.normal(jax.random.fold_in(_rk, 1), (64, 64, 256), jnp.float32)
        _lenS = 64 - jax.random.randint(jax.random.fold_in(_rk, 7), (64,), 0, max(1, 64 // 4) + 1, jnp.int32)
        _lenS2 = 128 - jax.random.randint(jax.random.fold_in(_rk, 8), (64,), 0, max(1, 128 // 4) + 1, jnp.int32)
        _ctx_2048P = jax.random.normal(jax.random.fold_in(_rk, 11), (64, 16, 256), jnp.float32)
        _ctx_2048c = jax.random.dirichlet(jax.random.fold_in(_rk, 511), 0.3 * jnp.ones((16,), jnp.float32), (64, 128))
        _ctx_2048t = jnp.einsum('bsk,bkd->bsd', _ctx_2048c, _ctx_2048P)
        _ctx_2048t = _ctx_2048t * jax.lax.rsqrt(jnp.mean(jnp.square(_ctx_2048t)) + 1e-12) * 0.953939
        ctx_2048 = -0.000514642 + 1.00011 * (_ctx_2048t + 0.3 * jax.random.normal(jax.random.fold_in(_rk, 611), (64, 128, 256), jnp.float32))
        return (x, ctx_2048)
    x, ctx_2048 = _rec_inputs()

    def _L0_xattn_setup():
        import jax, jax.numpy as jnp
        import numpy as np
        D_MODEL = 256
        NUM_HEADS = 16
        HEAD_DIM = D_MODEL // NUM_HEADS

        def _fq_sym(x, axis):
            s = jnp.max(jnp.abs(x), axis=axis, keepdims=True) / 127.0
            s = jnp.maximum(s, 1e-08)
            q = jnp.clip(jnp.round(x / s), -127.0, 127.0) * s
            return x + jax.lax.stop_gradient(q - x)

        def _fq_unsigned(x, axis):
            s = jnp.max(x, axis=axis, keepdims=True) / 255.0
            s = jnp.maximum(s, 1e-08)
            q = jnp.clip(jnp.round(x / s), 0.0, 255.0) * s
            return x + jax.lax.stop_gradient(q - x)
        key = jax.random.key(seed)
        ks = jax.random.split(key, 8)
        B, N, M, C = (2, 256, 64, D_MODEL)
        return {'x': jax.random.normal(ks[0], (B, N, C), jnp.float32), 'cond': jax.random.normal(ks[1], (B, M, C), jnp.float32), 'Wq': jax.random.normal(ks[2], (C, C), jnp.float32) * 0.02, 'bq': jnp.zeros((C,), jnp.float32), 'Wkv': jax.random.normal(ks[3], (C, 2 * C), jnp.float32) * 0.02, 'bkv': jnp.zeros((2 * C,), jnp.float32), 'Wp': jax.random.normal(ks[4], (C, C), jnp.float32) * 0.02, 'bp': jnp.zeros((C,), jnp.float32)}
    _L0_xattn_all = _L0_xattn_setup()
    _L0_xattn_in = {k: v for k, v in _L0_xattn_all.items() if k in ('Wq', 'bq', 'Wkv', 'bkv', 'Wp', 'bp')}
    del _L0_xattn_all

    def _L0_attn_setup():
        import jax, jax.numpy as jnp
        import numpy as np
        B, T, C = (4, 256, 256)
        N, K = (16, 4)
        G, H = (N // K, C // N)

        def _rmsnorm(x):
            var = jnp.mean(jnp.square(x.astype(jnp.float32)), axis=-1, keepdims=True)
            return (x * jax.lax.rsqrt(var + 1e-06)).astype(x.dtype)

        def _sine_table(features, length, max_timescale=10000.0):
            fraction = jnp.arange(0, features, 2, dtype=jnp.float32) / features
            timescale = max_timescale ** fraction
            sinusoid = jnp.einsum('i,j->ij', jnp.arange(length).astype(jnp.float32), 1.0 / timescale, precision=jax.lax.Precision.HIGHEST)
            sinusoid = jnp.concatenate([sinusoid, sinusoid], axis=-1)
            return (jnp.sin(sinusoid), jnp.cos(sinusoid))

        def _rotate_half(x):
            x1, x2 = jnp.split(x, 2, axis=-1)
            return jnp.concatenate([-x2, x1], axis=-1)
        key = jax.random.key(seed)
        kx, kq, kk, kv, ko = jax.random.split(key, 5)
        q_std = float(np.sqrt(2.0 / (5.0 * C)))
        o_std = 2.0 / 24 / float(np.sqrt(N * H))
        return {'x': jax.random.normal(kx, (B, T, C), dtype=jnp.float32), 'Wq': jax.random.normal(kq, (C, N * H), dtype=jnp.float32) * q_std, 'Wk': jax.random.normal(kk, (C, K * H), dtype=jnp.float32) * q_std, 'Wv': jax.random.normal(kv, (C, K * H), dtype=jnp.float32) * q_std, 'Wout': jax.random.normal(ko, (N * H, C), dtype=jnp.float32) * o_std}
    _L0_attn_all = _L0_attn_setup()
    _L0_attn_in = {k: v for k, v in _L0_attn_all.items() if k in ('Wq', 'Wk', 'Wv', 'Wout')}
    del _L0_attn_all

    def _L0_ffn_setup():
        import jax, jax.numpy as jnp
        import numpy as np
        HIDDEN = 256
        N_EXPERTS = 8
        N_SHARED = 2
        TOP_K = 2
        MOE_FF = 176
        SHARED_FF = N_SHARED * MOE_FF
        SCALE = 2.5
        BATCH, SEQ = (2, 128)
        key = jax.random.key(seed)
        ks = jax.random.split(key, 8)
        s = 0.02
        return {'hidden_states': jax.random.normal(ks[0], (BATCH, SEQ, HIDDEN), jnp.float32), 'gate_w': jax.random.normal(ks[1], (N_EXPERTS, HIDDEN), jnp.float32) * s, 'shared_wg': jax.random.normal(ks[2], (SHARED_FF, HIDDEN), jnp.float32) * s, 'shared_wu': jax.random.normal(ks[3], (SHARED_FF, HIDDEN), jnp.float32) * s, 'shared_wd': jax.random.normal(ks[4], (HIDDEN, SHARED_FF), jnp.float32) * s, 'exp_wg': jax.random.normal(ks[5], (N_EXPERTS, MOE_FF, HIDDEN), jnp.float32) * s, 'exp_wu': jax.random.normal(ks[6], (N_EXPERTS, MOE_FF, HIDDEN), jnp.float32) * s, 'exp_wd': jax.random.normal(ks[7], (N_EXPERTS, HIDDEN, MOE_FF), jnp.float32) * s}
    _L0_ffn_all = _L0_ffn_setup()
    _L0_ffn_in = {k: v for k, v in _L0_ffn_all.items() if k in ('gate_w', 'shared_wg', 'shared_wu', 'shared_wd', 'exp_wg', 'exp_wu', 'exp_wd')}
    del _L0_ffn_all
    return {'x': x, 'ctx_2048': ctx_2048, 'L0_xattn_Wq': _L0_xattn_in['Wq'], 'L0_xattn_bq': _L0_xattn_in['bq'], 'L0_xattn_Wkv': _L0_xattn_in['Wkv'], 'L0_xattn_bkv': _L0_xattn_in['bkv'], 'L0_xattn_Wp': _L0_xattn_in['Wp'], 'L0_xattn_bp': _L0_xattn_in['bp'], 'L0_attn_Wq': _L0_attn_in['Wq'], 'L0_attn_Wk': _L0_attn_in['Wk'], 'L0_attn_Wv': _L0_attn_in['Wv'], 'L0_attn_Wout': _L0_attn_in['Wout'], 'L0_ffn_gate_w': _L0_ffn_in['gate_w'], 'L0_ffn_shared_wg': _L0_ffn_in['shared_wg'], 'L0_ffn_shared_wu': _L0_ffn_in['shared_wu'], 'L0_ffn_shared_wd': _L0_ffn_in['shared_wd'], 'L0_ffn_exp_wg': _L0_ffn_in['exp_wg'], 'L0_ffn_exp_wu': _L0_ffn_in['exp_wu'], 'L0_ffn_exp_wd': _L0_ffn_in['exp_wd']}

def reference(x, ctx_2048, L0_xattn_Wq, L0_xattn_bq, L0_xattn_Wkv, L0_xattn_bkv, L0_xattn_Wp, L0_xattn_bp, L0_attn_Wq, L0_attn_Wk, L0_attn_Wv, L0_attn_Wout, L0_ffn_gate_w, L0_ffn_shared_wg, L0_ffn_shared_wu, L0_ffn_shared_wd, L0_ffn_exp_wg, L0_ffn_exp_wu, L0_ffn_exp_wd):
    import jax
    import jax.numpy as jnp

    def _L0_xattn_ref(x, cond, Wq, bq, Wkv, bkv, Wp, bp):
        import jax, jax.numpy as jnp
        import numpy as np
        D_MODEL = 256
        NUM_HEADS = 16
        HEAD_DIM = D_MODEL // NUM_HEADS

        def _fq_sym(x, axis):
            s = jnp.max(jnp.abs(x), axis=axis, keepdims=True) / 127.0
            s = jnp.maximum(s, 1e-08)
            q = jnp.clip(jnp.round(x / s), -127.0, 127.0) * s
            return x + jax.lax.stop_gradient(q - x)

        def _fq_unsigned(x, axis):
            s = jnp.max(x, axis=axis, keepdims=True) / 255.0
            s = jnp.maximum(s, 1e-08)
            q = jnp.clip(jnp.round(x / s), 0.0, 255.0) * s
            return x + jax.lax.stop_gradient(q - x)
        B, N, C = x.shape
        H, hd = (NUM_HEADS, HEAD_DIM)
        q = (x @ Wq + bq).reshape(1, B * N, H, hd)
        kv = (cond @ Wkv + bkv).reshape(1, -1, 2, H, hd)
        k, v = (kv[:, :, 0], kv[:, :, 1])
        scale = 1.0 / np.sqrt(hd).astype(np.float32)
        q = jnp.transpose(q * scale, (0, 2, 1, 3))
        k = jnp.transpose(k, (0, 2, 1, 3))
        v = jnp.transpose(v, (0, 2, 1, 3))
        q = _fq_sym(q, axis=-1)
        k = _fq_sym(k, axis=-1)
        v = _fq_sym(v, axis=2)
        attn = jnp.einsum('bhqd,bhkd->bhqk', q, k)
        attn = jax.nn.softmax(attn.astype(jnp.float32), axis=-1)
        attn = _fq_unsigned(attn, axis=-1)
        out = jnp.einsum('bhqk,bhkd->bhqd', attn, v)
        out = jnp.transpose(out, (0, 2, 1, 3)).reshape(B, N, C)
        return out @ Wp + bp

    def _L0_attn_ref(x, Wq, Wk, Wv, Wout):
        import jax, jax.numpy as jnp
        import numpy as np
        B, T, C = (4, 256, 256)
        N, K = (16, 4)
        G, H = (N // K, C // N)

        def _rmsnorm(x):
            var = jnp.mean(jnp.square(x.astype(jnp.float32)), axis=-1, keepdims=True)
            return (x * jax.lax.rsqrt(var + 1e-06)).astype(x.dtype)

        def _sine_table(features, length, max_timescale=10000.0):
            fraction = jnp.arange(0, features, 2, dtype=jnp.float32) / features
            timescale = max_timescale ** fraction
            sinusoid = jnp.einsum('i,j->ij', jnp.arange(length).astype(jnp.float32), 1.0 / timescale, precision=jax.lax.Precision.HIGHEST)
            sinusoid = jnp.concatenate([sinusoid, sinusoid], axis=-1)
            return (jnp.sin(sinusoid), jnp.cos(sinusoid))

        def _rotate_half(x):
            x1, x2 = jnp.split(x, 2, axis=-1)
            return jnp.concatenate([-x2, x1], axis=-1)
        b, t, c = x.shape
        q = _rmsnorm(x @ Wq)
        k = _rmsnorm(x @ Wk)
        v = x @ Wv
        q = q.reshape(b, t, K, G, H)
        k = k.reshape(b, t, K, H)
        v = v.reshape(b, t, K, H)
        sin, cos = _sine_table(H, t)
        qcos, qsin = (cos[None, :, None, None, :], sin[None, :, None, None, :])
        kcos, ksin = (cos[None, :, None, :], sin[None, :, None, :])
        q = (q * qcos + _rotate_half(q) * qsin).astype(q.dtype)
        k = (k * kcos + _rotate_half(k) * ksin).astype(k.dtype)
        scale = jax.lax.rsqrt(jnp.array(H, dtype=jnp.float32)).astype(q.dtype)
        q = q * scale
        logits = jnp.einsum('btkgh,bskh->bkgts', q, k)
        probs = jax.nn.softmax(logits.astype(jnp.float32), axis=-1).astype(logits.dtype)
        enc = jnp.einsum('bkgts,bskh->btkgh', probs, v)
        return enc.reshape(b, t, N * H) @ Wout

    def _L0_ffn_ref(hidden_states, gate_w, shared_wg, shared_wu, shared_wd, exp_wg, exp_wu, exp_wd):
        import jax, jax.numpy as jnp
        import numpy as np
        HIDDEN = 256
        N_EXPERTS = 8
        N_SHARED = 2
        TOP_K = 2
        MOE_FF = 176
        SHARED_FF = N_SHARED * MOE_FF
        SCALE = 2.5
        BATCH, SEQ = (2, 128)
        B, S, D = hidden_states.shape
        T = B * S
        xf = hidden_states.reshape(T, D)
        scores = jax.nn.sigmoid(xf @ gate_w.T)
        topk_w, topk_idx = jax.lax.top_k(scores, TOP_K)
        topk_w = topk_w / (topk_w.sum(axis=-1, keepdims=True) + 1e-20)
        topk_w = topk_w * SCALE
        shared_out = jax.nn.silu(xf @ shared_wg.T) * (xf @ shared_wu.T) @ shared_wd.T
        h = jax.nn.silu(jnp.einsum('td,efd->etf', xf, exp_wg)) * jnp.einsum('td,efd->etf', xf, exp_wu)
        all_out = jnp.einsum('etf,edf->etd', h, exp_wd)
        picked = all_out[topk_idx, jnp.arange(T)[:, None]]
        routed_out = (topk_w[..., None] * picked).sum(axis=1)
        return (shared_out + routed_out).reshape(B, S, D)
    x = x + _L0_xattn_ref(_layernorm(x, axis=-1), ctx_2048, L0_xattn_Wq, L0_xattn_bq, L0_xattn_Wkv, L0_xattn_bkv, L0_xattn_Wp, L0_xattn_bp)
    x = x + _L0_attn_ref(_layernorm(x, axis=-1), L0_attn_Wq, L0_attn_Wk, L0_attn_Wv, L0_attn_Wout)
    x = x + _L0_ffn_ref(_layernorm(x, axis=-1), L0_ffn_gate_w, L0_ffn_shared_wg, L0_ffn_shared_wu, L0_ffn_shared_wd, L0_ffn_exp_wg, L0_ffn_exp_wu, L0_ffn_exp_wd)
    return x

_drawn_inputs = setup_inputs


def setup_inputs(seed=0):
    import zlib

    import numpy as np

    out = dict(_drawn_inputs(seed))
    spreads = {'L0_xattn_bq': (0.0, 0.8), 'L0_xattn_bkv': (0.0, 0.1), 'L0_xattn_bp': (0.0, 0.674)}
    factors = {'ctx_2048': 8.0,
     'L0_xattn_Wq': 8.0,
     'L0_xattn_Wkv': 8.0,
     'L0_attn_Wq': 18.111,
     'L0_attn_Wk': 17.775,
     'L0_attn_Wv': 4.696,
     'L0_attn_Wout': 4.659,
     'L0_ffn_shared_wg': 2.886,
     'L0_ffn_shared_wu': 2.851,
     'L0_ffn_shared_wd': 2.853,
     'L0_ffn_gate_w': 8.0,
     'L0_ffn_exp_wg': 8.0,
     'L0_ffn_exp_wu': 8.0,
     'L0_ffn_exp_wd': 8.0}
    for name, (base, spread) in spreads.items():
        noise = np.random.default_rng([zlib.crc32(name.encode()), seed]).standard_normal(out[name].shape)
        drawn = base * np.exp(spread * noise) if base else spread * noise
        out[name] = jnp.asarray(drawn.astype(out[name].dtype))
    for name, factor in factors.items():
        out[name] = (out[name] * factor).astype(out[name].dtype)
    return out
```

```python
from contextlib import ExitStack

import numpy as np

import concourse.bass as bass
from concourse import mybir

F32 = mybir.dt.float32
BF16 = mybir.dt.bfloat16
U16 = mybir.dt.uint16
ACT = mybir.ActivationFunctionType
ALU = mybir.AluOpType
AX = mybir.AxisListType

P = 128
D = 256
DC = D // P
H = 16
HD = D // H
BANK = 512
ROUND = 12582912.0
LN255 = float(np.log(255.0))
EPS_STEP = 1e-8
LN_EPS = 1e-5


def build(nc, a, out):
    NT = a["x"].shape[0] * a["x"].shape[1]
    NK = a["ctx_T"].shape[1]
    QT, KT = NT // P, NK // P
    UNITS = H * QT
    CH = 2 * BANK
    NCH = NK // CH
    PARTS = 3
    KR = PARTS * HD
    CG = 4

    x_t = a["x"].rearrange("b t d -> (b t) d").rearrange("(n p) d -> p n d", p=P)
    out_t = out.rearrange("b t d -> (b t) d").rearrange("(n p) d -> p n d", p=P)

    kT_d = nc.dram_tensor("keys_transposed", [H * KR, NK], BF16, kind="Internal").ap()
    qT_d = nc.dram_tensor("queries_transposed", [D, NT], BF16, kind="Internal").ap()

    top = ExitStack()
    with top:
        def sb(name, shape, dt, ctx=top):
            return ctx.enter_context(nc.sbuf_tensor(name, shape, dt))

        def ps(name, shape, dt, ctx):
            per_bank = BANK * 4 // mybir.dt.size(dt)
            used = int(np.prod(shape[1:]))
            whole = ctx.enter_context(nc.psum_tensor(name, [P, -(-used // per_bank) * per_bank], dt))
            names = [f"d{i}" for i in range(len(shape) - 1)]
            return whole[:, 0:used].rearrange(f"p ({' '.join(names)}) -> p {' '.join(names)}",
                                              **dict(zip(names, shape[1:])))

        def sem(name, ctx=top):
            return ctx.enter_context(nc.semaphore(name))

        x_all = sb("x_all", [P, QT, D], F32)
        ident = sb("ident", [P, P], F32)
        ident_h = sb("ident_h", [P, P], BF16)
        ones = sb("ones", [P, P], F32)
        eps = sb("eps", [P, 1], F32)
        mean_var = sb("mean_var", [P, QT, 2], F32)
        rstd = sb("rstd", [P, QT], F32)
        std = sb("std", [P, QT], F32)

        mid = ExitStack()
        att = sb("att", [P, UNITS + 1, HD], F32, mid)
        wp_sb = sb("wp_sb", [P, DC, D], F32, mid)
        wps_sb = sb("wps_sb", [P, DC, D], F32, mid)
        bp_sb = sb("bp_sb", [1, D], F32, mid)
        q_step = sb("q_step", [P, UNITS + 2], F32, mid)
        v_int = sb("v_int", [P, KT, D], BF16, mid)

        pre = ExitStack()
        wkv_sb = sb("wkv_sb", [P, DC, 2 * D], F32, pre)
        bkv_sb = sb("bkv_sb", [P, 2 * D], F32, pre)
        wq_sb = sb("wq_sb", [P, DC, D], F32, pre)
        bq_sb = sb("bq_sb", [1, D], F32, pre)
        v_f = sb("v_f", [P, KT, D], F32, pre)

        s_w = sem("weights_loaded")
        s_x = sem("x_loaded")
        s_zero = sem("constants_filled")
        s_id = sem("constants_ready")
        with nc.Block() as block:
            @block.sync
            def _(sp):
                sp.dma_start(x_all[:], x_t).then_inc(s_x, 16)
                for dst, src in ((wkv_sb, a["L0_xattn_Wkv"]), (wq_sb, a["L0_xattn_Wq"]), (wp_sb, a["L0_xattn_Wp"])):
                    sp.dma_start(dst[:], src.rearrange("(c p) n -> p c n", p=P)).then_inc(s_w, 16)
                for dst, src in ((bq_sb, a["L0_xattn_bq"]), (bp_sb, a["L0_xattn_bp"])):
                    sp.dma_start(dst[:], src.rearrange("(a n) -> a n", a=1)).then_inc(s_w, 16)
                sp.wait_ge(s_zero, 4)
                for r in range(PARTS):
                    sp.dma_start(bkv_sb[32 * r:32 * r + 1, :],
                                 a["L0_xattn_bkv"].rearrange("(a n) -> a n", a=1)).then_inc(s_w, 16)
                sp.wait_ge(s_w, 8 * 16)
                sp.wait_ge(s_x, 16)

            @block.gpsimd
            def _(pool):
                nc.gpsimd.memset(ident[:], 0.0).then_inc(s_zero, 1)
                nc.gpsimd.memset(ident_h[:], 0.0).then_inc(s_zero, 1)
                nc.gpsimd.memset(ones[:], 1.0)
                nc.gpsimd.memset(eps[:], LN_EPS).then_inc(s_zero, 1)
                nc.gpsimd.memset(bkv_sb[:], 0.0).then_inc(s_zero, 1)
                pool.wait_ge(s_zero, 4)
                for m in (ident, ident_h):
                    nc.gpsimd.affine_select(out=m[:], in_=m[:], compare_op=ALU.not_equal, fill=1.0, base=0,
                                            pattern=[[-1, P]], channel_multiplier=1).then_inc(s_id, 1)
                pool.wait_ge(s_id, 2)

        def layer_norm(which):
            with ExitStack() as ln:
                stats = sb(f"stats_{which}", [P, QT, 6], F32, ln)
                s_st = sem(f"statistics_{which}", ln)
                s_sd = sem(f"deviation_{which}", ln)
                with nc.Block() as block:
                    @block.vector
                    def _(dve):
                        for t in range(QT):
                            last = nc.vector.bn_stats(stats[:, t, :], x_all[:, t, :])
                        last.then_inc(s_st, 1)
                        dve.wait_ge(s_st, 1)
                        for t in range(QT):
                            last = nc.vector.bn_aggr(mean_var[:, t, :], stats[:, t, :])
                        last.then_inc(s_st, 1)
                        dve.wait_ge(s_sd, 1)
                        nc.vector.reciprocal(rstd[:], std[:])

                    @block.scalar
                    def _(act):
                        act.wait_ge(s_st, 2)
                        nc.scalar.activation(std[:], mean_var[:, :, 1], ACT.Sqrt, bias=eps[:]).then_inc(s_sd, 1)

        layer_norm("query")

        G = 2
        NI = KT // G
        cs = ExitStack()
        cT = [sb(f"cT{i}", [P, DC, G * P], F32, cs) for i in range(2)]
        b_low = sb("b_low", [P, 2 * D], F32, cs)
        b_mid = sb("b_mid", [P, 2 * D], BF16, cs)
        b_parts = sb("b_parts", [P, 2 * D], BF16, cs)
        ones_h = sb("ones_h", [P, P], BF16, cs)
        k_f = [sb(f"k_f{i}", [P, G, D], F32, cs) for i in range(2)]
        k_amax = sb("k_amax", [P, G, H], F32, cs)
        k_st = sb("k_st", [P, G, H], F32, cs)
        k_rst = sb("k_rst", [P, G, H], F32, cs)
        k_a = sb("k_a", [P, G, D], F32, cs)
        k_b = sb("k_b", [P, G, D], F32, cs)
        k_parts = [sb(f"k_parts{i}", [P, G, H, PARTS, HD], BF16, cs) for i in range(2)]
        KC = H * KR // P
        kT_s = [sb(f"kT_s{i}", [P, KC, G, P], BF16, cs) for i in range(2)]
        pKV = [ps(f"pKV{i}", [P, G, 2 * D], F32, cs) for i in range(2)]
        pKT = [ps(f"pKT{i}", [P, G, 2 * BANK], BF16, cs) for i in range(2)]
        s_c = [sem(f"ctx_loaded{i}", cs) for i in range(2)]
        s_bp = sem("bias_parts", cs)
        s_kv = sem("kv_ready", cs)
        s_kc = sem("keys_copied", cs)
        s_vc = sem("values_copied", cs)
        s_kch = sem("key_steps", cs)
        s_kp = sem("key_parts_ready", cs)
        s_ktp = sem("keys_transposed", cs)
        s_kts = sem("keys_transposed_copied", cs)
        s_kst = [sem(f"keys_stored{i}", cs) for i in range(2)]
        START = 2

        def after(it):
            return it + START + 1

        def heads(ap):
            return ap.rearrange("p g (h d) -> p (g h) d", d=HD)

        def spread(ap):
            return ap.rearrange("p g h -> p (g h)").unsqueeze(2).to_broadcast([P, G * H, HD])

        with nc.Block() as block:
            cT_d = a["ctx_T"].rearrange("(c p) n -> p c n", p=P)

            @block.sync
            def _(sp):
                def load(it, i):
                    sp.dma_start(cT[i][:], cT_d[:, :, bass.ds(it * G * P, G * P)]).then_inc(s_c[i], 16)
                load(0, 0)
                load(1, 1)
                with sp.Fori(0, NI // 2 - 1) as k:
                    for i in range(2):
                        it = k * 2 + i
                        sp.wait_ge(s_kv, after(it))
                        load(it + 2, i)

            @block.gpsimd
            def _(pool):
                with pool.Fori(0, NI // 2) as k:
                    for i in range(2):
                        it = k * 2 + i
                        pool.wait_ge(s_kts, after(it))
                        pool.dma_start(kT_d.rearrange("(c p) n -> p c n", p=P)[:, :, bass.ds(it * G * P, G * P)],
                                       kT_s[i][:].rearrange("p c g n -> p c (g n)")).then_inc(s_kst[i], 16)
                for i in range(2):
                    pool.wait_ge(s_kst[i], 16 * (NI // 2))

            @block.tensor
            def _(pe):
                pe.sem_inc(s_kv, START)
                pe.sem_inc(s_ktp, START)

                def project(it, k, i):
                    pe.wait_ge(s_c[i], 16 * (k + 1))
                    pe.wait_ge(s_kc, after(it - 2))
                    pe.wait_ge(s_vc, after(it - 2))
                    for g in range(G):
                        nc.tensor.matmul(pKV[i][:, g, :], ones_h[:], b_parts[:], start=True, stop=False)
                        for c in range(DC):
                            mm = nc.tensor.matmul(pKV[i][:, g, :], cT[i][:, c, g * P:(g + 1) * P], wkv_sb[:, c, :],
                                                  start=False, stop=c == DC - 1)
                    mm.then_inc(s_kv, 1)

                def turn(it, i):
                    pe.wait_ge(s_kp, after(it))
                    pe.wait_ge(s_kts, after(it - 2))
                    for g in range(G):
                        flat = k_parts[i][:, g].rearrange("p h r d -> p (h r d)")
                        for c in range(KC):
                            mm = nc.tensor.transpose(pKT[i][:, g, c * P:(c + 1) * P], flat[:, c * P:(c + 1) * P],
                                                     ident_h[:])
                    mm.then_inc(s_ktp, 1)
                pe.wait_ge(s_bp, 8)
                project(0, 0, 0)
                project(1, 0, 1)
                with pe.Fori(0, NI // 2 - 1) as k:
                    for i in range(2):
                        turn(k * 2 + i, i)
                        project(k * 2 + i + 2, k + 1, i)
                turn(NI - 2, 0)
                turn(NI - 1, 1)

            @block.scalar
            def _(act):
                act.sem_inc(s_kc, START)
                act.sem_inc(s_vc, START)
                act.sem_inc(s_kts, START)

                def copies(it, i):
                    act.wait_ge(s_kv, after(it))
                    act.wait_ge(s_kp, after(it - 2))
                    nc.scalar.copy(k_f[i][:], pKV[i][:, :, 0:D]).then_inc(s_kc, 1)
                    nc.scalar.copy(v_f[:, bass.ds(it * G, G), :], pKV[i][:, :, D:2 * D]).then_inc(s_vc, 1)

                def evacuate(it, i, stores):
                    act.wait_ge(s_ktp, after(it))
                    if stores is not None:
                        act.wait_ge(s_kst[i], 16 * stores)
                    nc.scalar.copy(kT_s[i][:].rearrange("p c g n -> p g c n"),
                                   pKT[i][:, :, 0:KC * P].rearrange("p g (c n) -> p g c n", n=P)).then_inc(s_kts, 1)
                copies(0, 0)
                copies(1, 1)
                for i in range(2):
                    evacuate(i, i, None)
                    copies(i + 2, i)
                with act.Fori(1, NI // 2 - 1) as k:
                    for i in range(2):
                        evacuate(k * 2 + i, i, k)
                        copies(k * 2 + i + 2, i)
                evacuate(NI - 2, 0, NI // 2 - 1)
                evacuate(NI - 1, 1, NI // 2 - 1)

            @block.vector
            def _(dve):
                dve.sem_inc(s_kp, START)
                Q = 32
                nc.vector.memset(ones_h[:], 1.0).then_inc(s_bp, 1)
                nc.vector.memset(b_parts[:], 0.0).then_inc(s_bp, 1)
                nc.vector.tensor_copy(b_mid[:], bkv_sb[:]).then_inc(s_bp, 1)
                dve.wait_ge(s_bp, 3)
                nc.vector.tensor_copy(b_parts[0:Q, :], b_mid[0:Q, :]).then_inc(s_bp, 1)
                nc.vector.tensor_tensor(b_low[:], bkv_sb[:], b_mid[:], ALU.subtract).then_inc(s_bp, 1)
                dve.wait_ge(s_bp, 5)
                nc.vector.tensor_copy(b_mid[:], b_low[:]).then_inc(s_bp, 1)
                dve.wait_ge(s_bp, 6)
                nc.vector.tensor_copy(b_parts[Q:2 * Q, :], b_mid[Q:2 * Q, :]).then_inc(s_bp, 1)
                nc.vector.tensor_tensor(b_parts[2 * Q:3 * Q, :], b_low[2 * Q:3 * Q, :], b_mid[2 * Q:3 * Q, :],
                                        ALU.subtract).then_inc(s_bp, 1)

                def quantise(it, i):
                    LINKS = 9
                    done = [0]

                    def link(ins):
                        done[0] += 1
                        ins.then_inc(s_kch, 1)
                        dve.wait_ge(s_kch, it * LINKS + done[0])
                    dve.wait_ge(s_kc, after(it))
                    k = heads(k_f[i][:])
                    link(nc.vector.tensor_reduce(k_amax[:], k, AX.X, ALU.max, apply_absolute_value=True))
                    link(nc.vector.tensor_scalar(k_st[:], k_amax[:], 1.0 / 127.0, EPS_STEP, ALU.mult, ALU.max))
                    link(nc.vector.reciprocal(k_rst[:], k_st[:]))
                    link(nc.vector.tensor_tensor(heads(k_a[:]), k, spread(k_rst[:]), ALU.mult))
                    link(nc.vector.tensor_scalar(k_b[:], k_a[:], ROUND, ROUND, ALU.add, ALU.subtract))
                    link(nc.vector.tensor_tensor(heads(k_a[:]), heads(k_b[:]), spread(k_st[:]), ALU.mult))
                    dve.wait_ge(s_ktp, after(it - 2))
                    part = [k_parts[i][:, :, :, r, :].rearrange("p g h d -> p (g h) d") for r in range(PARTS)]
                    link(nc.vector.tensor_copy(part[0], heads(k_a[:])))
                    link(nc.vector.tensor_tensor(heads(k_b[:]), heads(k_a[:]), part[0], ALU.subtract))
                    link(nc.vector.tensor_copy(part[1], heads(k_b[:])))
                    nc.vector.tensor_tensor(part[2], heads(k_b[:]), part[1], ALU.subtract).then_inc(s_kp, 1)
                with dve.Fori(0, NI // 2) as k:
                    for i in range(2):
                        quantise(k * 2 + i, i)
        cs.close()

        NI_Q = QT // G
        qs = ExitStack()
        xn = sb("xn", [P, G, D], F32, qs)
        xT = sb("xT", [P, G, DC, P], F32, qs)
        q_f = sb("q_f", [P, G, D], F32, qs)
        q_amax = sb("q_amax", [P, G, H], F32, qs)
        q_st = sb("q_st", [P, G, H], F32, qs)
        q_rst = sb("q_rst", [P, G, H], F32, qs)
        q_a = sb("q_a", [P, G, D], F32, qs)
        q_int = sb("q_int", [P, G, D], BF16, qs)
        qT_s = sb("qT_s", [P, DC, G, P], BF16, qs)
        pX = ps("pX", [P, G, DC, P], F32, qs)
        pQ = ps("pQ", [P, G, D], F32, qs)
        pQT = ps("pQT", [P, G, DC, P], BF16, qs)
        s_xn = sem("x_normalised", qs)
        s_xt = sem("x_transposed", qs)
        s_xc = sem("x_transposed_copied", qs)
        s_q = sem("queries_ready", qs)
        s_qc = sem("queries_copied", qs)
        s_qch = sem("query_steps", qs)
        s_qi = sem("query_integers_ready", qs)
        s_qtp = sem("queries_transposed", qs)
        s_qts = sem("queries_transposed_copied", qs)
        s_qst = sem("queries_stored", qs)
        with nc.Block() as block:
            @block.gpsimd
            def _(pool):
                for it in range(NI_Q):
                    if it > 0:
                        pool.wait_ge(s_xt, it)
                    for g in range(G):
                        t = it * G + g
                        last = nc.gpsimd.tensor_scalar(xn[:, g, :], x_all[:, t, :], mean_var[:, t, 0:1],
                                                       rstd[:, t:t + 1], ALU.subtract, ALU.mult)
                        last.then_inc(s_xn, 1)

            @block.tensor
            def _(pe):
                def project(it):
                    pe.wait_ge(s_xn, G * (it + 1))
                    pe.wait_ge(s_xc, it)
                    for g in range(G):
                        for c in range(DC):
                            mm = nc.tensor.transpose(pX[:, g, c, :], xn[:, g, c * P:(c + 1) * P], ident[:])
                    mm.then_inc(s_xt, 1)
                    pe.wait_ge(s_xc, it + 1)
                    pe.wait_ge(s_qc, it)
                    for g in range(G):
                        nc.tensor.matmul(pQ[:, g, :], ones[0:1, :], bq_sb[:], start=True, stop=False)
                        for c in range(DC):
                            mm = nc.tensor.matmul(pQ[:, g, :], xT[:, g, c, :], wq_sb[:, c, :],
                                                  start=False, stop=c == DC - 1)
                    mm.then_inc(s_q, 1)

                def turn(it):
                    pe.wait_ge(s_qi, it + 1)
                    pe.wait_ge(s_qts, it)
                    for g in range(G):
                        for c in range(DC):
                            mm = nc.tensor.transpose(pQT[:, g, c, :], q_int[:, g, c * P:(c + 1) * P], ident_h[:])
                    mm.then_inc(s_qtp, 1)
                project(0)
                with pe.Fori(1, NI_Q) as it:
                    project(it)
                    turn(it - 1)
                turn(NI_Q - 1)

            @block.scalar
            def _(act):
                def copies(it):
                    act.wait_ge(s_xt, it + 1)
                    act.wait_ge(s_q, it)
                    nc.scalar.copy(xT[:].rearrange("p g c n -> p (g c n)"),
                                   pX[:].rearrange("p g c n -> p (g c n)")).then_inc(s_xc, 1)
                    act.wait_ge(s_q, it + 1)
                    act.wait_ge(s_qi, it)
                    nc.scalar.mul(q_f[:], pQ[:], 1.0 / float(np.sqrt(HD))).then_inc(s_qc, 1)

                def evacuate(it):
                    act.wait_ge(s_qtp, it + 1)
                    act.wait_ge(s_qst, 16 * it)
                    nc.scalar.copy(qT_s[:].rearrange("p c g n -> p g c n"), pQT[:]).then_inc(s_qts, 1)
                copies(0)
                with act.Fori(1, NI_Q) as it:
                    copies(it)
                    evacuate(it - 1)
                evacuate(NI_Q - 1)

            @block.vector
            def _(dve):
                with dve.Fori(0, NI_Q) as it:
                    LINKS = 5
                    done = [0]

                    def link(ins):
                        done[0] += 1
                        ins.then_inc(s_qch, 1)
                        dve.wait_ge(s_qch, it * LINKS + done[0])
                    dve.wait_ge(s_qc, it + 1)
                    link(nc.vector.tensor_reduce(q_amax[:], heads(q_f[:]), AX.X, ALU.max, apply_absolute_value=True))
                    link(nc.vector.tensor_scalar(q_st[:], q_amax[:], 1.0 / 127.0, EPS_STEP, ALU.mult, ALU.max))
                    link(nc.vector.tensor_copy(q_step[:, 0:UNITS].rearrange("p (h t) -> p t h", h=H)
                                               [:, bass.ds(it * G, G), :], q_st[:]))
                    link(nc.vector.reciprocal(q_rst[:], q_st[:]))
                    link(nc.vector.tensor_tensor(heads(q_a[:]), heads(q_f[:]), spread(q_rst[:]), ALU.mult))
                    dve.wait_ge(s_qtp, it)
                    nc.vector.tensor_scalar(q_int[:], q_a[:], ROUND, ROUND, ALU.add, ALU.subtract).then_inc(s_qi, 1)

            @block.sync
            def _(sp):
                with sp.Fori(0, NI_Q) as it:
                    sp.wait_ge(s_qts, it + 1)
                    sp.dma_start(qT_d.rearrange("(c p) n -> p c n", p=P)[:, :, bass.ds(it * G * P, G * P)],
                                 qT_s[:].rearrange("p c g n -> p c (g n)")).then_inc(s_qst, 16)
                sp.wait_ge(s_qst, 16 * NI_Q)
        qs.close()

        vs = ExitStack()
        v_amax = sb("v_amax", [P, D], F32, vs)
        v_col = sb("v_col", [P, DC], F32, vs)
        v_step = sb("v_step", [P, DC], F32, vs)
        v_diag = sb("v_diag", [P, DC, P], F32, vs)
        v_rst = sb("v_rst", [P, D], F32, vs)
        pV = ps("pV", [P, DC, P], F32, vs)
        pVB = ps("pVB", [P, D], F32, vs)
        s_v = sem("value_steps", vs)
        s_vp = sem("value_products", vs)
        s_vi = sem("value_integers", vs)
        VB = 8
        with nc.Block() as block:
            @block.vector
            def _(dve):
                nc.vector.tensor_reduce(v_amax[:], v_f[:].rearrange("p t c -> p c t"), AX.X, ALU.max,
                                        apply_absolute_value=True).then_inc(s_v, 1)
                dve.wait_ge(s_vp, 1)
                nc.vector.tensor_reduce(v_col[:], pV[:], AX.X, ALU.max).then_inc(s_v, 1)
                dve.wait_ge(s_v, 2)
                nc.vector.tensor_scalar(v_step[:], v_col[:], 1.0 / 127.0, EPS_STEP, ALU.mult,
                                        ALU.max).then_inc(s_v, 1)
                dve.wait_ge(s_v, 3)
                for c in range(DC):
                    nc.vector.tensor_scalar(v_diag[:, c, :], ident[:], v_step[:, c:c + 1], None,
                                            ALU.mult).then_inc(s_v, 1)
                    nc.vector.tensor_scalar(wps_sb[:, c, :], wp_sb[:, c, :], v_step[:, c:c + 1], None, ALU.mult)
                dve.wait_ge(s_vp, 2)
                nc.vector.reciprocal(v_rst[:], pVB[:]).then_inc(s_v, 1)
                dve.wait_ge(s_v, 6)
                for b in range(KT // VB):
                    part = v_f[:, b * VB:(b + 1) * VB, :]
                    nc.vector.tensor_tensor(part, part, v_rst[:].unsqueeze(1).to_broadcast([P, VB, D]),
                                            ALU.mult).then_inc(s_vi, 1)
                    dve.wait_ge(s_vi, b + 1)
                    nc.vector.tensor_scalar(v_int[:, b * VB:(b + 1) * VB, :], part, ROUND, ROUND, ALU.add,
                                            ALU.subtract)

            @block.tensor
            def _(pe):
                pe.wait_ge(s_v, 1)
                for c in range(DC):
                    mm = nc.tensor.transpose(pV[:, c, :], v_amax[:, c * P:(c + 1) * P], ident[:])
                mm.then_inc(s_vp, 1)
                pe.wait_ge(s_v, 5)
                for c in range(DC):
                    mm = nc.tensor.matmul(pVB[:, c * P:(c + 1) * P], ones[:], v_diag[:, c, :], start=True, stop=True)
                mm.then_inc(s_vp, 1)
        vs.close()
        pre.close()

        RING = 3
        LAG = 2
        M = [(2 * j, 2 * j + 1) for j in range(6)] + [(b,) for b in range(12, 16)]
        NM = len(M)
        PE_STEPS = ("E0 E1 T6- AV0 M0 AV1 T7- M1 E2 E3 T0 M2 M3 T1 AV2 E4 M4 AV3 T2 M5 E5 T3 M6 E6 M7 T4 E7 M8 "
                    "FOLD M9 T5").split()
        DVE_STEPS = "C6- M0 M1 C0 M2 M3 M4 M5 C3 M6 M7 C4 M8 DEN M9 MAX INV BIAS FIN".split()
        ACT_STEPS = "E0 E1 C7- E2 E3 C1 E4 C2 E5 OC E6 E7 C5".split()
        FILLS = [x for x in PE_STEPS if x[0] in "ME"]
        AVS = sum(x[0:2] == "AV" for x in PE_STEPS)
        assert len(FILLS) == NM + NCH and len(FILLS) % RING == 0
        ON_ACT = sorted(int(x[1]) for x in ACT_STEPS if x[0] == "C")
        ON_DVE = sorted(int(x[1]) for x in DVE_STEPS if x[0] == "C")
        assert sorted(ON_ACT + ON_DVE) == list(range(NCH))
        TPC = CH // P
        LOADS_Q = 16 * 2 * PARTS
        STAGED0, STAGED = 6, 4

        xs = ExitStack()
        k_area = x_all[:].rearrange("p t d -> p (t d)").bitcast(BF16)
        k_op = [k_area[:, i * NK:(i + 1) * NK] for i in range(2)]
        q_op = [sb(f"q_op{i}", [P, NT + 2 * P], BF16, xs) for i in range(2)]
        v_op = sb("v_op", [P, KT, 32], BF16, xs)
        q_m = [sb(f"q_m{i}", [P, P], BF16, xs) for i in range(2)]
        q_e = [sb(f"q_e{i}", [P, P], BF16, xs) for i in range(2)]
        step_m = [sb(f"step_m{i}", [P, 1], F32, xs) for i in range(2)]
        step_e = [sb(f"step_e{i}", [P, 1], F32, xs) for i in range(2)]
        n_op = sb("n_op", [P, NK], U16, xs)
        nT = [sb(f"nT{i}", [P, KT, P], BF16, xs) for i in range(2)]
        m_part = [sb(f"m_part{i}", [P, NM], F32, xs) for i in range(2)]
        m_un = [sb(f"m_un{i}", [P, 1], F32, xs) for i in range(2)]
        bias = [sb(f"bias{i}", [P, 1], F32, xs) for i in range(2)]
        e_sum = [sb(f"e_sum{i}", [P, NCH], F32, xs) for i in range(2)]
        den = sb("den", [P, 1], F32, xs)
        rden = sb("rden", [P, 1], F32, xs)
        oT = sb("oT", [P, P], F32, xs)
        fold = sb("fold", [P, HD], F32, xs)
        ring = [ps(f"ring{i}", [P, CH], F32, xs) for i in range(RING)]
        pN = ps("pN", [P, CH], BF16, xs)
        pO = ps("pO", [P, P + HD], F32, xs)

        s_k = [sem(f"head_keys_loaded{i}", xs) for i in range(2)]
        s_qh = [sem(f"head_queries_loaded{i}", xs) for i in range(2)]
        s_init = sem("initialised", xs)
        s_pad = sem("operands_padded", xs)
        s_fold = sem("fold_ready", xs)
        s_un = sem("unit_staged", xs)
        s_vo = sem("head_values_staged", xs)
        s_m = sem("max_scores_ready", xs)
        s_mu = sem("max_scores_used", xs)
        s_mg = sem("unit_max_ready", xs)
        s_b = sem("bias_ready", xs)
        s_e = sem("exp_scores_ready", xs)
        s_eu = sem("exp_done", xs)
        s_t = sem("chunk_transposed", xs)
        s_td = sem("chunk_copied_by_vector", xs)
        s_ta = sem("chunk_copied_by_scalar", xs)
        s_av = sem("value_product_done", xs)
        s_oc = sem("value_product_copied", xs)
        s_of = sem("value_product_folded", xs)
        s_den = sem("denominator_ready", xs)
        s_rd = sem("reciprocal_ready", xs)
        s_fin = sem("unit_finished", xs)

        def chunks(u, j):
            return (u + 1) * NCH + j + 1

        def maxes(u, i):
            return u * NM + i + 1

        def by(who, u, j):
            return (u + 1) * len(who) + who.index(j) + 1

        def wait_copied(e, u, j):
            if j in ON_ACT:
                e.wait_ge(s_ta, by(ON_ACT, u, j))
            else:
                e.wait_ge(s_td, by(ON_DVE, u, j))

        def slot(name):
            return ring[FILLS.index(name) % RING]

        def chunk_of(x, u):
            return (u - 1, int(x[1])) if x.endswith("-") else (u, int(x[1]))

        def each_unit(eng, period):
            with eng.Fori(0, H // 2) as pair:
                for hp in range(2):
                    h = pair * 2 + hp
                    period(h * QT, pair, h, 0, hp, 0, "first")
                    with eng.Fori(0, QT // 2 - 1) as i:
                        for k in (1, 2):
                            period(h * QT + i * 2 + k, pair, h, i * 2 + k, hp, k % 2, "inner")
                    period(h * QT + QT - 1, pair, h, QT - 1, hp, 1, "last")

        with nc.Block() as block:
            @block.sync
            def _(sp):
                def load(h, i, following):
                    sp.dma_start(k_op[i][0:KR, :], kT_d[bass.ds(h * KR, KR), :]).then_inc(s_k[i], 16)
                    for r in range(PARTS):
                        rows = slice(r * HD, (r + 1) * HD)
                        sp.dma_start(q_op[i][rows, 0:NT], qT_d[bass.ds(h * HD, HD), :]).then_inc(s_qh[i], 16)
                        sp.dma_start(q_op[i][rows, NT:NT + 2 * P],
                                     qT_d[bass.ds(following * HD, HD), 0:2 * P]).then_inc(s_qh[i], 16)

                def reload(h, i, following):
                    last = (h - 1) * QT - 1
                    sp.wait_ge(s_e, chunks(last, NCH - 1))
                    sp.wait_ge(s_un, STAGED0 + STAGED * (last + 1))
                    load(h, i, following)
                sp.wait_ge(s_pad, 4)
                load(0, 0, 1)
                load(1, 1, 2)
                with sp.Fori(1, H // 2 - 1) as pair:
                    reload(pair * 2, 0, pair * 2 + 1)
                    reload(pair * 2 + 1, 1, pair * 2 + 2)
                reload(H - 2, 0, H - 1)
                reload(H - 1, 1, 0)
                sp.wait_ge(s_e, chunks((H - 1) * QT - 1, NCH - 1))
                sp.dma_start(k_op[0][0:KR, :], kT_d[0:KR, :]).then_inc(s_k[0], 16)
                sp.wait_ge(s_k[0], 16 * (H // 2 + 1))
                sp.wait_ge(s_k[1], 16 * (H // 2))
                for i in range(2):
                    sp.wait_ge(s_qh[i], LOADS_Q * (H // 2))

            @block.gpsimd
            def _(pool):
                for i in range(2):
                    nc.gpsimd.memset(k_op[i].bitcast(F32), 0.0).then_inc(s_pad, 1)
                    nc.gpsimd.memset(q_op[i][:].bitcast(F32), 0.0).then_inc(s_pad, 1)
                nc.gpsimd.memset(n_op[:, (NCH - LAG) * CH:NK], 0.0).then_inc(s_init, 1)
                nc.gpsimd.memset(nT[1][:, 0:(NCH - LAG) * TPC, :], 0.0).then_inc(s_init, 1)
                nc.gpsimd.memset(v_op[:], 0.0).then_inc(s_init, 1)
                nc.gpsimd.memset(e_sum[1][:], 1.0).then_inc(s_init, 1)
                nc.gpsimd.memset(q_step[:, UNITS:UNITS + 2], 0.0).then_inc(s_init, 1)
                pool.wait_ge(s_init, 5)

                def stage(u, t, hp, q_to, step_to):
                    nc.gpsimd.tensor_copy(step_to[:], q_step[:, bass.ds(u, 1)]).then_inc(s_un, 1)
                    nc.gpsimd.tensor_copy(q_to[:], q_op[hp][:, bass.ds(t * P, P)]).then_inc(s_un, 1)
                pool.wait_ge(s_qh[0], LOADS_Q)
                stage(0, 0, 0, q_m[0], step_m[0])
                stage(1, 1, 0, q_m[1], step_m[1])
                stage(0, 0, 0, q_e[0], step_e[0])

                def period(u, pair, h, t, hp, par, where):
                    if where == "first":
                        pool.wait_ge(s_qh[hp], LOADS_Q * (pair + 1))
                    pool.wait_ge(s_eu, chunks(u - 1, NCH - 1))
                    pool.wait_ge(s_b, u + 1)
                    stage(u + 2, t + 2, hp, q_m[par], step_m[par])
                    stage(u + 1, t + 1, hp, q_e[1 - par], step_e[1 - par])
                    if where == "first":
                        pool.wait_ge(s_av, u + 1)
                        nc.gpsimd.tensor_copy(v_op[:, :, 0:HD],
                                              v_int[:, :, bass.ds(h * HD, HD)]).then_inc(s_vo, 1)
                each_unit(pool, period)

            @block.tensor
            def _(pe):
                def scores(name, q_un, keys, ready):
                    j = int(name[1])
                    for n, b in enumerate(M[j] if name[0] == "M" else (2 * j, 2 * j + 1)):
                        mm = nc.tensor.matmul(slot(name)[:, n * BANK:(n + 1) * BANK], q_un[:],
                                              keys[:, b * BANK:(b + 1) * BANK], start=True, stop=True)
                    mm.then_inc(ready, 1)

                def fill(name, p, q_un, keys, ready):
                    at = FILLS.index(name)
                    before = FILLS[at - RING]
                    q = p if at >= RING else p - 1
                    if before[0] == "E":
                        pe.wait_ge(s_eu, chunks(q, int(before[1])))
                    else:
                        pe.wait_ge(s_mu, maxes(q + 1, int(before[1])))
                    scores(name, q_un, keys, ready)

                def transposes(u, j):
                    pe.wait_ge(s_eu, chunks(u, j))
                    wait_copied(pe, *((u, j - 1) if j else (u - 1, NCH - 1)))
                    for b in range(TPC):
                        at = j * CH + b * P
                        mm = nc.tensor.transpose(pN[:, b * P:(b + 1) * P], n_op[:, at:at + P].bitcast(BF16), ident_h[:])
                    mm.then_inc(s_t, 1)

                def value_product(u, n, buf):
                    last_copy = (n + 1) * NCH // AVS - 1
                    for who, done in ((ON_ACT, s_ta), (ON_DVE, s_td)):
                        pe.wait_ge(done, by(who, u, max(j for j in who if j <= last_copy)))
                    for b in range(n * KT // AVS, (n + 1) * KT // AVS):
                        mm = nc.tensor.matmul(pO[32 * (b % CG):32 * (b % CG) + 32, 0:P], v_op[:, b, :],
                                              nT[buf][:, b, :], start=b < CG, stop=b >= KT - CG)
                    if n == AVS - 1:
                        mm.then_inc(s_av, 1)

                def period(u, pair, h, t, hp, par, where):
                    pe.wait_ge(s_un, STAGED0 + STAGED * u)
                    if where == "last":
                        pe.wait_ge(s_k[1 - hp], 16 * (pair + 1 + hp))
                    for x in PE_STEPS:
                        if x[0] == "M":
                            fill(x, u, q_m[1 - par], k_op[1 - hp if where == "last" else hp], s_m)
                        elif x[0] == "E":
                            fill(x, u, q_e[par], k_op[hp], s_e)
                        elif x[0] == "T":
                            transposes(*chunk_of(x, u))
                        elif x[0:2] == "AV":
                            if x == "AV0":
                                pe.wait_ge(s_fin, u)
                                pe.wait_ge(s_vo, h if where == "first" else h + 1)
                            value_product(u - 1, int(x[2]), 1 - par)
                        else:
                            pe.wait_ge(s_oc, u + 1)
                            nc.tensor.matmul(pO[:, P:P + HD], oT[:], fold[:], start=True, stop=True).then_inc(s_of, 1)
                pe.sem_inc(s_e, NCH)
                pe.sem_inc(s_t, NCH - LAG)
                pe.wait_ge(s_init, 5)
                pe.wait_ge(s_fold, CG)
                pe.wait_ge(s_un, STAGED0)
                pe.wait_ge(s_k[0], 16)
                for i in range(NM):
                    if i:
                        pe.wait_ge(s_mu, i)
                    scores(f"M{i}", q_m[0], k_op[0], s_m)
                each_unit(pe, period)
                u, par = UNITS, 0
                for x in PE_STEPS:
                    if x.endswith("-"):
                        transposes(*chunk_of(x, u))
                pe.wait_ge(s_fin, u)
                for n in range(AVS):
                    value_product(u - 1, n, 1 - par)
                pe.wait_ge(s_oc, u + 1)
                nc.tensor.matmul(pO[:, P:P + HD], oT[:], fold[:], start=True, stop=True).then_inc(s_of, 1)

            @block.vector
            def _(dve):
                def chunk_max(u, i, par):
                    dve.wait_ge(s_m, maxes(u, i))
                    nc.vector.tensor_reduce(m_part[par][:, i:i + 1], slot(f"M{i}")[:, 0:len(M[i]) * BANK],
                                            AX.X, ALU.max).then_inc(s_mu, 1)

                def unit_max(u, par):
                    dve.wait_ge(s_mu, maxes(u, NM - 1))
                    nc.vector.tensor_reduce(m_un[par][:], m_part[par][:], AX.X, ALU.max, negate=True).then_inc(s_mg, 1)

                def make_bias(u, par):
                    dve.wait_ge(s_mg, u + 1)
                    nc.vector.tensor_scalar(bias[par][:], m_un[par][:], step_m[par][:], LN255, ALU.mult,
                                            ALU.add).then_inc(s_b, 1)

                def copy_chunk(u, j, buf):
                    if j == ON_DVE[0]:
                        dve.wait_ge(s_av, u)
                    dve.wait_ge(s_t, chunks(u, j))
                    nc.vector.tensor_copy(nT[buf][:, j * TPC:(j + 1) * TPC, :].rearrange("p a b -> p (a b)"),
                                          pN[:].bitcast(U16)).then_inc(s_td, 1)

                def denominator(u, buf):
                    dve.wait_ge(s_eu, chunks(u, NCH - 1))
                    dve.wait_ge(s_rd, u + 1)
                    nc.vector.tensor_reduce(den[:], e_sum[buf][:], AX.X, ALU.add).then_inc(s_den, 1)

                def invert(u):
                    dve.wait_ge(s_den, u + 2)
                    dve.wait_ge(s_fin, u + 1)
                    nc.vector.reciprocal(rden[:], den[:]).then_inc(s_rd, 1)

                def finish(u):
                    dve.wait_ge(s_of, u + 2)
                    dve.wait_ge(s_rd, u + 2)
                    nc.vector.tensor_scalar(att[:, bass.ds(u + 1, 1), :].rearrange("p a d -> p (a d)"), pO[:, P:P + HD],
                                            rden[:], None, ALU.mult).then_inc(s_fin, 1)

                def period(u, pair, h, t, hp, par, where):
                    dve.wait_ge(s_un, STAGED0 + STAGED * u)
                    for x in DVE_STEPS:
                        if x == "MAX":
                            unit_max(u + 1, 1 - par)
                        elif x == "INV":
                            invert(u - 1)
                        elif x[0] == "M":
                            chunk_max(u + 1, int(x[1]), 1 - par)
                        elif x[0] == "C":
                            copy_chunk(*chunk_of(x, u), 1 - par if x.endswith("-") else par)
                        elif x == "DEN":
                            denominator(u - 1, 1 - par)
                        elif x == "FIN":
                            finish(u - 1)
                        else:
                            make_bias(u + 1, 1 - par)
                dve.sem_inc(s_td, sum(j < NCH - LAG for j in ON_DVE))
                for g in range(CG):
                    nc.vector.tensor_copy(fold[32 * g:32 * g + 32, :],
                                          ident[32 * g:32 * g + 32, 32 * g:32 * g + HD]).then_inc(s_fold, 1)
                dve.wait_ge(s_un, STAGED0)
                for i in range(NM):
                    chunk_max(0, i, 0)
                unit_max(0, 0)
                make_bias(0, 0)
                each_unit(dve, period)
                for x in DVE_STEPS:
                    if x.endswith("-"):
                        copy_chunk(*chunk_of(x, UNITS), 1)
                denominator(UNITS - 1, 1)
                invert(UNITS - 1)
                finish(UNITS - 1)

            @block.scalar
            def _(act):
                def exponential(u, j, par):
                    if j == 0:
                        act.wait_ge(s_b, u + 1)
                        act.wait_ge(s_un, STAGED0 + STAGED * u)
                        act.wait_ge(s_den, u)
                    act.wait_ge(s_e, chunks(u, j))
                    act.wait_ge(s_t, chunks(u - 1, j))
                    nc.scalar.activation(n_op[:, j * CH:(j + 1) * CH], slot(f"E{j}")[:], ACT.Exp, bias=bias[par][:],
                                         scale=step_e[par][:], accum_out=e_sum[par][:, j:j + 1]).then_inc(s_eu, 1)

                def copy_chunk(u, j, buf):
                    if j == ON_ACT[0]:
                        act.wait_ge(s_av, u)
                    act.wait_ge(s_t, chunks(u, j))
                    nc.scalar.copy(nT[buf][:, j * TPC:(j + 1) * TPC, :].rearrange("p a b -> p (a b)"),
                                   pN[:].bitcast(U16)).then_inc(s_ta, 1)

                def copy_product(u):
                    act.wait_ge(s_av, u + 2)
                    act.wait_ge(s_of, u + 1)
                    nc.scalar.copy(oT[:], pO[:, 0:P]).then_inc(s_oc, 1)

                def period(u, pair, h, t, hp, par, where):
                    for x in ACT_STEPS:
                        if x[0] == "E":
                            exponential(u, int(x[1]), par)
                        elif x[0] == "C":
                            copy_chunk(*chunk_of(x, u), 1 - par if x.endswith("-") else par)
                        else:
                            copy_product(u - 1)
                act.sem_inc(s_eu, NCH)
                act.sem_inc(s_ta, sum(j < NCH - LAG for j in ON_ACT))
                each_unit(act, period)
                for x in ACT_STEPS:
                    if x.endswith("-"):
                        copy_chunk(*chunk_of(x, UNITS), 1)
                copy_product(UNITS - 1)
        xs.close()

        pj = ExitStack()
        a_c = sb("a_c", [P, DC, P], F32, pj)
        a_o = sb("a_o", [P, D], F32, pj)
        aT = sb("aT", [P, DC, P], F32, pj)
        pA = ps("pA", [P, DC, P], F32, pj)
        pY = ps("pY", [P, D], F32, pj)
        s_g = sem("heads_gathered", pj)
        s_at = sem("heads_transposed", pj)
        s_ac = sem("heads_transposed_copied", pj)
        s_y = sem("projected", pj)
        s_r = sem("residual_added", pj)
        s_xa = sem("x_reloaded", pj)
        with nc.Block() as block:
            @block.sync
            def _(sp):
                sp.dma_start(x_all[:], x_t).then_inc(s_xa, 16)

            @block.gpsimd
            def _(pool):
                with pool.Fori(0, QT) as t:
                    pool.wait_ge(s_at, t)
                    nc.gpsimd.tensor_copy(a_o[:].rearrange("p (h d) -> p h d", d=HD),
                                          att[:, 1:UNITS + 1, :].rearrange("p (h t) d -> p h t d", h=H)
                                          [:, :, bass.ds(t, 1), :].rearrange("p h a d -> p h (a d)")).then_inc(s_g, 1)

            @block.tensor
            def _(pe):
                with pe.Fori(0, QT) as t:
                    pe.wait_ge(s_g, t + 1)
                    pe.wait_ge(s_ac, t)
                    for c in range(DC):
                        mm = nc.tensor.transpose(pA[:, c, :], a_o[:, c * P:(c + 1) * P], ident[:])
                    mm.then_inc(s_at, 1)
                    pe.wait_ge(s_ac, t + 1)
                    pe.wait_ge(s_r, t)
                    nc.tensor.matmul(pY[:], ones[0:1, :], bp_sb[:], start=True, stop=False)
                    for c in range(DC):
                        mm = nc.tensor.matmul(pY[:], aT[:, c, :], wps_sb[:, c, :], start=False, stop=c == DC - 1)
                    mm.then_inc(s_y, 1)

            @block.scalar
            def _(act):
                with act.Fori(0, QT) as t:
                    act.wait_ge(s_at, t + 1)
                    act.wait_ge(s_y, t)
                    nc.scalar.copy(aT[:], pA[:]).then_inc(s_ac, 1)

            @block.vector
            def _(dve):
                dve.wait_ge(s_xa, 16)
                with dve.Fori(0, QT) as t:
                    row = x_all[:, bass.ds(t, 1), :].rearrange("p a d -> p (a d)")
                    dve.wait_ge(s_y, t + 1)
                    nc.vector.tensor_tensor(row, row, pY[:], ALU.add).then_inc(s_r, 1)
        pj.close()
        mid.close()

        B = 64
        NB = P // B
        KH = 4
        GH = H // KH
        KD = KH * HD
        QK = D + KD
        HC = P // HD
        RMS_EPS = 1e-6
        layer_norm("first")

        sa = ExitStack()
        wqkv_sb = sb("wqkv_sb", [P, DC, QK + KD], F32, sa)
        wo_sb = sb("wo_sb", [P, DC, D], F32, sa)
        rope = sb("rope", [P, 2, HD], F32, sa)
        qkv = sb("qkv", [P, QT, QK + KD], F32, sa)
        v_sw = sb("v_sw", [P, QT, KD], F32, sa)
        squares = sb("squares", [P, QT, 2], F32, sa)
        rms = sb("rms", [P, QT, 2], F32, sa)
        rms_r = sb("rms_r", [P, QT, 2], F32, sa)
        rms_eps = sb("rms_eps", [P, 1], F32, sa)
        head_mask = sb("head_mask", [P, HC], F32, sa)

        s1 = ExitStack()
        y_n = [sb(f"y_n{i}", [P, D], F32, s1) for i in range(2)]
        yT = [sb(f"yT{i}", [P, DC, P], F32, s1) for i in range(2)]
        sq_out = sb("sq_out", [P, D], F32, s1)
        pB = [ps(f"pB{i}", [P, DC, P], F32, s1) for i in range(2)]
        pC = [ps(f"pC{i}", [P, BANK], F32, s1) for i in range(2)]
        pS = [ps(f"pS{i}", [P, KD], F32, s1) for i in range(2)]
        s_sw = sem("self_weights_loaded", s1)
        s_yn = sem("self_normalised", s1)
        s_yt = sem("self_transposed", s1)
        s_yc = sem("self_transposed_copied", s1)
        s_pr = sem("self_projected", s1)
        s_sq = sem("self_squares", s1)
        s_cp = sem("self_projections_copied", s1)
        s_rm = sem("self_rms", s1)
        s_rs = sem("self_rms_root", s1)
        s_ep = sem("self_rms_eps_filled", s1)
        with nc.Block() as block:
            @block.sync
            def _(sp):
                at = 0
                for src in (a["L0_attn_Wq"], a["L0_attn_Wk"], a["L0_attn_Wv"]):
                    n = src.shape[1]
                    sp.dma_start(wqkv_sb[:, :, at:at + n], src.rearrange("(c p) n -> p c n", p=P)).then_inc(s_sw, 16)
                    at += n
                sp.dma_start(wo_sb[:], a["L0_attn_Wout"].rearrange("(c p) n -> p c n", p=P)).then_inc(s_sw, 16)
                sp.dma_start(rope[:], a["rope"]).then_inc(s_sw, 16)
                sp.wait_ge(s_sw, 5 * 16)

            @block.gpsimd
            def _(pool):
                nc.gpsimd.memset(rms_eps[:], RMS_EPS).then_inc(s_ep, 1)
                for t in range(QT):
                    if t >= 2:
                        pool.wait_ge(s_yt, t - 1)
                    nc.gpsimd.tensor_scalar(y_n[t % 2][:], x_all[:, t, :], mean_var[:, t, 0:1], rstd[:, t:t + 1],
                                            ALU.subtract, ALU.mult).then_inc(s_yn, 1)

            @block.tensor
            def _(pe):
                def turn(t, i):
                    pe.wait_ge(s_yn, t + 1)
                    for c in range(DC):
                        mm = nc.tensor.transpose(pB[i][:, c, :], y_n[i][:, c * P:(c + 1) * P], ident[:])
                    mm.then_inc(s_yt, 1)

                def project(t, i):
                    pe.wait_ge(s_yc, t + 1)
                    for c in range(DC):
                        nc.tensor.matmul(pC[i][:, 0:QK + KD], yT[i][:, c, :], wqkv_sb[:, c, :],
                                         start=c == 0, stop=c == DC - 1)
                    for b in range(NB):
                        for c in range(DC):
                            mm = nc.tensor.matmul(pS[i][b * B:(b + 1) * B, :],
                                                  yT[i][:, c, (1 - b) * B:(2 - b) * B],
                                                  wqkv_sb[:, c, QK:QK + KD], start=c == 0, stop=c == DC - 1)
                    mm.then_inc(s_pr, 1)
                pe.wait_ge(s_sw, 5 * 16)
                turn(0, 0)
                with pe.Fori(0, QT // 2 - 1) as k:
                    for i in range(2):
                        t = k * 2 + i
                        pe.wait_ge(s_yc, t)
                        turn(t + 1, 1 - i)
                        pe.wait_ge(s_cp, 2 * t)
                        project(t, i)
                pe.wait_ge(s_yc, QT - 2)
                turn(QT - 1, 1)
                for i in range(2):
                    pe.wait_ge(s_cp, 2 * (QT - 2 + i))
                    project(QT - 2 + i, i)

            @block.scalar
            def _(act):
                def step(t, i):
                    act.wait_ge(s_yt, t + 1)
                    nc.scalar.copy(yT[i][:], pB[i][:]).then_inc(s_yc, 1)
                    act.wait_ge(s_pr, t + 1)
                    for n, (lo, hi) in enumerate(((0, D), (D, QK))):
                        act.wait_ge(s_sq, 2 * t + n)
                        nc.scalar.activation(sq_out[:, 0:hi - lo], pC[i][:, lo:hi], ACT.Square,
                                             accum_out=squares[:, bass.ds(t, 1), n:n + 1].rearrange("p a b -> p (a b)")
                                             ).then_inc(s_sq, 1)
                with act.Fori(0, QT // 2) as k:
                    for i in range(2):
                        step(k * 2 + i, i)
                act.wait_ge(s_rm, 1)
                nc.scalar.activation(rms[:], squares[:], ACT.Sqrt, bias=rms_eps[:]).then_inc(s_rs, 1)

            @block.vector
            def _(dve):
                with dve.Fori(0, QT // 2) as k:
                    for i in range(2):
                        t = k * 2 + i
                        dve.wait_ge(s_pr, t + 1)
                        dve.wait_ge(s_sq, 2 * t + 2)
                        nc.vector.tensor_copy(qkv[:, bass.ds(t, 1), :].rearrange("p a n -> p (a n)"),
                                              pC[i][:, 0:QK + KD]).then_inc(s_cp, 1)
                        nc.vector.tensor_copy(v_sw[:, bass.ds(t, 1), :].rearrange("p a n -> p (a n)"),
                                              pS[i][:]).then_inc(s_cp, 1)
                for n, width in enumerate((D, KD)):
                    last = nc.vector.tensor_scalar(squares[:, :, n], squares[:, :, n], 1.0 / width, None, ALU.mult)
                last.then_inc(s_rm, 1)
                nc.vector.tensor_reduce(head_mask[:], ident[:].rearrange("p (h d) -> p h d", d=HD), AX.X, ALU.add)
                dve.wait_ge(s_rs, 1)
                nc.vector.reciprocal(rms_r[:], rms[:]).then_inc(s_rm, 1)
                dve.wait_ge(s_rm, 2)
                nc.vector.tensor_scalar(rms_r[:, :, 0], rms_r[:, :, 0], 1.0 / float(np.sqrt(HD)), None, ALU.mult)
                nc.vector.tensor_tensor(qkv[:, :, D:QK], qkv[:, :, D:QK],
                                        rms_r[:, :, 1:2].to_broadcast([P, QT, KD]), ALU.mult)
        s1.close()

        RT = 4
        s2 = ExitStack()
        rot = [sb(f"rot{i}", [P, RT, QK], F32, s2) for i in range(2)]
        s_ro = sem("rotated_half", s2)
        s_rc = sem("rotated_cosine", s2)
        with nc.Block() as block:
            cos, sin = rope[:, 0, :], rope[:, 1, :]
            HH = HD // 2

            @block.vector
            def _(dve):
                for n in range(QT // RT):
                    qk = qkv[:, n * RT:(n + 1) * RT, 0:QK].rearrange("p t (h d) -> p t h d", d=HD)
                    r = rot[n % 2][:].rearrange("p t (h d) -> p t h d", d=HD)
                    for half in range(2):
                        to, frm = slice(half * HH, (half + 1) * HH), slice((1 - half) * HH, (2 - half) * HH)
                        nc.vector.tensor_tensor(r[:, :, :, to], qk[:, :, :, frm],
                                                sin[:, to].unsqueeze(1).unsqueeze(1).to_broadcast(
                                                    [P, RT, QK // HD, HH]), ALU.mult).then_inc(s_ro, 1)
                    dve.wait_ge(s_ro, 2 * n + 2)
                    nc.vector.tensor_tensor(qk, qk, cos.unsqueeze(1).unsqueeze(1).to_broadcast([P, RT, QK // HD, HD]),
                                            ALU.mult).then_inc(s_rc, 1)
                    dve.wait_ge(s_rc, n + 1)
                    nc.vector.tensor_tensor(qk, qk, r, ALU.add)
        s2.close()

        s3 = ExitStack()
        k_rep = [sb(f"k_rep{i}", [P, H, HD], F32, s3) for i in range(2)]
        q_s = [sb(f"q_s{i}", [P, D], F32, s3) for i in range(2)]
        qT = [sb(f"qT{i}", [P, DC, P], F32, s3) for i in range(2)]
        kT = [sb(f"kT{i}", [P, DC, P], F32, s3) for i in range(2)]
        k_bd = sb("k_bd", [P, DC, NB, HC, B], F32, s3)
        v_bd = [sb(f"v_bd{i}", [P, NB, KH, 2, HD], F32, s3) for i in range(2)]
        l_max = sb("l_max", [P, H], F32, s3)
        l_sub = sb("l_sub", [P, H, B], F32, s3)
        prob = sb("prob", [P, H, B], F32, s3)
        p_sum = sb("p_sum", [P, H], F32, s3)
        p_rec = sb("p_rec", [P, H], F32, s3)
        pT_s = sb("pT_s", [P, H // 2, P], F32, s3)
        enc = sb("enc", [P, H, HD], F32, s3)
        eT = sb("eT", [P, DC, P], F32, s3)
        pK = ps("pK", [P, 2, DC, P], F32, s3)
        pL = ps("pL", [P, H, B], F32, s3)
        pP = ps("pP", [P, H // 2, P], F32, s3)
        pE = ps("pE", [P, D], F32, s3)
        pF = ps("pF", [P, DC, P], F32, s3)
        pG = ps("pG", [P, D], F32, s3)
        s_kr = sem("keys_repeated", s3)
        s_qk = sem("qk_transposed", s3)
        s_qkc = sem("qk_transposed_copied", s3)
        s_bd = sem("keys_placed", s3)
        s_vz = sem("values_cleared", s3)
        s_vb = sem("values_placed", s3)
        s_l = sem("logits_ready", s3)
        s_lc = sem("softmax_steps", s3)
        s_lm = sem("logit_maximum", s3)
        s_ls = sem("logits_shifted", s3)
        s_p = sem("probabilities_ready", s3)
        s_pt = sem("probabilities_transposed", s3)
        s_pc = sem("probabilities_copied", s3)
        s_en = sem("values_mixed", s3)
        s_ec = sem("mixed_normalised", s3)
        s_et = sem("mixed_transposed", s3)
        s_ect = sem("mixed_transposed_copied", s3)
        s_o = sem("self_output_ready", s3)
        s_x2 = sem("self_residual_added", s3)
        with nc.Block() as block:
            def pairs(eng, step):
                with eng.Fori(0, QT // 2) as k:
                    for i in range(2):
                        step(k * 2 + i, i)

            @block.gpsimd
            def _(pool):
                for i in range(2):
                    nc.gpsimd.memset(v_bd[i][:], 0.0).then_inc(s_vz, 1)
                pool.wait_ge(s_vz, 2)

                def step(t, i):
                    pool.wait_ge(s_qkc, t)
                    k_src = qkv[:, bass.ds(t, 1), D:QK].rearrange("p a (k d) -> p (a k) d", d=HD)
                    nc.gpsimd.tensor_copy(k_rep[i][:].rearrange("p (k g) d -> p k g d", g=GH),
                                          k_src.unsqueeze(2).to_broadcast([P, KH, GH, HD])).then_inc(s_kr, 1)
                    nc.gpsimd.tensor_copy(q_s[i][:], qkv[:, bass.ds(t, 1), 0:D].rearrange("p a n -> p (a n)")
                                          ).then_inc(s_kr, 1)
                    pool.wait_ge(s_qkc, t + 1)
                    pool.wait_ge(s_l, t)
                    for c in range(DC):
                        for b in range(NB):
                            nc.gpsimd.tensor_tensor(
                                k_bd[:, c, b], kT[i][:, c, b * B:(b + 1) * B].unsqueeze(1).to_broadcast([P, HC, B]),
                                head_mask[:].unsqueeze(2).to_broadcast([P, HC, B]), ALU.mult).then_inc(s_bd, 1)
                pairs(pool, step)

            @block.tensor
            def _(pe):
                def keys(t, i):
                    pe.wait_ge(s_kr, 2 * (t + 1))
                    pe.wait_ge(s_qkc, t)
                    for c in range(DC):
                        nc.tensor.transpose(pK[:, 0, c, :], q_s[i][:, c * P:(c + 1) * P], ident[:])
                        mm = nc.tensor.transpose(pK[:, 1, c, :], k_rep[i][:].rearrange("p h d -> p (h d)")
                                                 [:, c * P:(c + 1) * P], ident[:])
                    mm.then_inc(s_qk, 1)

                def logits(t, i):
                    pe.wait_ge(s_bd, DC * NB * (t + 1))
                    pe.wait_ge(s_ls, t)
                    for c in range(DC):
                        for b in range(NB):
                            mm = nc.tensor.matmul(pL[b * B:(b + 1) * B, c * HC:(c + 1) * HC, :],
                                                  qT[i][:, c, b * B:(b + 1) * B], k_bd[:, c, b],
                                                  start=True, stop=True)
                    mm.then_inc(s_l, 1)

                def mix(t, i):
                    pe.wait_ge(s_p, t + 1)
                    pe.wait_ge(s_pc, t)
                    for h in range(H // 2):
                        mm = nc.tensor.transpose(pP[:, h, :], prob[:, 2 * h:2 * h + 2, :].rearrange("p h s -> p (h s)"),
                                                 ident[:])
                    mm.then_inc(s_pt, 1)
                    pe.wait_ge(s_pc, t + 1)
                    pe.wait_ge(s_vb, 4 * (t + 1))
                    pe.wait_ge(s_ec, t)
                    for b in range(NB):
                        for h in range(H // 2):
                            mm = nc.tensor.matmul(pE[b * B:(b + 1) * B, 2 * h * HD:(2 * h + 2) * HD],
                                                  pT_s[:, h, b * B:(b + 1) * B],
                                                  v_bd[i][:, b, 2 * h // GH].rearrange("p a d -> p (a d)"),
                                                  start=True, stop=True)
                    mm.then_inc(s_en, 1)
                    pe.wait_ge(s_ec, t + 1)
                    pe.wait_ge(s_ect, t)
                    for c in range(DC):
                        mm = nc.tensor.transpose(pF[:, c, :], enc[:].rearrange("p h d -> p (h d)")
                                                 [:, c * P:(c + 1) * P], ident[:])
                    mm.then_inc(s_et, 1)
                    pe.wait_ge(s_ect, t + 1)
                    pe.wait_ge(s_x2, t)
                    for c in range(DC):
                        mm = nc.tensor.matmul(pG[:], eT[:, c, :], wo_sb[:, c, :], start=c == 0, stop=c == DC - 1)
                    mm.then_inc(s_o, 1)

                keys(0, 0)
                with pe.Fori(0, QT // 2 - 1) as k:
                    for i in range(2):
                        logits(k * 2 + i, i)
                        keys(k * 2 + i + 1, 1 - i)
                        mix(k * 2 + i, i)
                logits(QT - 2, 0)
                keys(QT - 1, 1)
                mix(QT - 2, 0)
                logits(QT - 1, 1)
                mix(QT - 1, 1)

            @block.scalar
            def _(act):
                def copy_keys(t, i):
                    act.wait_ge(s_qk, t + 1)
                    act.wait_ge(s_l, t)
                    nc.scalar.copy(qT[i][:], pK[:, 0])
                    nc.scalar.copy(kT[i][:], pK[:, 1]).then_inc(s_qkc, 1)

                def rest(t, i):
                    act.wait_ge(s_ls, t + 1)
                    act.wait_ge(s_pt, t)
                    act.wait_ge(s_lc, 2 * t)
                    nc.scalar.activation(prob[:], l_sub[:], ACT.Exp,
                                         scale=rms_r[:, bass.ds(t, 1), 0:1].rearrange("p a b -> p (a b)")
                                         ).then_inc(s_p, 1)
                    act.wait_ge(s_pt, t + 1)
                    act.wait_ge(s_en, t)
                    nc.scalar.copy(pT_s[:], pP[:]).then_inc(s_pc, 1)
                    act.wait_ge(s_et, t + 1)
                    act.wait_ge(s_o, t)
                    nc.scalar.copy(eT[:], pF[:]).then_inc(s_ect, 1)
                copy_keys(0, 0)
                with act.Fori(0, QT // 2 - 1) as k:
                    for i in range(2):
                        copy_keys(k * 2 + i + 1, 1 - i)
                        rest(k * 2 + i, i)
                copy_keys(QT - 1, 1)
                rest(QT - 2, 0)
                rest(QT - 1, 1)

            @block.vector
            def _(dve):
                def step(t, i):
                    own = qkv[:, bass.ds(t, 1), QK:QK + KD].rearrange("p a (k d) -> p (a k) d", d=HD)
                    other = v_sw[:, bass.ds(t, 1), :].rearrange("p a (k d) -> p (a k) d", d=HD)
                    dve.wait_ge(s_vz, 2)
                    dve.wait_ge(s_en, t)
                    for b in range(NB):
                        for half in range(2):
                            rows = slice(half * B, (half + 1) * B)
                            src = own if b == half else other
                            nc.vector.tensor_copy(v_bd[i][rows, b, :, half, :], src[rows]).then_inc(s_vb, 1)
                    dve.wait_ge(s_l, t + 1)
                    nc.vector.tensor_reduce(l_max[:], pL[:], AX.X, ALU.max).then_inc(s_lm, 1)
                    dve.wait_ge(s_lm, t + 1)
                    dve.wait_ge(s_p, t)
                    nc.vector.tensor_tensor(l_sub[:], pL[:], l_max[:].unsqueeze(2).to_broadcast([P, H, B]),
                                            ALU.subtract).then_inc(s_ls, 1)
                    dve.wait_ge(s_p, t + 1)
                    nc.vector.tensor_reduce(p_sum[:], prob[:], AX.X, ALU.add).then_inc(s_lc, 1)
                    dve.wait_ge(s_lc, 2 * t + 1)
                    nc.vector.reciprocal(p_rec[:], p_sum[:]).then_inc(s_lc, 1)
                    dve.wait_ge(s_en, t + 1)
                    dve.wait_ge(s_lc, 2 * t + 2)
                    dve.wait_ge(s_et, t)
                    nc.vector.tensor_tensor(enc[:], pE[:].rearrange("p (h d) -> p h d", d=HD),
                                            p_rec[:].unsqueeze(2).to_broadcast([P, H, HD]), ALU.mult).then_inc(s_ec, 1)
                    row = x_all[:, bass.ds(t, 1), :].rearrange("p a d -> p (a d)")
                    dve.wait_ge(s_o, t + 1)
                    nc.vector.tensor_tensor(row, row, pG[:], ALU.add).then_inc(s_x2, 1)
                pairs(dve, step)
        s3.close()
        sa.close()
        layer_norm("second")

        E = a["gate"].shape[1]
        W = a["down"].shape[0]
        NE = a["down"].shape[1] // 2
        SH = NE - E
        TB = 4
        NBLK = QT // TB
        SCALE = 2.5
        mo = ExitStack()
        wg_sb = sb("wg_sb", [P, DC, 2 * NE * W], F32, mo)
        wu_sb = sb("wu_sb", [P, DC, 2 * NE * W], F32, mo)
        wd_sb = sb("wd_sb", [W, 2 * NE, D], F32, mo)
        gate_sb = sb("gate_sb", [P, DC, E], F32, mo)
        zT = sb("zT", [P, DC, QT, P], F32, mo)
        score = sb("score", [P, QT, E], F32, mo)
        weight = sb("weight", [P, QT, NE], F32, mo)

        r1 = ExitStack()
        z_n = [sb(f"z_n{i}", [P, D], F32, r1) for i in range(2)]
        before = sb("before", [P, E, E], F32, r1)
        gt = sb("gt", [P, QT, E, E], F32, r1)
        eq = sb("eq", [P, QT, E, E], F32, r1)
        rank = sb("rank", [P, QT, E], F32, r1)
        top = sb("top", [P, QT, E], F32, r1)
        total = sb("total", [P, QT], F32, r1)
        total_r = sb("total_r", [P, QT], F32, r1)
        pZ = [ps(f"pZ{i}", [P, DC, P], F32, r1) for i in range(2)]
        pR = ps("pR", [P, QT, E], F32, r1)
        s_mw = sem("moe_weights_loaded", mo)
        s_zn = sem("moe_normalised", r1)
        s_zt = sem("moe_transposed", r1)
        s_zc = sem("moe_transposed_copied", r1)
        s_r = sem("router_logits_ready", r1)
        s_sc = sem("router_scores_ready", r1)
        s_rt = sem("router_steps", r1)
        s_bf = sem("order_mask", r1)
        with nc.Block() as block:
            @block.sync
            def _(sp):
                for dst, src in ((gate_sb, a["gate"]), (wg_sb, a["up_gate"]), (wu_sb, a["up"])):
                    sp.dma_start(dst[:], src.rearrange("(c p) n -> p c n", p=P)).then_inc(s_mw, 16)
                sp.dma_start(wd_sb[:], a["down"]).then_inc(s_mw, 16)

            @block.gpsimd
            def _(pool):
                nc.gpsimd.memset(before[:], 1.0).then_inc(s_bf, 1)
                pool.wait_ge(s_bf, 1)
                nc.gpsimd.affine_select(out=before[:], in_=before[:], compare_op=ALU.is_ge, fill=0.0, base=-1,
                                        pattern=[[1, E], [-1, E]], channel_multiplier=0).then_inc(s_bf, 1)
                for t in range(QT):
                    if t >= 2:
                        pool.wait_ge(s_zt, t - 1)
                    nc.gpsimd.tensor_scalar(z_n[t % 2][:], x_all[:, t, :], mean_var[:, t, 0:1], rstd[:, t:t + 1],
                                            ALU.subtract, ALU.mult).then_inc(s_zn, 1)

            @block.tensor
            def _(pe):
                def turn(t, i):
                    pe.wait_ge(s_zn, t + 1)
                    for c in range(DC):
                        mm = nc.tensor.transpose(pZ[i][:, c, :], z_n[i][:, c * P:(c + 1) * P], ident[:])
                    mm.then_inc(s_zt, 1)
                pe.wait_ge(s_mw, 4 * 16)
                for t in range(QT):
                    if t >= 2:
                        pe.wait_ge(s_zc, t - 1)
                    turn(t, t % 2)
                    if t >= 1:
                        pe.wait_ge(s_zc, t)
                        for c in range(DC):
                            nc.tensor.matmul(pR[:, t - 1, :], zT[:, c, t - 1, :], gate_sb[:, c, :],
                                             start=c == 0, stop=c == DC - 1)
                pe.wait_ge(s_zc, QT)
                for c in range(DC):
                    mm = nc.tensor.matmul(pR[:, QT - 1, :], zT[:, c, QT - 1, :], gate_sb[:, c, :],
                                          start=c == 0, stop=c == DC - 1)
                mm.then_inc(s_r, 1)

            @block.scalar
            def _(act):
                for t in range(QT):
                    act.wait_ge(s_zt, t + 1)
                    nc.scalar.copy(zT[:, :, t, :], pZ[t % 2][:]).then_inc(s_zc, 1)
                act.wait_ge(s_r, 1)
                nc.scalar.activation(score[:], pR[:], ACT.Sigmoid).then_inc(s_sc, 1)

            @block.vector
            def _(dve):
                done = [0]

                def link(ins):
                    done[0] += 1
                    ins.then_inc(s_rt, 1)
                    dve.wait_ge(s_rt, done[0])
                mine = score[:].unsqueeze(3).to_broadcast([P, QT, E, E])
                other = score[:].unsqueeze(2).to_broadcast([P, QT, E, E])
                dve.wait_ge(s_sc, 1)
                dve.wait_ge(s_bf, 2)
                link(nc.vector.tensor_tensor(gt[:], other, mine, ALU.is_gt))
                link(nc.vector.tensor_tensor(eq[:], other, mine, ALU.is_equal))
                link(nc.vector.tensor_tensor(eq[:], eq[:], before[:].unsqueeze(1).to_broadcast([P, QT, E, E]),
                                             ALU.mult))
                link(nc.vector.tensor_tensor(gt[:], gt[:], eq[:], ALU.add))
                link(nc.vector.tensor_reduce(rank[:], gt[:], AX.X, ALU.add))
                link(nc.vector.tensor_scalar(rank[:], rank[:], 1.5, None, ALU.is_lt))
                link(nc.vector.tensor_tensor(top[:], score[:], rank[:], ALU.mult))
                link(nc.vector.tensor_reduce(total[:], top[:], AX.X, ALU.add))
                link(nc.vector.tensor_scalar(total[:], total[:], 1e-20, None, ALU.add))
                link(nc.vector.reciprocal(total_r[:], total[:]))
                link(nc.vector.tensor_tensor(top[:], top[:], total_r[:].unsqueeze(2).to_broadcast([P, QT, E]),
                                             ALU.mult))
                nc.vector.tensor_scalar(weight[:, :, SH:NE], top[:], SCALE, None, ALU.mult)
                nc.vector.memset(weight[:, :, 0:SH], 1.0)
        r1.close()

        m2 = ExitStack()
        h_s = [sb(f"h_s{i}", [W, 2, TB * P], F32, m2) for i in range(2)]
        h_o = [sb(f"h_o{i}", [W, 2, TB * P], F32, m2) for i in range(2)]
        pGt = [ps(f"pGt{i}", [P, TB * P], F32, m2) for i in range(2)]
        pUp = [ps(f"pUp{i}", [P, TB * P], F32, m2) for i in range(2)]
        pDn = ps("pDn", [P, TB, D], F32, m2)
        s_up = sem("up_products_ready", m2)
        s_si = sem("gate_activated", m2)
        s_h = sem("hidden_ready", m2)
        s_d = sem("down_product_ready", m2)
        s_a = sem("expert_added", m2)
        s_out = sem("output_stored", m2)

        def halves(n):
            return n + 3

        with nc.Block() as block:
            @block.tensor
            def _(pe):
                def tokens(blk, c):
                    return zT[:, c, bass.ds(blk * TB, TB), :].rearrange("p t n -> p (t n)")

                def up(blk, e, i):
                    for f in range(2):
                        n = 2 * (blk * NE + e) + f
                        cols = slice((2 * e + f) * W, (2 * e + f + 1) * W)
                        pe.wait_ge(s_h, halves(n - 2))
                        for dst, w in ((pGt[f], wg_sb), (pUp[f], wu_sb)):
                            for c in range(DC):
                                mm = nc.tensor.matmul(dst[0:W, :], w[:, c, cols], tokens(blk, c),
                                                      start=c == 0, stop=c == DC - 1)
                        mm.then_inc(s_up, 1)

                def down(blk, e, i):
                    n = blk * NE + e
                    pe.wait_ge(s_h, halves(2 * n + 1))
                    pe.wait_ge(s_a, TB * n)
                    for t in range(TB):
                        for f in range(2):
                            mm = nc.tensor.matmul(pDn[:, t, :], h_o[i][:, f, t * P:(t + 1) * P],
                                                  wd_sb[:, 2 * e + f, :], start=f == 0, stop=f == 1)
                    mm.then_inc(s_d, 1)
                with pe.Fori(0, NBLK) as blk:
                    up(blk, 0, 0)
                    for e in range(1, NE):
                        up(blk, e, e % 2)
                        down(blk, e - 1, (e - 1) % 2)
                    down(blk, NE - 1, (NE - 1) % 2)

            @block.scalar
            def _(act):
                with act.Fori(0, NBLK) as blk:
                    for e in range(NE):
                        for f in range(2):
                            n = 2 * (blk * NE + e) + f
                            act.wait_ge(s_up, n + 1)
                            if e < 2:
                                act.wait_ge(s_h, halves(2 * NE * blk - 1))
                            else:
                                act.wait_ge(s_h, halves(n - 4))
                            nc.scalar.activation(h_s[e % 2][:, f, :], pGt[f][0:W, :], ACT.Silu).then_inc(s_si, 1)

            @block.vector
            def _(dve):
                def add(blk, e):
                    n = blk * NE + e
                    dve.wait_ge(s_d, n + 1)
                    for t in range(TB):
                        tile = blk * TB + t
                        row = x_all[:, bass.ds(tile, 1), :].rearrange("p a d -> p (a d)")
                        w = weight[:, bass.ds(tile, 1), e:e + 1].rearrange("p a b -> p (a b)")
                        dve.wait_ge(s_a, TB * n + t)
                        nc.vector.scalar_tensor_tensor(out=row, in0=pDn[:, t, :], scalar=w, in1=row, op0=ALU.mult,
                                                       op1=ALU.add).then_inc(s_a, 1)

                dve.sem_inc(s_h, 2)
                with dve.Fori(0, NBLK) as blk:
                    for e in range(NE):
                        for f in range(2):
                            n = 2 * (blk * NE + e) + f
                            dve.wait_ge(s_si, n + 1)
                            if e < 2:
                                dve.wait_ge(s_d, blk * NE)
                            else:
                                dve.wait_ge(s_d, blk * NE + e - 1)
                            nc.vector.tensor_tensor(h_o[e % 2][:, f, :], h_s[e % 2][:, f, :], pUp[f][0:W, :],
                                                    ALU.mult).then_inc(s_h, 1)
                        if e:
                            add(blk, e - 1)
                    add(blk, NE - 1)

            @block.sync
            def _(sp):
                with sp.Fori(0, NBLK) as blk:
                    sp.wait_ge(s_a, NE * TB * (blk + 1))
                    sp.dma_start(out_t[:, bass.ds(blk * TB, TB), :], x_all[:, bass.ds(blk * TB, TB), :]).then_inc(s_out, 16)
                sp.wait_ge(s_out, 16 * NBLK)
        m2.close()
        mo.close()


_INS = ["x", "L0_xattn_Wq", "L0_xattn_bq", "L0_xattn_Wkv", "L0_xattn_bkv", "L0_xattn_Wp", "L0_xattn_bp",
        "L0_attn_Wq", "L0_attn_Wk", "L0_attn_Wv", "L0_attn_Wout"]


def rope_table(batch=64):
    fraction = np.arange(0, HD, 2, dtype=np.float32) / np.float32(HD)
    timescale = (np.float32(10000.0) ** fraction).astype(np.float32)
    position = (np.arange(P) % batch).astype(np.float32)
    angle = position[:, None] * (np.float32(1.0) / timescale)[None, :]
    cos, sin = np.cos(angle), np.sin(angle)
    return np.stack([np.concatenate([cos, cos], 1), np.concatenate([-sin, sin], 1)], 1).astype(np.float32)


def lay_out(inputs):
    arrays = {name: np.ascontiguousarray(inputs[name]) for name in _INS}
    ctx = np.asarray(inputs["ctx_2048"])
    arrays["ctx_T"] = np.ascontiguousarray(ctx.reshape(-1, ctx.shape[-1]).T)
    arrays["rope"] = rope_table()
    arrays["gate"] = np.ascontiguousarray(np.asarray(inputs["L0_ffn_gate_w"]).T)

    def up(shared, experts):
        shared, experts = np.asarray(shared), np.asarray(experts)
        rows = np.concatenate([shared, experts.reshape(-1, experts.shape[-1])])
        return np.ascontiguousarray(rows.T)
    arrays["up_gate"] = up(inputs["L0_ffn_shared_wg"], inputs["L0_ffn_exp_wg"])
    arrays["up"] = up(inputs["L0_ffn_shared_wu"], inputs["L0_ffn_exp_wu"])
    shared, experts = np.asarray(inputs["L0_ffn_shared_wd"]), np.asarray(inputs["L0_ffn_exp_wd"])
    rows = np.concatenate([shared.T, experts.transpose(0, 2, 1).reshape(-1, experts.shape[1])])
    half = experts.shape[2] // 2
    arrays["down"] = np.ascontiguousarray(rows.reshape(-1, half, rows.shape[1]).transpose(1, 0, 2))
    return arrays


def kernel(**inputs):
    import concourse.bacc as _bacc
    from concourse.bass_utils import run_bass_kernel_spmd as _run

    nc = _bacc.Bacc("TRN2", target_bir_lowering=False, num_devices=1)
    arrays = lay_out(inputs)
    args = {n: nc.dram_tensor(f"in_{n}", v.shape, mybir.dt.from_np(v.dtype), kind="ExternalInput").ap()
            for n, v in arrays.items()}
    out = nc.dram_tensor("out_0", arrays["x"].shape, F32, kind="ExternalOutput").ap()
    build(nc, args, out)
    r = _run(nc, [{f"in_{n}": v for n, v in arrays.items()}], core_ids=[0])
    return r.results[0]["out_0"]
```

```python
from contextlib import ExitStack

import numpy as np

import concourse.bass as bass
from concourse import mybir

F32 = mybir.dt.float32
BF16 = mybir.dt.bfloat16
U16 = mybir.dt.uint16
ACT = mybir.ActivationFunctionType
ALU = mybir.AluOpType
AX = mybir.AxisListType

P = 128
D = 256
DC = D // P
H = 16
HD = D // H
BANK = 512
ROUND = 12582912.0
LN255 = float(np.log(255.0))
EPS_STEP = 1e-8
LN_EPS = 1e-5


def build(nc, a, out):
    NT = a["x"].shape[0] * a["x"].shape[1]
    NK = a["ctx_T"].shape[1]
    QT, KT = NT // P, NK // P
    UNITS = H * QT
    CH = 2 * BANK
    NCH = NK // CH
    PARTS = 3
    KR = PARTS * HD
    CG = 4

    x_t = a["x"].rearrange("b t d -> (b t) d").rearrange("(n p) d -> p n d", p=P)
    out_t = out.rearrange("b t d -> (b t) d").rearrange("(n p) d -> p n d", p=P)

    kT_d = nc.dram_tensor("keys_transposed", [H * KR, NK], BF16, kind="Internal").ap()
    qT_d = nc.dram_tensor("queries_transposed", [D, NT], BF16, kind="Internal").ap()

    top = ExitStack()
    with top:
        def sb(name, shape, dt, ctx=top):
            return ctx.enter_context(nc.sbuf_tensor(name, shape, dt))

        def ps(name, shape, dt, ctx):
            per_bank = BANK * 4 // mybir.dt.size(dt)
            used = int(np.prod(shape[1:]))
            whole = ctx.enter_context(nc.psum_tensor(name, [P, -(-used // per_bank) * per_bank], dt))
            names = [f"d{i}" for i in range(len(shape) - 1)]
            return whole[:, 0:used].rearrange(f"p ({' '.join(names)}) -> p {' '.join(names)}",
                                              **dict(zip(names, shape[1:])))

        def sem(name, ctx=top):
            return ctx.enter_context(nc.semaphore(name))

        x_all = sb("x_all", [P, QT, D], F32)
        ident = sb("ident", [P, P], F32)
        ident_h = sb("ident_h", [P, P], BF16)
        ones = sb("ones", [P, P], F32)
        eps = sb("eps", [P, 1], F32)
        mean_var = sb("mean_var", [P, QT, 2], F32)
        rstd = sb("rstd", [P, QT], F32)
        std = sb("std", [P, QT], F32)

        mid = ExitStack()
        att = sb("att", [P, UNITS + 1, HD], F32, mid)
        wp_sb = sb("wp_sb", [P, DC, D], F32, mid)
        wps_sb = sb("wps_sb", [P, DC, D], F32, mid)
        bp_sb = sb("bp_sb", [1, D], F32, mid)
        q_step = sb("q_step", [P, UNITS + 2], F32, mid)
        v_int = sb("v_int", [P, KT, D], BF16, mid)

        pre = ExitStack()
        wkv_sb = sb("wkv_sb", [P, DC, 2 * D], F32, pre)
        bkv_sb = sb("bkv_sb", [P, 2 * D], F32, pre)
        wq_sb = sb("wq_sb", [P, DC, D], F32, pre)
        bq_sb = sb("bq_sb", [1, D], F32, pre)
        v_f = sb("v_f", [P, KT, D], F32, pre)

        s_w = sem("weights_loaded")
        s_x = sem("x_loaded")
        s_zero = sem("constants_filled")
        s_id = sem("constants_ready")
        with nc.Block() as block:
            @block.sync
            def _(sp):
                sp.dma_start(x_all[:], x_t).then_inc(s_x, 16)
                for dst, src in ((wkv_sb, a["L0_xattn_Wkv"]), (wq_sb, a["L0_xattn_Wq"]), (wp_sb, a["L0_xattn_Wp"])):
                    sp.dma_start(dst[:], src.rearrange("(c p) n -> p c n", p=P)).then_inc(s_w, 16)
                for dst, src in ((bq_sb, a["L0_xattn_bq"]), (bp_sb, a["L0_xattn_bp"])):
                    sp.dma_start(dst[:], src.rearrange("(a n) -> a n", a=1)).then_inc(s_w, 16)
                sp.wait_ge(s_zero, 4)
                for r in range(PARTS):
                    sp.dma_start(bkv_sb[32 * r:32 * r + 1, :],
                                 a["L0_xattn_bkv"].rearrange("(a n) -> a n", a=1)).then_inc(s_w, 16)
                sp.wait_ge(s_w, 8 * 16)
                sp.wait_ge(s_x, 16)

            @block.gpsimd
            def _(pool):
                nc.gpsimd.memset(ident[:], 0.0).then_inc(s_zero, 1)
                nc.gpsimd.memset(ident_h[:], 0.0).then_inc(s_zero, 1)
                nc.gpsimd.memset(ones[:], 1.0)
                nc.gpsimd.memset(eps[:], LN_EPS).then_inc(s_zero, 1)
                nc.gpsimd.memset(bkv_sb[:], 0.0).then_inc(s_zero, 1)
                pool.wait_ge(s_zero, 4)
                for m in (ident, ident_h):
                    nc.gpsimd.affine_select(out=m[:], in_=m[:], compare_op=ALU.not_equal, fill=1.0, base=0,
                                            pattern=[[-1, P]], channel_multiplier=1).then_inc(s_id, 1)
                pool.wait_ge(s_id, 2)

        def layer_norm(which):
            with ExitStack() as ln:
                stats = sb(f"stats_{which}", [P, QT, 6], F32, ln)
                s_st = sem(f"statistics_{which}", ln)
                s_sd = sem(f"deviation_{which}", ln)
                with nc.Block() as block:
                    @block.vector
                    def _(dve):
                        for t in range(QT):
                            last = nc.vector.bn_stats(stats[:, t, :], x_all[:, t, :])
                        last.then_inc(s_st, 1)
                        dve.wait_ge(s_st, 1)
                        for t in range(QT):
                            last = nc.vector.bn_aggr(mean_var[:, t, :], stats[:, t, :])
                        last.then_inc(s_st, 1)
                        dve.wait_ge(s_sd, 1)
                        nc.vector.reciprocal(rstd[:], std[:])

                    @block.scalar
                    def _(act):
                        act.wait_ge(s_st, 2)
                        nc.scalar.activation(std[:], mean_var[:, :, 1], ACT.Sqrt, bias=eps[:]).then_inc(s_sd, 1)

        layer_norm("query")

        G = 2
        NI = KT // G
        cs = ExitStack()
        cT = [sb(f"cT{i}", [P, DC, G * P], F32, cs) for i in range(2)]
        b_low = sb("b_low", [P, 2 * D], F32, cs)
        b_mid = sb("b_mid", [P, 2 * D], BF16, cs)
        b_parts = sb("b_parts", [P, 2 * D], BF16, cs)
        ones_h = sb("ones_h", [P, P], BF16, cs)
        k_f = [sb(f"k_f{i}", [P, G, D], F32, cs) for i in range(2)]
        k_amax = sb("k_amax", [P, G, H], F32, cs)
        k_st = sb("k_st", [P, G, H], F32, cs)
        k_rst = sb("k_rst", [P, G, H], F32, cs)
        k_a = sb("k_a", [P, G, D], F32, cs)
        k_b = sb("k_b", [P, G, D], F32, cs)
        k_parts = [sb(f"k_parts{i}", [P, G, H, PARTS, HD], BF16, cs) for i in range(2)]
        KC = H * KR // P
        kT_s = [sb(f"kT_s{i}", [P, KC, G, P], BF16, cs) for i in range(2)]
        pKV = [ps(f"pKV{i}", [P, G, 2 * D], F32, cs) for i in range(2)]
        pKT = [ps(f"pKT{i}", [P, G, 2 * BANK], BF16, cs) for i in range(2)]
        s_c = [sem(f"ctx_loaded{i}", cs) for i in range(2)]
        s_bp = sem("bias_parts", cs)
        s_kv = sem("kv_ready", cs)
        s_kc = sem("keys_copied", cs)
        s_vc = sem("values_copied", cs)
        s_kch = sem("key_steps", cs)
        s_kp = sem("key_parts_ready", cs)
        s_ktp = sem("keys_transposed", cs)
        s_kts = sem("keys_transposed_copied", cs)
        s_kst = [sem(f"keys_stored{i}", cs) for i in range(2)]
        START = 2

        def after(it):
            return it + START + 1

        def heads(ap):
            return ap.rearrange("p g (h d) -> p (g h) d", d=HD)

        def spread(ap):
            return ap.rearrange("p g h -> p (g h)").unsqueeze(2).to_broadcast([P, G * H, HD])

        with nc.Block() as block:
            cT_d = a["ctx_T"].rearrange("(c p) n -> p c n", p=P)

            @block.sync
            def _(sp):
                def load(it, i):
                    sp.dma_start(cT[i][:], cT_d[:, :, bass.ds(it * G * P, G * P)]).then_inc(s_c[i], 16)
                load(0, 0)
                load(1, 1)
                with sp.Fori(0, NI // 2 - 1) as k:
                    for i in range(2):
                        it = k * 2 + i
                        sp.wait_ge(s_kv, after(it))
                        load(it + 2, i)

            @block.gpsimd
            def _(pool):
                with pool.Fori(0, NI // 2) as k:
                    for i in range(2):
                        it = k * 2 + i
                        pool.wait_ge(s_kts, after(it))
                        pool.dma_start(kT_d.rearrange("(c p) n -> p c n", p=P)[:, :, bass.ds(it * G * P, G * P)],
                                       kT_s[i][:].rearrange("p c g n -> p c (g n)")).then_inc(s_kst[i], 16)
                for i in range(2):
                    pool.wait_ge(s_kst[i], 16 * (NI // 2))

            @block.tensor
            def _(pe):
                pe.sem_inc(s_kv, START)
                pe.sem_inc(s_ktp, START)

                def project(it, k, i):
                    pe.wait_ge(s_c[i], 16 * (k + 1))
                    pe.wait_ge(s_kc, after(it - 2))
                    pe.wait_ge(s_vc, after(it - 2))
                    for g in range(G):
                        nc.tensor.matmul(pKV[i][:, g, :], ones_h[:], b_parts[:], start=True, stop=False)
                        for c in range(DC):
                            mm = nc.tensor.matmul(pKV[i][:, g, :], cT[i][:, c, g * P:(g + 1) * P], wkv_sb[:, c, :],
                                                  start=False, stop=c == DC - 1)
                    mm.then_inc(s_kv, 1)

                def turn(it, i):
                    pe.wait_ge(s_kp, after(it))
                    pe.wait_ge(s_kts, after(it - 2))
                    for g in range(G):
                        flat = k_parts[i][:, g].rearrange("p h r d -> p (h r d)")
                        for c in range(KC):
                            mm = nc.tensor.transpose(pKT[i][:, g, c * P:(c + 1) * P], flat[:, c * P:(c + 1) * P],
                                                     ident_h[:])
                    mm.then_inc(s_ktp, 1)
                pe.wait_ge(s_bp, 8)
                project(0, 0, 0)
                project(1, 0, 1)
                with pe.Fori(0, NI // 2 - 1) as k:
                    for i in range(2):
                        turn(k * 2 + i, i)
                        project(k * 2 + i + 2, k + 1, i)
                turn(NI - 2, 0)
                turn(NI - 1, 1)

            @block.scalar
            def _(act):
                act.sem_inc(s_kc, START)
                act.sem_inc(s_vc, START)
                act.sem_inc(s_kts, START)

                def copies(it, i):
                    act.wait_ge(s_kv, after(it))
                    act.wait_ge(s_kp, after(it - 2))
                    nc.scalar.copy(k_f[i][:], pKV[i][:, :, 0:D]).then_inc(s_kc, 1)
                    nc.scalar.copy(v_f[:, bass.ds(it * G, G), :], pKV[i][:, :, D:2 * D]).then_inc(s_vc, 1)

                def evacuate(it, i, stores):
                    act.wait_ge(s_ktp, after(it))
                    if stores is not None:
                        act.wait_ge(s_kst[i], 16 * stores)
                    nc.scalar.copy(kT_s[i][:].rearrange("p c g n -> p g c n"),
                                   pKT[i][:, :, 0:KC * P].rearrange("p g (c n) -> p g c n", n=P)).then_inc(s_kts, 1)
                copies(0, 0)
                copies(1, 1)
                for i in range(2):
                    evacuate(i, i, None)
                    copies(i + 2, i)
                with act.Fori(1, NI // 2 - 1) as k:
                    for i in range(2):
                        evacuate(k * 2 + i, i, k)
                        copies(k * 2 + i + 2, i)
                evacuate(NI - 2, 0, NI // 2 - 1)
                evacuate(NI - 1, 1, NI // 2 - 1)

            @block.vector
            def _(dve):
                dve.sem_inc(s_kp, START)
                Q = 32
                nc.vector.memset(ones_h[:], 1.0).then_inc(s_bp, 1)
                nc.vector.memset(b_parts[:], 0.0).then_inc(s_bp, 1)
                nc.vector.tensor_copy(b_mid[:], bkv_sb[:]).then_inc(s_bp, 1)
                dve.wait_ge(s_bp, 3)
                nc.vector.tensor_copy(b_parts[0:Q, :], b_mid[0:Q, :]).then_inc(s_bp, 1)
                nc.vector.tensor_tensor(b_low[:], bkv_sb[:], b_mid[:], ALU.subtract).then_inc(s_bp, 1)
                dve.wait_ge(s_bp, 5)
                nc.vector.tensor_copy(b_mid[:], b_low[:]).then_inc(s_bp, 1)
                dve.wait_ge(s_bp, 6)
                nc.vector.tensor_copy(b_parts[Q:2 * Q, :], b_mid[Q:2 * Q, :]).then_inc(s_bp, 1)
                nc.vector.tensor_tensor(b_parts[2 * Q:3 * Q, :], b_low[2 * Q:3 * Q, :], b_mid[2 * Q:3 * Q, :],
                                        ALU.subtract).then_inc(s_bp, 1)

                def quantise(it, i):
                    LINKS = 9
                    done = [0]

                    def link(ins):
                        done[0] += 1
                        ins.then_inc(s_kch, 1)
                        dve.wait_ge(s_kch, it * LINKS + done[0])
                    dve.wait_ge(s_kc, after(it))
                    k = heads(k_f[i][:])
                    link(nc.vector.tensor_reduce(k_amax[:], k, AX.X, ALU.max, apply_absolute_value=True))
                    link(nc.vector.tensor_scalar(k_st[:], k_amax[:], 1.0 / 127.0, EPS_STEP, ALU.mult, ALU.max))
                    link(nc.vector.reciprocal(k_rst[:], k_st[:]))
                    link(nc.vector.tensor_tensor(heads(k_a[:]), k, spread(k_rst[:]), ALU.mult))
                    link(nc.vector.tensor_scalar(k_b[:], k_a[:], ROUND, ROUND, ALU.add, ALU.subtract))
                    link(nc.vector.tensor_tensor(heads(k_a[:]), heads(k_b[:]), spread(k_st[:]), ALU.mult))
                    dve.wait_ge(s_ktp, after(it - 2))
                    part = [k_parts[i][:, :, :, r, :].rearrange("p g h d -> p (g h) d") for r in range(PARTS)]
                    link(nc.vector.tensor_copy(part[0], heads(k_a[:])))
                    link(nc.vector.tensor_tensor(heads(k_b[:]), heads(k_a[:]), part[0], ALU.subtract))
                    link(nc.vector.tensor_copy(part[1], heads(k_b[:])))
                    nc.vector.tensor_tensor(part[2], heads(k_b[:]), part[1], ALU.subtract).then_inc(s_kp, 1)
                with dve.Fori(0, NI // 2) as k:
                    for i in range(2):
                        quantise(k * 2 + i, i)
        cs.close()

        NI_Q = QT // G
        qs = ExitStack()
        xn = sb("xn", [P, G, D], F32, qs)
        xT = sb("xT", [P, G, DC, P], F32, qs)
        q_f = sb("q_f", [P, G, D], F32, qs)
        q_amax = sb("q_amax", [P, G, H], F32, qs)
        q_st = sb("q_st", [P, G, H], F32, qs)
        q_rst = sb("q_rst", [P, G, H], F32, qs)
        q_a = sb("q_a", [P, G, D], F32, qs)
        q_int = sb("q_int", [P, G, D], BF16, qs)
        qT_s = sb("qT_s", [P, DC, G, P], BF16, qs)
        pX = ps("pX", [P, G, DC, P], F32, qs)
        pQ = ps("pQ", [P, G, D], F32, qs)
        pQT = ps("pQT", [P, G, DC, P], BF16, qs)
        s_xn = sem("x_normalised", qs)
        s_xt = sem("x_transposed", qs)
        s_xc = sem("x_transposed_copied", qs)
        s_q = sem("queries_ready", qs)
        s_qc = sem("queries_copied", qs)
        s_qch = sem("query_steps", qs)
        s_qi = sem("query_integers_ready", qs)
        s_qtp = sem("queries_transposed", qs)
        s_qts = sem("queries_transposed_copied", qs)
        s_qst = sem("queries_stored", qs)
        with nc.Block() as block:
            @block.gpsimd
            def _(pool):
                for it in range(NI_Q):
                    if it > 0:
                        pool.wait_ge(s_xt, it)
                    for g in range(G):
                        t = it * G + g
                        last = nc.gpsimd.tensor_scalar(xn[:, g, :], x_all[:, t, :], mean_var[:, t, 0:1],
                                                       rstd[:, t:t + 1], ALU.subtract, ALU.mult)
                        last.then_inc(s_xn, 1)

            @block.tensor
            def _(pe):
                def project(it):
                    pe.wait_ge(s_xn, G * (it + 1))
                    pe.wait_ge(s_xc, it)
                    for g in range(G):
                        for c in range(DC):
                            mm = nc.tensor.transpose(pX[:, g, c, :], xn[:, g, c * P:(c + 1) * P], ident[:])
                    mm.then_inc(s_xt, 1)
                    pe.wait_ge(s_xc, it + 1)
                    pe.wait_ge(s_qc, it)
                    for g in range(G):
                        nc.tensor.matmul(pQ[:, g, :], ones[0:1, :], bq_sb[:], start=True, stop=False)
                        for c in range(DC):
                            mm = nc.tensor.matmul(pQ[:, g, :], xT[:, g, c, :], wq_sb[:, c, :],
                                                  start=False, stop=c == DC - 1)
                    mm.then_inc(s_q, 1)

                def turn(it):
                    pe.wait_ge(s_qi, it + 1)
                    pe.wait_ge(s_qts, it)
                    for g in range(G):
                        for c in range(DC):
                            mm = nc.tensor.transpose(pQT[:, g, c, :], q_int[:, g, c * P:(c + 1) * P], ident_h[:])
                    mm.then_inc(s_qtp, 1)
                project(0)
                with pe.Fori(1, NI_Q) as it:
                    project(it)
                    turn(it - 1)
                turn(NI_Q - 1)

            @block.scalar
            def _(act):
                def copies(it):
                    act.wait_ge(s_xt, it + 1)
                    act.wait_ge(s_q, it)
                    nc.scalar.copy(xT[:].rearrange("p g c n -> p (g c n)"),
                                   pX[:].rearrange("p g c n -> p (g c n)")).then_inc(s_xc, 1)
                    act.wait_ge(s_q, it + 1)
                    act.wait_ge(s_qi, it)
                    nc.scalar.mul(q_f[:], pQ[:], 1.0 / float(np.sqrt(HD))).then_inc(s_qc, 1)

                def evacuate(it):
                    act.wait_ge(s_qtp, it + 1)
                    act.wait_ge(s_qst, 16 * it)
                    nc.scalar.copy(qT_s[:].rearrange("p c g n -> p g c n"), pQT[:]).then_inc(s_qts, 1)
                copies(0)
                with act.Fori(1, NI_Q) as it:
                    copies(it)
                    evacuate(it - 1)
                evacuate(NI_Q - 1)

            @block.vector
            def _(dve):
                with dve.Fori(0, NI_Q) as it:
                    LINKS = 5
                    done = [0]

                    def link(ins):
                        done[0] += 1
                        ins.then_inc(s_qch, 1)
                        dve.wait_ge(s_qch, it * LINKS + done[0])
                    dve.wait_ge(s_qc, it + 1)
                    link(nc.vector.tensor_reduce(q_amax[:], heads(q_f[:]), AX.X, ALU.max, apply_absolute_value=True))
                    link(nc.vector.tensor_scalar(q_st[:], q_amax[:], 1.0 / 127.0, EPS_STEP, ALU.mult, ALU.max))
                    link(nc.vector.tensor_copy(q_step[:, 0:UNITS].rearrange("p (h t) -> p t h", h=H)
                                               [:, bass.ds(it * G, G), :], q_st[:]))
                    link(nc.vector.reciprocal(q_rst[:], q_st[:]))
                    link(nc.vector.tensor_tensor(heads(q_a[:]), heads(q_f[:]), spread(q_rst[:]), ALU.mult))
                    dve.wait_ge(s_qtp, it)
                    nc.vector.tensor_scalar(q_int[:], q_a[:], ROUND, ROUND, ALU.add, ALU.subtract).then_inc(s_qi, 1)

            @block.sync
            def _(sp):
                with sp.Fori(0, NI_Q) as it:
                    sp.wait_ge(s_qts, it + 1)
                    sp.dma_start(qT_d.rearrange("(c p) n -> p c n", p=P)[:, :, bass.ds(it * G * P, G * P)],
                                 qT_s[:].rearrange("p c g n -> p c (g n)")).then_inc(s_qst, 16)
                sp.wait_ge(s_qst, 16 * NI_Q)
        qs.close()

        vs = ExitStack()
        v_amax = sb("v_amax", [P, D], F32, vs)
        v_col = sb("v_col", [P, DC], F32, vs)
        v_step = sb("v_step", [P, DC], F32, vs)
        v_diag = sb("v_diag", [P, DC, P], F32, vs)
        v_rst = sb("v_rst", [P, D], F32, vs)
        pV = ps("pV", [P, DC, P], F32, vs)
        pVB = ps("pVB", [P, D], F32, vs)
        s_v = sem("value_steps", vs)
        s_vp = sem("value_products", vs)
        s_vi = sem("value_integers", vs)
        VB = 8
        with nc.Block() as block:
            @block.vector
            def _(dve):
                nc.vector.tensor_reduce(v_amax[:], v_f[:].rearrange("p t c -> p c t"), AX.X, ALU.max,
                                        apply_absolute_value=True).then_inc(s_v, 1)
                dve.wait_ge(s_vp, 1)
                nc.vector.tensor_reduce(v_col[:], pV[:], AX.X, ALU.max).then_inc(s_v, 1)
                dve.wait_ge(s_v, 2)
                nc.vector.tensor_scalar(v_step[:], v_col[:], 1.0 / 127.0, EPS_STEP, ALU.mult,
                                        ALU.max).then_inc(s_v, 1)
                dve.wait_ge(s_v, 3)
                for c in range(DC):
                    nc.vector.tensor_scalar(v_diag[:, c, :], ident[:], v_step[:, c:c + 1], None,
                                            ALU.mult).then_inc(s_v, 1)
                    nc.vector.tensor_scalar(wps_sb[:, c, :], wp_sb[:, c, :], v_step[:, c:c + 1], None, ALU.mult)
                dve.wait_ge(s_vp, 2)
                nc.vector.reciprocal(v_rst[:], pVB[:]).then_inc(s_v, 1)
                dve.wait_ge(s_v, 6)
                for b in range(KT // VB):
                    part = v_f[:, b * VB:(b + 1) * VB, :]
                    nc.vector.tensor_tensor(part, part, v_rst[:].unsqueeze(1).to_broadcast([P, VB, D]),
                                            ALU.mult).then_inc(s_vi, 1)
                    dve.wait_ge(s_vi, b + 1)
                    nc.vector.tensor_scalar(v_int[:, b * VB:(b + 1) * VB, :], part, ROUND, ROUND, ALU.add,
                                            ALU.subtract)

            @block.tensor
            def _(pe):
                pe.wait_ge(s_v, 1)
                for c in range(DC):
                    mm = nc.tensor.transpose(pV[:, c, :], v_amax[:, c * P:(c + 1) * P], ident[:])
                mm.then_inc(s_vp, 1)
                pe.wait_ge(s_v, 5)
                for c in range(DC):
                    mm = nc.tensor.matmul(pVB[:, c * P:(c + 1) * P], ones[:], v_diag[:, c, :], start=True, stop=True)
                mm.then_inc(s_vp, 1)
        vs.close()
        pre.close()

        RING = 3
        LAG = 2
        M = [(2 * j, 2 * j + 1) for j in range(6)] + [(b,) for b in range(12, 16)]
        NM = len(M)
        PE_STEPS = ("T6- E0 E1 M0 T7- T0 M1 E2 M2 T1 E3 M3 E4 T2 M4 T3 E5 M5 AV M6 M7 E6 FOLD T4 E7 M8 T5 "
                    "M9").split()
        DVE_STEPS = "M0 C7- M1 M2 C1 DEN M3 C2 INV M4 M5 M6 M7 FIN C4 M8 M9 MAX BIAS C5".split()
        ACT_STEPS = "C6- E0 E1 C0 E2 E3 E4 C3 E5 OC E6 E7".split()
        FILLS = [x for x in PE_STEPS if x[0] in "ME"]
        TURNS = [x for x in PE_STEPS if x[0] == "T" or x == "AV"]
        assert len(FILLS) == NM + NCH and len(FILLS) % RING == 0 and len(TURNS) % 2 == 1
        ON_ACT = sorted(int(x[1]) for x in ACT_STEPS if x[0] == "C")
        ON_DVE = sorted(int(x[1]) for x in DVE_STEPS if x[0] == "C")
        assert sorted(ON_ACT + ON_DVE) == list(range(NCH))
        TPC = CH // P
        LOADS_Q = 16 * 2 * PARTS
        STAGED0, STAGED = 6, 4

        xs = ExitStack()
        k_area = x_all[:].rearrange("p t d -> p (t d)").bitcast(BF16)
        k_op = [k_area[:, i * NK:(i + 1) * NK] for i in range(2)]
        q_op = [sb(f"q_op{i}", [P, NT + 2 * P], BF16, xs) for i in range(2)]
        v_op = sb("v_op", [P, KT, 32], BF16, xs)
        q_m = [sb(f"q_m{i}", [P, P], BF16, xs) for i in range(2)]
        q_e = [sb(f"q_e{i}", [P, P], BF16, xs) for i in range(2)]
        step_m = [sb(f"step_m{i}", [P, 1], F32, xs) for i in range(2)]
        step_e = [sb(f"step_e{i}", [P, 1], F32, xs) for i in range(2)]
        n_op = sb("n_op", [P, NK], U16, xs)
        nT = [sb(f"nT{i}", [P, KT, P], BF16, xs) for i in range(2)]
        m_part = [sb(f"m_part{i}", [P, NM], F32, xs) for i in range(2)]
        m_un = [sb(f"m_un{i}", [P, 1], F32, xs) for i in range(2)]
        bias = [sb(f"bias{i}", [P, 1], F32, xs) for i in range(2)]
        e_sum = [sb(f"e_sum{i}", [P, NCH], F32, xs) for i in range(2)]
        den = sb("den", [P, 1], F32, xs)
        rden = sb("rden", [P, 1], F32, xs)
        oT = sb("oT", [P, P], F32, xs)
        fold = sb("fold", [P, HD], F32, xs)
        ring = [ps(f"ring{i}", [P, CH], F32, xs) for i in range(RING)]
        turns = [ps(f"turns{i}", [P, BANK], F32, xs) for i in range(2)]

        s_k = [sem(f"head_keys_loaded{i}", xs) for i in range(2)]
        s_qh = [sem(f"head_queries_loaded{i}", xs) for i in range(2)]
        s_init = sem("initialised", xs)
        s_pad = sem("operands_padded", xs)
        s_fold = sem("fold_ready", xs)
        s_un = sem("unit_staged", xs)
        s_vo = sem("head_values_staged", xs)
        s_m = sem("max_scores_ready", xs)
        s_mu = sem("max_scores_used", xs)
        s_mg = sem("unit_max_ready", xs)
        s_b = sem("bias_ready", xs)
        s_e = sem("exp_scores_ready", xs)
        s_eu = sem("exp_done", xs)
        s_t = sem("chunk_transposed", xs)
        s_td = sem("chunk_copied_by_vector", xs)
        s_ta = sem("chunk_copied_by_scalar", xs)
        s_av = sem("value_product_done", xs)
        s_oc = sem("value_product_copied", xs)
        s_of = sem("value_product_folded", xs)
        s_den = sem("denominator_ready", xs)
        s_rd = sem("reciprocal_ready", xs)
        s_fin = sem("unit_finished", xs)

        def chunks(u, j):
            return (u + 1) * NCH + j + 1

        def maxes(u, i):
            return u * NM + i + 1

        def by(who, u, j):
            return (u + 1) * len(who) + who.index(j) + 1

        def wait_copied(e, u, j):
            if j in ON_ACT:
                e.wait_ge(s_ta, by(ON_ACT, u, j))
            else:
                e.wait_ge(s_td, by(ON_DVE, u, j))

        def slot(name):
            return ring[FILLS.index(name) % RING]

        def turn_bank(x, par):
            return turns[(TURNS.index(x) + par) % 2]

        def chunk_of(x, u):
            return (u - 1, int(x[1])) if x.endswith("-") else (u, int(x[1]))

        def each_unit(eng, period):
            with eng.Fori(0, H // 2) as pair:
                for hp in range(2):
                    h = pair * 2 + hp
                    period(h * QT, pair, h, 0, hp, 0, "first")
                    with eng.Fori(0, QT // 2 - 1) as i:
                        for k in (1, 2):
                            period(h * QT + i * 2 + k, pair, h, i * 2 + k, hp, k % 2, "inner")
                    period(h * QT + QT - 1, pair, h, QT - 1, hp, 1, "last")

        with nc.Block() as block:
            @block.sync
            def _(sp):
                def load(h, i, following):
                    sp.dma_start(k_op[i][0:KR, :], kT_d[bass.ds(h * KR, KR), :]).then_inc(s_k[i], 16)
                    for r in range(PARTS):
                        rows = slice(r * HD, (r + 1) * HD)
                        sp.dma_start(q_op[i][rows, 0:NT], qT_d[bass.ds(h * HD, HD), :]).then_inc(s_qh[i], 16)
                        sp.dma_start(q_op[i][rows, NT:NT + 2 * P],
                                     qT_d[bass.ds(following * HD, HD), 0:2 * P]).then_inc(s_qh[i], 16)

                def reload(h, i, following):
                    last = (h - 1) * QT - 1
                    sp.wait_ge(s_e, chunks(last, NCH - 1))
                    sp.wait_ge(s_un, STAGED0 + STAGED * (last + 1))
                    load(h, i, following)
                sp.wait_ge(s_pad, 4)
                load(0, 0, 1)
                load(1, 1, 2)
                with sp.Fori(1, H // 2 - 1) as pair:
                    reload(pair * 2, 0, pair * 2 + 1)
                    reload(pair * 2 + 1, 1, pair * 2 + 2)
                reload(H - 2, 0, H - 1)
                reload(H - 1, 1, 0)
                sp.wait_ge(s_e, chunks((H - 1) * QT - 1, NCH - 1))
                sp.dma_start(k_op[0][0:KR, :], kT_d[0:KR, :]).then_inc(s_k[0], 16)
                sp.wait_ge(s_k[0], 16 * (H // 2 + 1))
                sp.wait_ge(s_k[1], 16 * (H // 2))
                for i in range(2):
                    sp.wait_ge(s_qh[i], LOADS_Q * (H // 2))

            @block.gpsimd
            def _(pool):
                for i in range(2):
                    nc.gpsimd.memset(k_op[i].bitcast(F32), 0.0).then_inc(s_pad, 1)
                    nc.gpsimd.memset(q_op[i][:].bitcast(F32), 0.0).then_inc(s_pad, 1)
                nc.gpsimd.memset(n_op[:, (NCH - LAG) * CH:NK], 0.0).then_inc(s_init, 1)
                nc.gpsimd.memset(nT[1][:, 0:(NCH - LAG) * TPC, :], 0.0).then_inc(s_init, 1)
                nc.gpsimd.memset(v_op[:], 0.0).then_inc(s_init, 1)
                nc.gpsimd.memset(e_sum[1][:], 1.0).then_inc(s_init, 1)
                nc.gpsimd.memset(q_step[:, UNITS:UNITS + 2], 0.0).then_inc(s_init, 1)
                pool.wait_ge(s_init, 5)

                def stage(u, t, hp, q_to, step_to):
                    nc.gpsimd.tensor_copy(step_to[:], q_step[:, bass.ds(u, 1)]).then_inc(s_un, 1)
                    nc.gpsimd.tensor_copy(q_to[:], q_op[hp][:, bass.ds(t * P, P)]).then_inc(s_un, 1)
                pool.wait_ge(s_qh[0], LOADS_Q)
                stage(0, 0, 0, q_m[0], step_m[0])
                stage(1, 1, 0, q_m[1], step_m[1])
                stage(0, 0, 0, q_e[0], step_e[0])

                def period(u, pair, h, t, hp, par, where):
                    if where == "first":
                        pool.wait_ge(s_qh[hp], LOADS_Q * (pair + 1))
                    pool.wait_ge(s_eu, chunks(u - 1, NCH - 1))
                    pool.wait_ge(s_b, u + 1)
                    stage(u + 2, t + 2, hp, q_m[par], step_m[par])
                    stage(u + 1, t + 1, hp, q_e[1 - par], step_e[1 - par])
                    if where == "first":
                        pool.wait_ge(s_av, u + 1)
                        nc.gpsimd.tensor_copy(v_op[:, :, 0:HD],
                                              v_int[:, :, bass.ds(h * HD, HD)]).then_inc(s_vo, 1)
                each_unit(pool, period)

            @block.tensor
            def _(pe):
                def scores(name, q_un, keys, ready):
                    j = int(name[1])
                    for n, b in enumerate(M[j] if name[0] == "M" else (2 * j, 2 * j + 1)):
                        mm = nc.tensor.matmul(slot(name)[:, n * BANK:(n + 1) * BANK], q_un[:],
                                              keys[:, b * BANK:(b + 1) * BANK], start=True, stop=True)
                    mm.then_inc(ready, 1)

                def fill(name, p, q_un, keys, ready):
                    at = FILLS.index(name)
                    before = FILLS[at - RING]
                    q = p if at >= RING else p - 1
                    if before[0] == "E":
                        pe.wait_ge(s_eu, chunks(q, int(before[1])))
                    else:
                        pe.wait_ge(s_mu, maxes(q + 1, int(before[1])))
                    scores(name, q_un, keys, ready)

                def wait_turn(x, p):
                    k = TURNS.index(x) - 2
                    before, q = TURNS[k], p if k >= 0 else p - 1
                    if before == "AV":
                        pe.wait_ge(s_fin, q + 1)
                    else:
                        wait_copied(pe, *chunk_of(before, q))

                def transposes(x, p, par):
                    u, j = chunk_of(x, p)
                    pe.wait_ge(s_eu, chunks(u, j))
                    wait_turn(x, p)
                    to = turn_bank(x, par).bitcast(BF16)
                    for b in range(TPC):
                        at = j * CH + b * P
                        mm = nc.tensor.transpose(to[:, b * P:(b + 1) * P], n_op[:, at:at + P].bitcast(BF16), ident_h[:])
                    mm.then_inc(s_t, 1)

                def value_product(u, par, buf):
                    pe.wait_ge(s_ta, by(ON_ACT, u, ON_ACT[-1]))
                    pe.wait_ge(s_td, by(ON_DVE, u, ON_DVE[-1]))
                    to = turn_bank("AV", par)
                    for b in range(KT):
                        mm = nc.tensor.matmul(to[32 * (b % CG):32 * (b % CG) + 32, 0:P], v_op[:, b, :],
                                              nT[buf][:, b, :], start=b < CG, stop=b >= KT - CG)
                    mm.then_inc(s_av, 1)

                def fold_groups(u, par):
                    pe.wait_ge(s_oc, u + 2)
                    nc.tensor.matmul(turn_bank("AV", par)[:, P:P + HD], oT[:], fold[:], start=True,
                                     stop=True).then_inc(s_of, 1)

                def period(u, pair, h, t, hp, par, where):
                    pe.wait_ge(s_un, STAGED0 + STAGED * u)
                    if where == "last":
                        pe.wait_ge(s_k[1 - hp], 16 * (pair + 1 + hp))
                    for x in PE_STEPS:
                        if x[0] == "M":
                            fill(x, u, q_m[1 - par], k_op[1 - hp if where == "last" else hp], s_m)
                        elif x[0] == "E":
                            fill(x, u, q_e[par], k_op[hp], s_e)
                        elif x[0] == "T":
                            transposes(x, u, par)
                        elif x == "AV":
                            pe.wait_ge(s_vo, h if where == "first" else h + 1)
                            wait_turn(x, u)
                            value_product(u - 1, par, 1 - par)
                        else:
                            fold_groups(u - 1, par)
                pe.sem_inc(s_e, NCH)
                pe.sem_inc(s_t, NCH - LAG)
                pe.wait_ge(s_init, 5)
                pe.wait_ge(s_fold, CG)
                pe.wait_ge(s_un, STAGED0)
                pe.wait_ge(s_k[0], 16)
                for i in range(NM):
                    if i:
                        pe.wait_ge(s_mu, i)
                    scores(f"M{i}", q_m[0], k_op[0], s_m)
                each_unit(pe, period)
                for x in PE_STEPS:
                    if x.endswith("-"):
                        transposes(x, UNITS, 0)
                value_product(UNITS - 1, 0, 1)
                fold_groups(UNITS - 1, 0)

            @block.vector
            def _(dve):
                def chunk_max(u, i, par):
                    dve.wait_ge(s_m, maxes(u, i))
                    nc.vector.tensor_reduce(m_part[par][:, i:i + 1], slot(f"M{i}")[:, 0:len(M[i]) * BANK],
                                            AX.X, ALU.max).then_inc(s_mu, 1)

                def unit_max(u, par):
                    dve.wait_ge(s_mu, maxes(u, NM - 1))
                    nc.vector.tensor_reduce(m_un[par][:], m_part[par][:], AX.X, ALU.max, negate=True).then_inc(s_mg, 1)

                def make_bias(u, par):
                    dve.wait_ge(s_mg, u + 1)
                    nc.vector.tensor_scalar(bias[par][:], m_un[par][:], step_m[par][:], LN255, ALU.mult,
                                            ALU.add).then_inc(s_b, 1)

                def copy_chunk(x, p, par):
                    u, j = chunk_of(x, p)
                    buf = 1 - par if x.endswith("-") else par
                    if j == ON_DVE[0]:
                        dve.wait_ge(s_av, u)
                    dve.wait_ge(s_t, chunks(u, j))
                    nc.vector.tensor_copy(nT[buf][:, j * TPC:(j + 1) * TPC, :].rearrange("p a b -> p (a b)"),
                                          turn_bank("T" + x[1:], par).bitcast(U16)).then_inc(s_td, 1)

                def denominator(u, buf):
                    dve.wait_ge(s_eu, chunks(u, NCH - 1))
                    dve.wait_ge(s_rd, u + 1)
                    nc.vector.tensor_reduce(den[:], e_sum[buf][:], AX.X, ALU.add).then_inc(s_den, 1)

                def invert(u):
                    dve.wait_ge(s_den, u + 2)
                    dve.wait_ge(s_fin, u + 1)
                    nc.vector.reciprocal(rden[:], den[:]).then_inc(s_rd, 1)

                def finish(u, par):
                    dve.wait_ge(s_of, u + 2)
                    dve.wait_ge(s_rd, u + 2)
                    nc.vector.tensor_scalar(att[:, bass.ds(u + 1, 1), :].rearrange("p a d -> p (a d)"), turn_bank("AV", par)[:, P:P + HD],
                                            rden[:], None, ALU.mult).then_inc(s_fin, 1)

                def period(u, pair, h, t, hp, par, where):
                    dve.wait_ge(s_un, STAGED0 + STAGED * u)
                    for x in DVE_STEPS:
                        if x == "MAX":
                            unit_max(u + 1, 1 - par)
                        elif x == "INV":
                            invert(u - 1)
                        elif x[0] == "M":
                            chunk_max(u + 1, int(x[1]), 1 - par)
                        elif x[0] == "C":
                            copy_chunk(x, u, par)
                        elif x == "DEN":
                            denominator(u - 1, 1 - par)
                        elif x == "FIN":
                            finish(u - 1, par)
                        else:
                            make_bias(u + 1, 1 - par)
                dve.sem_inc(s_td, sum(j < NCH - LAG for j in ON_DVE))
                for g in range(CG):
                    nc.vector.tensor_copy(fold[32 * g:32 * g + 32, :],
                                          ident[32 * g:32 * g + 32, 32 * g:32 * g + HD]).then_inc(s_fold, 1)
                dve.wait_ge(s_un, STAGED0)
                for i in range(NM):
                    chunk_max(0, i, 0)
                unit_max(0, 0)
                make_bias(0, 0)
                each_unit(dve, period)
                for x in DVE_STEPS:
                    if x.endswith("-"):
                        copy_chunk(x, UNITS, 0)
                denominator(UNITS - 1, 1)
                invert(UNITS - 1)
                finish(UNITS - 1, 0)

            @block.scalar
            def _(act):
                def exponential(u, j, par):
                    if j == 0:
                        act.wait_ge(s_b, u + 1)
                        act.wait_ge(s_un, STAGED0 + STAGED * u)
                        act.wait_ge(s_den, u)
                    act.wait_ge(s_e, chunks(u, j))
                    act.wait_ge(s_t, chunks(u - 1, j))
                    nc.scalar.activation(n_op[:, j * CH:(j + 1) * CH], slot(f"E{j}")[:], ACT.Exp, bias=bias[par][:],
                                         scale=step_e[par][:], accum_out=e_sum[par][:, j:j + 1]).then_inc(s_eu, 1)

                def copy_chunk(x, p, par):
                    u, j = chunk_of(x, p)
                    buf = 1 - par if x.endswith("-") else par
                    if j == ON_ACT[0]:
                        act.wait_ge(s_av, u)
                    act.wait_ge(s_t, chunks(u, j))
                    nc.scalar.copy(nT[buf][:, j * TPC:(j + 1) * TPC, :].rearrange("p a b -> p (a b)"),
                                   turn_bank("T" + x[1:], par).bitcast(U16)).then_inc(s_ta, 1)

                def copy_product(u, par):
                    act.wait_ge(s_av, u + 2)
                    act.wait_ge(s_of, u + 1)
                    nc.scalar.copy(oT[:], turn_bank("AV", par)[:, 0:P]).then_inc(s_oc, 1)

                def period(u, pair, h, t, hp, par, where):
                    for x in ACT_STEPS:
                        if x[0] == "E":
                            exponential(u, int(x[1]), par)
                        elif x[0] == "C":
                            copy_chunk(x, u, par)
                        else:
                            copy_product(u - 1, par)
                act.sem_inc(s_eu, NCH)
                act.sem_inc(s_ta, sum(j < NCH - LAG for j in ON_ACT))
                each_unit(act, period)
                for x in ACT_STEPS:
                    if x.endswith("-"):
                        copy_chunk(x, UNITS, 0)
                copy_product(UNITS - 1, 0)
        xs.close()

        pj = ExitStack()
        a_c = sb("a_c", [P, DC, P], F32, pj)
        a_o = sb("a_o", [P, D], F32, pj)
        aT = sb("aT", [P, DC, P], F32, pj)
        pA = ps("pA", [P, DC, P], F32, pj)
        pY = ps("pY", [P, D], F32, pj)
        s_g = sem("heads_gathered", pj)
        s_at = sem("heads_transposed", pj)
        s_ac = sem("heads_transposed_copied", pj)
        s_y = sem("projected", pj)
        s_r = sem("residual_added", pj)
        s_xa = sem("x_reloaded", pj)
        with nc.Block() as block:
            @block.sync
            def _(sp):
                sp.dma_start(x_all[:], x_t).then_inc(s_xa, 16)

            @block.gpsimd
            def _(pool):
                with pool.Fori(0, QT) as t:
                    pool.wait_ge(s_at, t)
                    nc.gpsimd.tensor_copy(a_o[:].rearrange("p (h d) -> p h d", d=HD),
                                          att[:, 1:UNITS + 1, :].rearrange("p (h t) d -> p h t d", h=H)
                                          [:, :, bass.ds(t, 1), :].rearrange("p h a d -> p h (a d)")).then_inc(s_g, 1)

            @block.tensor
            def _(pe):
                with pe.Fori(0, QT) as t:
                    pe.wait_ge(s_g, t + 1)
                    pe.wait_ge(s_ac, t)
                    for c in range(DC):
                        mm = nc.tensor.transpose(pA[:, c, :], a_o[:, c * P:(c + 1) * P], ident[:])
                    mm.then_inc(s_at, 1)
                    pe.wait_ge(s_ac, t + 1)
                    pe.wait_ge(s_r, t)
                    nc.tensor.matmul(pY[:], ones[0:1, :], bp_sb[:], start=True, stop=False)
                    for c in range(DC):
                        mm = nc.tensor.matmul(pY[:], aT[:, c, :], wps_sb[:, c, :], start=False, stop=c == DC - 1)
                    mm.then_inc(s_y, 1)

            @block.scalar
            def _(act):
                with act.Fori(0, QT) as t:
                    act.wait_ge(s_at, t + 1)
                    act.wait_ge(s_y, t)
                    nc.scalar.copy(aT[:], pA[:]).then_inc(s_ac, 1)

            @block.vector
            def _(dve):
                dve.wait_ge(s_xa, 16)
                with dve.Fori(0, QT) as t:
                    row = x_all[:, bass.ds(t, 1), :].rearrange("p a d -> p (a d)")
                    dve.wait_ge(s_y, t + 1)
                    nc.vector.tensor_tensor(row, row, pY[:], ALU.add).then_inc(s_r, 1)
        pj.close()
        mid.close()

        B = 64
        NB = P // B
        KH = 4
        GH = H // KH
        KD = KH * HD
        QK = D + KD
        HC = P // HD
        RMS_EPS = 1e-6
        layer_norm("first")

        sa = ExitStack()
        wqkv_sb = sb("wqkv_sb", [P, DC, QK + KD], F32, sa)
        wo_sb = sb("wo_sb", [P, DC, D], F32, sa)
        rope = sb("rope", [P, 2, HD], F32, sa)
        qkv = sb("qkv", [P, QT, QK + KD], F32, sa)
        v_sw = sb("v_sw", [P, QT, KD], F32, sa)
        squares = sb("squares", [P, QT, 2], F32, sa)
        rms = sb("rms", [P, QT, 2], F32, sa)
        rms_r = sb("rms_r", [P, QT, 2], F32, sa)
        rms_eps = sb("rms_eps", [P, 1], F32, sa)
        head_mask = sb("head_mask", [P, HC], F32, sa)

        s1 = ExitStack()
        y_n = [sb(f"y_n{i}", [P, D], F32, s1) for i in range(2)]
        yT = [sb(f"yT{i}", [P, DC, P], F32, s1) for i in range(2)]
        sq_out = sb("sq_out", [P, D], F32, s1)
        pB = [ps(f"pB{i}", [P, DC, P], F32, s1) for i in range(2)]
        pC = [ps(f"pC{i}", [P, BANK], F32, s1) for i in range(2)]
        pS = [ps(f"pS{i}", [P, KD], F32, s1) for i in range(2)]
        s_sw = sem("self_weights_loaded", s1)
        s_yn = sem("self_normalised", s1)
        s_yt = sem("self_transposed", s1)
        s_yc = sem("self_transposed_copied", s1)
        s_pr = sem("self_projected", s1)
        s_sq = sem("self_squares", s1)
        s_cp = sem("self_projections_copied", s1)
        s_rm = sem("self_rms", s1)
        s_rs = sem("self_rms_root", s1)
        s_ep = sem("self_rms_eps_filled", s1)
        with nc.Block() as block:
            @block.sync
            def _(sp):
                at = 0
                for src in (a["L0_attn_Wq"], a["L0_attn_Wk"], a["L0_attn_Wv"]):
                    n = src.shape[1]
                    sp.dma_start(wqkv_sb[:, :, at:at + n], src.rearrange("(c p) n -> p c n", p=P)).then_inc(s_sw, 16)
                    at += n
                sp.dma_start(wo_sb[:], a["L0_attn_Wout"].rearrange("(c p) n -> p c n", p=P)).then_inc(s_sw, 16)
                sp.dma_start(rope[:], a["rope"]).then_inc(s_sw, 16)
                sp.wait_ge(s_sw, 5 * 16)

            @block.gpsimd
            def _(pool):
                nc.gpsimd.memset(rms_eps[:], RMS_EPS).then_inc(s_ep, 1)
                for t in range(QT):
                    if t >= 2:
                        pool.wait_ge(s_yt, t - 1)
                    nc.gpsimd.tensor_scalar(y_n[t % 2][:], x_all[:, t, :], mean_var[:, t, 0:1], rstd[:, t:t + 1],
                                            ALU.subtract, ALU.mult).then_inc(s_yn, 1)

            @block.tensor
            def _(pe):
                def turn(t, i):
                    pe.wait_ge(s_yn, t + 1)
                    for c in range(DC):
                        mm = nc.tensor.transpose(pB[i][:, c, :], y_n[i][:, c * P:(c + 1) * P], ident[:])
                    mm.then_inc(s_yt, 1)

                def project(t, i):
                    pe.wait_ge(s_yc, t + 1)
                    for c in range(DC):
                        nc.tensor.matmul(pC[i][:, 0:QK + KD], yT[i][:, c, :], wqkv_sb[:, c, :],
                                         start=c == 0, stop=c == DC - 1)
                    for b in range(NB):
                        for c in range(DC):
                            mm = nc.tensor.matmul(pS[i][b * B:(b + 1) * B, :],
                                                  yT[i][:, c, (1 - b) * B:(2 - b) * B],
                                                  wqkv_sb[:, c, QK:QK + KD], start=c == 0, stop=c == DC - 1)
                    mm.then_inc(s_pr, 1)
                pe.wait_ge(s_sw, 5 * 16)
                turn(0, 0)
                with pe.Fori(0, QT // 2 - 1) as k:
                    for i in range(2):
                        t = k * 2 + i
                        pe.wait_ge(s_yc, t)
                        turn(t + 1, 1 - i)
                        pe.wait_ge(s_cp, 2 * t)
                        project(t, i)
                pe.wait_ge(s_yc, QT - 2)
                turn(QT - 1, 1)
                for i in range(2):
                    pe.wait_ge(s_cp, 2 * (QT - 2 + i))
                    project(QT - 2 + i, i)

            @block.scalar
            def _(act):
                def step(t, i):
                    act.wait_ge(s_yt, t + 1)
                    nc.scalar.copy(yT[i][:], pB[i][:]).then_inc(s_yc, 1)
                    act.wait_ge(s_pr, t + 1)
                    for n, (lo, hi) in enumerate(((0, D), (D, QK))):
                        act.wait_ge(s_sq, 2 * t + n)
                        nc.scalar.activation(sq_out[:, 0:hi - lo], pC[i][:, lo:hi], ACT.Square,
                                             accum_out=squares[:, bass.ds(t, 1), n:n + 1].rearrange("p a b -> p (a b)")
                                             ).then_inc(s_sq, 1)
                with act.Fori(0, QT // 2) as k:
                    for i in range(2):
                        step(k * 2 + i, i)
                act.wait_ge(s_rm, 1)
                nc.scalar.activation(rms[:], squares[:], ACT.Sqrt, bias=rms_eps[:]).then_inc(s_rs, 1)

            @block.vector
            def _(dve):
                with dve.Fori(0, QT // 2) as k:
                    for i in range(2):
                        t = k * 2 + i
                        dve.wait_ge(s_pr, t + 1)
                        dve.wait_ge(s_sq, 2 * t + 2)
                        nc.vector.tensor_copy(qkv[:, bass.ds(t, 1), :].rearrange("p a n -> p (a n)"),
                                              pC[i][:, 0:QK + KD]).then_inc(s_cp, 1)
                        nc.vector.tensor_copy(v_sw[:, bass.ds(t, 1), :].rearrange("p a n -> p (a n)"),
                                              pS[i][:]).then_inc(s_cp, 1)
                for n, width in enumerate((D, KD)):
                    last = nc.vector.tensor_scalar(squares[:, :, n], squares[:, :, n], 1.0 / width, None, ALU.mult)
                last.then_inc(s_rm, 1)
                nc.vector.tensor_reduce(head_mask[:], ident[:].rearrange("p (h d) -> p h d", d=HD), AX.X, ALU.add)
                dve.wait_ge(s_rs, 1)
                nc.vector.reciprocal(rms_r[:], rms[:]).then_inc(s_rm, 1)
                dve.wait_ge(s_rm, 2)
                nc.vector.tensor_scalar(rms_r[:, :, 0], rms_r[:, :, 0], 1.0 / float(np.sqrt(HD)), None, ALU.mult)
                nc.vector.tensor_tensor(qkv[:, :, D:QK], qkv[:, :, D:QK],
                                        rms_r[:, :, 1:2].to_broadcast([P, QT, KD]), ALU.mult)
        s1.close()

        RT = 4
        s2 = ExitStack()
        rot = [sb(f"rot{i}", [P, RT, QK], F32, s2) for i in range(2)]
        s_ro = sem("rotated_half", s2)
        s_rc = sem("rotated_cosine", s2)
        with nc.Block() as block:
            cos, sin = rope[:, 0, :], rope[:, 1, :]
            HH = HD // 2

            @block.vector
            def _(dve):
                for n in range(QT // RT):
                    qk = qkv[:, n * RT:(n + 1) * RT, 0:QK].rearrange("p t (h d) -> p t h d", d=HD)
                    r = rot[n % 2][:].rearrange("p t (h d) -> p t h d", d=HD)
                    for half in range(2):
                        to, frm = slice(half * HH, (half + 1) * HH), slice((1 - half) * HH, (2 - half) * HH)
                        nc.vector.tensor_tensor(r[:, :, :, to], qk[:, :, :, frm],
                                                sin[:, to].unsqueeze(1).unsqueeze(1).to_broadcast(
                                                    [P, RT, QK // HD, HH]), ALU.mult).then_inc(s_ro, 1)
                    dve.wait_ge(s_ro, 2 * n + 2)
                    nc.vector.tensor_tensor(qk, qk, cos.unsqueeze(1).unsqueeze(1).to_broadcast([P, RT, QK // HD, HD]),
                                            ALU.mult).then_inc(s_rc, 1)
                    dve.wait_ge(s_rc, n + 1)
                    nc.vector.tensor_tensor(qk, qk, r, ALU.add)
        s2.close()

        s3 = ExitStack()
        k_rep = [sb(f"k_rep{i}", [P, H, HD], F32, s3) for i in range(2)]
        q_s = [sb(f"q_s{i}", [P, D], F32, s3) for i in range(2)]
        qT = [sb(f"qT{i}", [P, DC, P], F32, s3) for i in range(2)]
        kT = [sb(f"kT{i}", [P, DC, P], F32, s3) for i in range(2)]
        k_bd = [sb(f"k_bd{i}", [P, DC, NB, HC, B], F32, s3) for i in range(2)]
        v_bd = [sb(f"v_bd{i}", [P, NB, KH, 2, HD], F32, s3) for i in range(2)]
        l_max = sb("l_max", [P, H], F32, s3)
        l_sub = [sb(f"l_sub{i}", [P, H, B], F32, s3) for i in range(2)]
        prob = [sb(f"prob{i}", [P, H, B], F32, s3) for i in range(2)]
        p_sum = sb("p_sum", [P, H], F32, s3)
        p_rec = sb("p_rec", [P, H], F32, s3)
        pT_s = sb("pT_s", [P, H // 2, P], F32, s3)
        enc = sb("enc", [P, H, HD], F32, s3)
        eT = sb("eT", [P, DC, P], F32, s3)
        pK = ps("pK", [P, 2, DC, P], F32, s3)
        pL = [ps(f"pL{i}", [P, H, B], F32, s3) for i in range(2)]
        pP = ps("pP", [P, H // 2, P], F32, s3)
        p_last = ps("p_last", [P, 2, D], F32, s3)
        pE, pF, pG = p_last[:, 0, :], p_last[:, 1, :].rearrange("p (c n) -> p c n", n=P), p_last[:, 0, :]
        s_kr = sem("tile_queries_and_keys_staged", s3)
        s_qk = sem("qk_transposed", s3)
        s_qkc = sem("qk_transposed_copied", s3)
        s_bd = sem("keys_placed", s3)
        s_vz = sem("values_cleared", s3)
        s_vb = sem("values_placed", s3)
        s_l = sem("logits_ready", s3)
        s_lc = sem("softmax_steps", s3)
        s_lm = sem("logit_maximum", s3)
        s_ls = sem("logits_shifted", s3)
        s_p = sem("probabilities_ready", s3)
        s_pt = sem("probabilities_transposed", s3)
        s_pc = sem("probabilities_copied", s3)
        s_en = sem("values_mixed", s3)
        s_ec = sem("mixed_normalised", s3)
        s_et = sem("mixed_transposed", s3)
        s_ect = sem("mixed_transposed_copied", s3)
        s_o = sem("self_output_ready", s3)
        s_x2 = sem("self_residual_added", s3)
        with nc.Block() as block:
            def pipelined(eng, step):
                with eng.Fori(0, QT // 2 - 2) as k:
                    for i in range(2):
                        step(k * 2 + i, i, 3)
                for t in range(QT - 4, QT):
                    step(t, t % 2, QT - 1 - t)

            @block.gpsimd
            def _(pool):
                pool.sem_inc(s_bd, DC * NB * START)
                for i in range(2):
                    nc.gpsimd.memset(v_bd[i][:], 0.0).then_inc(s_vz, 1)

                def place_keys(t, i):
                    pool.wait_ge(s_qkc, after(t))
                    pool.wait_ge(s_l, after(t - 2))
                    for c in range(DC):
                        for b in range(NB):
                            nc.gpsimd.tensor_tensor(
                                k_bd[i][:, c, b], kT[i][:, c, b * B:(b + 1) * B].unsqueeze(1).to_broadcast([P, HC, B]),
                                head_mask[:].unsqueeze(2).to_broadcast([P, HC, B]), ALU.mult).then_inc(s_bd, 1)

                def step(t, i, left):
                    if left >= 2:
                        place_keys(t + 2, i)
                place_keys(0, 0)
                place_keys(1, 1)
                pipelined(pool, step)

            @block.tensor
            def _(pe):
                for s in (s_qk, s_l, s_pt, s_en, s_et, s_o):
                    pe.sem_inc(s, START)

                def keys(t, i):
                    pe.wait_ge(s_kr, after(t))
                    pe.wait_ge(s_qkc, after(t - 1))
                    for c in range(DC):
                        nc.tensor.transpose(pK[:, 0, c, :], q_s[i][:, c * P:(c + 1) * P], ident[:])
                        mm = nc.tensor.transpose(pK[:, 1, c, :], k_rep[i][:].rearrange("p h d -> p (h d)")
                                                 [:, c * P:(c + 1) * P], ident[:])
                    mm.then_inc(s_qk, 1)

                def logits(t, i):
                    pe.wait_ge(s_bd, DC * NB * after(t))
                    pe.wait_ge(s_ls, after(t - 2))
                    for c in range(DC):
                        for b in range(NB):
                            mm = nc.tensor.matmul(pL[i][b * B:(b + 1) * B, c * HC:(c + 1) * HC, :],
                                                  qT[i][:, c, b * B:(b + 1) * B], k_bd[i][:, c, b],
                                                  start=True, stop=True)
                    mm.then_inc(s_l, 1)

                def turn_probabilities(t, i):
                    pe.wait_ge(s_p, after(t))
                    pe.wait_ge(s_pc, after(t - 1))
                    for h in range(H // 2):
                        mm = nc.tensor.transpose(pP[:, h, :], prob[i][:, 2 * h:2 * h + 2, :]
                                                 .rearrange("p h s -> p (h s)"), ident[:])
                    mm.then_inc(s_pt, 1)

                def mix(t, i):
                    pe.wait_ge(s_pc, after(t))
                    pe.wait_ge(s_vb, 2 * NB * after(t))
                    pe.wait_ge(s_x2, after(t - 1))
                    for b in range(NB):
                        for h in range(H // 2):
                            mm = nc.tensor.matmul(pE[b * B:(b + 1) * B, 2 * h * HD:(2 * h + 2) * HD],
                                                  pT_s[:, h, b * B:(b + 1) * B],
                                                  v_bd[i][:, b, 2 * h // GH].rearrange("p a d -> p (a d)"),
                                                  start=True, stop=True)
                    mm.then_inc(s_en, 1)

                def turn_mixed(t):
                    pe.wait_ge(s_ec, after(t))
                    for c in range(DC):
                        mm = nc.tensor.transpose(pF[:, c, :], enc[:].rearrange("p h d -> p (h d)")
                                                 [:, c * P:(c + 1) * P], ident[:])
                    mm.then_inc(s_et, 1)

                def output(t):
                    pe.wait_ge(s_ect, after(t))
                    for c in range(DC):
                        mm = nc.tensor.matmul(pG, eT[:, c, :], wo_sb[:, c, :], start=c == 0, stop=c == DC - 1)
                    mm.then_inc(s_o, 1)

                def step(t, i, left):
                    turn_probabilities(t, i)
                    if left >= 1:
                        logits(t + 1, 1 - i)
                    mix(t, i)
                    if left >= 2:
                        keys(t + 2, i)
                    turn_mixed(t)
                    output(t)
                keys(0, 0)
                keys(1, 1)
                logits(0, 0)
                pipelined(pe, step)

            @block.scalar
            def _(act):
                for s in (s_kr, s_qkc, s_p, s_pc, s_ect):
                    act.sem_inc(s, START)

                def gather(t, i):
                    act.wait_ge(s_qk, after(t - 2))
                    nc.scalar.copy(q_s[i][:], qkv[:, bass.ds(t, 1), 0:D].rearrange("p a n -> p (a n)"))
                    k_src = qkv[:, bass.ds(t, 1), D:QK].rearrange("p a (k d) -> p (a k) d", d=HD)
                    nc.scalar.copy(k_rep[i][:].rearrange("p (k g) d -> p k g d", g=GH),
                                   k_src.unsqueeze(2).to_broadcast([P, KH, GH, HD])).then_inc(s_kr, 1)

                def copy_keys(t, i):
                    act.wait_ge(s_qk, after(t))
                    act.wait_ge(s_l, after(t - 2))
                    act.wait_ge(s_bd, DC * NB * after(t - 2))
                    nc.scalar.copy(qT[i][:], pK[:, 0])
                    nc.scalar.copy(kT[i][:], pK[:, 1]).then_inc(s_qkc, 1)

                def exponential(t, i):
                    act.wait_ge(s_ls, after(t))
                    act.wait_ge(s_pt, after(t - 2))
                    act.wait_ge(s_lc, 2 * after(t - 2))
                    nc.scalar.activation(prob[i][:], l_sub[i][:], ACT.Exp,
                                         scale=rms_r[:, bass.ds(t, 1), 0:1].rearrange("p a b -> p (a b)")
                                         ).then_inc(s_p, 1)

                def step(t, i, left):
                    act.wait_ge(s_pt, after(t))
                    act.wait_ge(s_en, after(t - 1))
                    nc.scalar.copy(pT_s[:], pP[:]).then_inc(s_pc, 1)
                    if left >= 3:
                        gather(t + 3, 1 - i)
                    if left >= 2:
                        copy_keys(t + 2, i)
                    act.wait_ge(s_et, after(t))
                    act.wait_ge(s_o, after(t - 1))
                    nc.scalar.copy(eT[:], pF).then_inc(s_ect, 1)
                    if left >= 1:
                        exponential(t + 1, 1 - i)
                gather(0, 0)
                gather(1, 1)
                copy_keys(0, 0)
                gather(2, 0)
                copy_keys(1, 1)
                exponential(0, 0)
                pipelined(act, step)

            @block.vector
            def _(dve):
                for s, n in ((s_vb, 2 * NB), (s_lm, 1), (s_ls, 1), (s_lc, 2), (s_ec, 1), (s_x2, 1)):
                    dve.sem_inc(s, n * START)
                dve.wait_ge(s_vz, 2)

                def place_values(t, i):
                    own = qkv[:, bass.ds(t, 1), QK:QK + KD].rearrange("p a (k d) -> p (a k) d", d=HD)
                    other = v_sw[:, bass.ds(t, 1), :].rearrange("p a (k d) -> p (a k) d", d=HD)
                    dve.wait_ge(s_en, after(t - 2))
                    for b in range(NB):
                        for half in range(2):
                            rows = slice(half * B, (half + 1) * B)
                            src = own if b == half else other
                            nc.vector.tensor_copy(v_bd[i][rows, b, :, half, :], src[rows]).then_inc(s_vb, 1)

                def maximum(t, i):
                    dve.wait_ge(s_l, after(t))
                    nc.vector.tensor_reduce(l_max[:], pL[i][:], AX.X, ALU.max).then_inc(s_lm, 1)

                def shift(t, i):
                    dve.wait_ge(s_lm, after(t))
                    dve.wait_ge(s_p, after(t - 2))
                    nc.vector.tensor_tensor(l_sub[i][:], pL[i][:], l_max[:].unsqueeze(2).to_broadcast([P, H, B]),
                                            ALU.subtract).then_inc(s_ls, 1)

                def step(t, i, left):
                    dve.wait_ge(s_p, after(t))
                    nc.vector.tensor_reduce(p_sum[:], prob[i][:], AX.X, ALU.add).then_inc(s_lc, 1)
                    dve.wait_ge(s_lc, 2 * after(t - 1) + 1)
                    nc.vector.reciprocal(p_rec[:], p_sum[:]).then_inc(s_lc, 1)
                    if left >= 1:
                        maximum(t + 1, 1 - i)
                    dve.wait_ge(s_en, after(t))
                    dve.wait_ge(s_lc, 2 * after(t))
                    dve.wait_ge(s_et, after(t - 1))
                    nc.vector.tensor_tensor(enc[:], pE.rearrange("p (h d) -> p h d", d=HD),
                                            p_rec[:].unsqueeze(2).to_broadcast([P, H, HD]), ALU.mult).then_inc(s_ec, 1)
                    if left >= 1:
                        shift(t + 1, 1 - i)
                    if left >= 2:
                        place_values(t + 2, i)
                    row = x_all[:, bass.ds(t, 1), :].rearrange("p a d -> p (a d)")
                    dve.wait_ge(s_o, after(t))
                    nc.vector.tensor_tensor(row, row, pG, ALU.add).then_inc(s_x2, 1)
                place_values(0, 0)
                place_values(1, 1)
                maximum(0, 0)
                shift(0, 0)
                pipelined(dve, step)
        s3.close()
        sa.close()
        layer_norm("second")

        E = a["gate"].shape[1]
        W = a["down"].shape[0]
        NE = a["down"].shape[1] // 2
        SH = NE - E
        TB = 4
        NBLK = QT // TB
        SCALE = 2.5
        mo = ExitStack()
        wg_sb = sb("wg_sb", [P, DC, 2 * NE * W], F32, mo)
        wu_sb = sb("wu_sb", [P, DC, 2 * NE * W], F32, mo)
        wd_sb = sb("wd_sb", [W, 2 * NE, D], F32, mo)
        gate_sb = sb("gate_sb", [P, DC, E], F32, mo)
        zT = sb("zT", [P, DC, QT, P], F32, mo)
        score = sb("score", [P, QT, E], F32, mo)
        weight = sb("weight", [P, QT, NE], F32, mo)

        r1 = ExitStack()
        z_n = [sb(f"z_n{i}", [P, D], F32, r1) for i in range(2)]
        before = sb("before", [P, E, E], F32, r1)
        gt = sb("gt", [P, QT, E, E], F32, r1)
        eq = sb("eq", [P, QT, E, E], F32, r1)
        rank = sb("rank", [P, QT, E], F32, r1)
        top = sb("top", [P, QT, E], F32, r1)
        total = sb("total", [P, QT], F32, r1)
        total_r = sb("total_r", [P, QT], F32, r1)
        pZ = [ps(f"pZ{i}", [P, DC, P], F32, r1) for i in range(2)]
        pR = ps("pR", [P, QT, E], F32, r1)
        s_mw = sem("moe_weights_loaded", mo)
        s_zn = sem("moe_normalised", r1)
        s_zt = sem("moe_transposed", r1)
        s_zc = sem("moe_transposed_copied", r1)
        s_r = sem("router_logits_ready", r1)
        s_sc = sem("router_scores_ready", r1)
        s_rt = sem("router_steps", r1)
        s_bf = sem("order_mask", r1)
        with nc.Block() as block:
            @block.sync
            def _(sp):
                for dst, src in ((gate_sb, a["gate"]), (wg_sb, a["up_gate"]), (wu_sb, a["up"])):
                    sp.dma_start(dst[:], src.rearrange("(c p) n -> p c n", p=P)).then_inc(s_mw, 16)
                sp.dma_start(wd_sb[:], a["down"]).then_inc(s_mw, 16)

            @block.gpsimd
            def _(pool):
                nc.gpsimd.memset(before[:], 1.0).then_inc(s_bf, 1)
                pool.wait_ge(s_bf, 1)
                nc.gpsimd.affine_select(out=before[:], in_=before[:], compare_op=ALU.is_ge, fill=0.0, base=-1,
                                        pattern=[[1, E], [-1, E]], channel_multiplier=0).then_inc(s_bf, 1)
                for t in range(QT):
                    if t >= 2:
                        pool.wait_ge(s_zt, t - 1)
                    nc.gpsimd.tensor_scalar(z_n[t % 2][:], x_all[:, t, :], mean_var[:, t, 0:1], rstd[:, t:t + 1],
                                            ALU.subtract, ALU.mult).then_inc(s_zn, 1)

            @block.tensor
            def _(pe):
                def turn(t, i):
                    pe.wait_ge(s_zn, t + 1)
                    for c in range(DC):
                        mm = nc.tensor.transpose(pZ[i][:, c, :], z_n[i][:, c * P:(c + 1) * P], ident[:])
                    mm.then_inc(s_zt, 1)
                pe.wait_ge(s_mw, 4 * 16)
                for t in range(QT):
                    if t >= 2:
                        pe.wait_ge(s_zc, t - 1)
                    turn(t, t % 2)
                    if t >= 1:
                        pe.wait_ge(s_zc, t)
                        for c in range(DC):
                            nc.tensor.matmul(pR[:, t - 1, :], zT[:, c, t - 1, :], gate_sb[:, c, :],
                                             start=c == 0, stop=c == DC - 1)
                pe.wait_ge(s_zc, QT)
                for c in range(DC):
                    mm = nc.tensor.matmul(pR[:, QT - 1, :], zT[:, c, QT - 1, :], gate_sb[:, c, :],
                                          start=c == 0, stop=c == DC - 1)
                mm.then_inc(s_r, 1)

            @block.scalar
            def _(act):
                for t in range(QT):
                    act.wait_ge(s_zt, t + 1)
                    nc.scalar.copy(zT[:, :, t, :], pZ[t % 2][:]).then_inc(s_zc, 1)
                act.wait_ge(s_r, 1)
                nc.scalar.activation(score[:], pR[:], ACT.Sigmoid).then_inc(s_sc, 1)

            @block.vector
            def _(dve):
                done = [0]

                def link(ins):
                    done[0] += 1
                    ins.then_inc(s_rt, 1)
                    dve.wait_ge(s_rt, done[0])
                mine = score[:].unsqueeze(3).to_broadcast([P, QT, E, E])
                other = score[:].unsqueeze(2).to_broadcast([P, QT, E, E])
                dve.wait_ge(s_sc, 1)
                dve.wait_ge(s_bf, 2)
                link(nc.vector.tensor_tensor(gt[:], other, mine, ALU.is_gt))
                link(nc.vector.tensor_tensor(eq[:], other, mine, ALU.is_equal))
                link(nc.vector.tensor_tensor(eq[:], eq[:], before[:].unsqueeze(1).to_broadcast([P, QT, E, E]),
                                             ALU.mult))
                link(nc.vector.tensor_tensor(gt[:], gt[:], eq[:], ALU.add))
                link(nc.vector.tensor_reduce(rank[:], gt[:], AX.X, ALU.add))
                link(nc.vector.tensor_scalar(rank[:], rank[:], 1.5, None, ALU.is_lt))
                link(nc.vector.tensor_tensor(top[:], score[:], rank[:], ALU.mult))
                link(nc.vector.tensor_reduce(total[:], top[:], AX.X, ALU.add))
                link(nc.vector.tensor_scalar(total[:], total[:], 1e-20, None, ALU.add))
                link(nc.vector.reciprocal(total_r[:], total[:]))
                link(nc.vector.tensor_tensor(top[:], top[:], total_r[:].unsqueeze(2).to_broadcast([P, QT, E]),
                                             ALU.mult))
                nc.vector.tensor_scalar(weight[:, :, SH:NE], top[:], SCALE, None, ALU.mult)
                nc.vector.memset(weight[:, :, 0:SH], 1.0)
        r1.close()

        m2 = ExitStack()
        h_s = [sb(f"h_s{i}", [W, 2, TB * P], F32, m2) for i in range(2)]
        h_o = [sb(f"h_o{i}", [W, 2, TB * P], F32, m2) for i in range(2)]
        pGt = [ps(f"pGt{i}", [P, TB * P], F32, m2) for i in range(2)]
        pUp = [ps(f"pUp{i}", [P, TB * P], F32, m2) for i in range(2)]
        pDn = ps("pDn", [P, TB, D], F32, m2)
        s_up = sem("up_products_ready", m2)
        s_si = sem("gate_activated", m2)
        s_h = sem("hidden_ready", m2)
        s_d = sem("down_product_ready", m2)
        s_a = sem("expert_added", m2)
        s_out = sem("output_stored", m2)

        def halves(n):
            return n + 3

        with nc.Block() as block:
            @block.tensor
            def _(pe):
                def tokens(blk, c):
                    return zT[:, c, bass.ds(blk * TB, TB), :].rearrange("p t n -> p (t n)")

                def up(blk, e, i):
                    for f in range(2):
                        n = 2 * (blk * NE + e) + f
                        cols = slice((2 * e + f) * W, (2 * e + f + 1) * W)
                        pe.wait_ge(s_h, halves(n - 2))
                        for dst, w in ((pGt[f], wg_sb), (pUp[f], wu_sb)):
                            for c in range(DC):
                                mm = nc.tensor.matmul(dst[0:W, :], w[:, c, cols], tokens(blk, c),
                                                      start=c == 0, stop=c == DC - 1)
                        mm.then_inc(s_up, 1)

                def down(blk, e, i):
                    n = blk * NE + e
                    pe.wait_ge(s_h, halves(2 * n + 1))
                    pe.wait_ge(s_a, TB * n)
                    for t in range(TB):
                        for f in range(2):
                            mm = nc.tensor.matmul(pDn[:, t, :], h_o[i][:, f, t * P:(t + 1) * P],
                                                  wd_sb[:, 2 * e + f, :], start=f == 0, stop=f == 1)
                    mm.then_inc(s_d, 1)
                with pe.Fori(0, NBLK) as blk:
                    up(blk, 0, 0)
                    for e in range(1, NE):
                        up(blk, e, e % 2)
                        down(blk, e - 1, (e - 1) % 2)
                    down(blk, NE - 1, (NE - 1) % 2)

            @block.scalar
            def _(act):
                with act.Fori(0, NBLK) as blk:
                    for e in range(NE):
                        for f in range(2):
                            n = 2 * (blk * NE + e) + f
                            act.wait_ge(s_up, n + 1)
                            if e < 2:
                                act.wait_ge(s_h, halves(2 * NE * blk - 1))
                            else:
                                act.wait_ge(s_h, halves(n - 4))
                            nc.scalar.activation(h_s[e % 2][:, f, :], pGt[f][0:W, :], ACT.Silu).then_inc(s_si, 1)

            @block.vector
            def _(dve):
                def add(blk, e):
                    n = blk * NE + e
                    dve.wait_ge(s_d, n + 1)
                    for t in range(TB):
                        tile = blk * TB + t
                        row = x_all[:, bass.ds(tile, 1), :].rearrange("p a d -> p (a d)")
                        w = weight[:, bass.ds(tile, 1), e:e + 1].rearrange("p a b -> p (a b)")
                        dve.wait_ge(s_a, TB * n + t)
                        nc.vector.scalar_tensor_tensor(out=row, in0=pDn[:, t, :], scalar=w, in1=row, op0=ALU.mult,
                                                       op1=ALU.add).then_inc(s_a, 1)

                dve.sem_inc(s_h, 2)
                with dve.Fori(0, NBLK) as blk:
                    for e in range(NE):
                        for f in range(2):
                            n = 2 * (blk * NE + e) + f
                            dve.wait_ge(s_si, n + 1)
                            if e < 2:
                                dve.wait_ge(s_d, blk * NE)
                            else:
                                dve.wait_ge(s_d, blk * NE + e - 1)
                            nc.vector.tensor_tensor(h_o[e % 2][:, f, :], h_s[e % 2][:, f, :], pUp[f][0:W, :],
                                                    ALU.mult).then_inc(s_h, 1)
                        if e:
                            add(blk, e - 1)
                    add(blk, NE - 1)

            @block.sync
            def _(sp):
                with sp.Fori(0, NBLK) as blk:
                    sp.wait_ge(s_a, NE * TB * (blk + 1))
                    sp.dma_start(out_t[:, bass.ds(blk * TB, TB), :], x_all[:, bass.ds(blk * TB, TB), :]).then_inc(s_out, 16)
                sp.wait_ge(s_out, 16 * NBLK)
        m2.close()
        mo.close()


_INS = ["x", "L0_xattn_Wq", "L0_xattn_bq", "L0_xattn_Wkv", "L0_xattn_bkv", "L0_xattn_Wp", "L0_xattn_bp",
        "L0_attn_Wq", "L0_attn_Wk", "L0_attn_Wv", "L0_attn_Wout"]


def rope_table(batch=64):
    fraction = np.arange(0, HD, 2, dtype=np.float32) / np.float32(HD)
    timescale = (np.float32(10000.0) ** fraction).astype(np.float32)
    position = (np.arange(P) % batch).astype(np.float32)
    angle = position[:, None] * (np.float32(1.0) / timescale)[None, :]
    cos, sin = np.cos(angle), np.sin(angle)
    return np.stack([np.concatenate([cos, cos], 1), np.concatenate([-sin, sin], 1)], 1).astype(np.float32)


def lay_out(inputs):
    arrays = {name: np.ascontiguousarray(inputs[name]) for name in _INS}
    ctx = np.asarray(inputs["ctx_2048"])
    arrays["ctx_T"] = np.ascontiguousarray(ctx.reshape(-1, ctx.shape[-1]).T)
    arrays["rope"] = rope_table()
    arrays["gate"] = np.ascontiguousarray(np.asarray(inputs["L0_ffn_gate_w"]).T)

    def up(shared, experts):
        shared, experts = np.asarray(shared), np.asarray(experts)
        rows = np.concatenate([shared, experts.reshape(-1, experts.shape[-1])])
        return np.ascontiguousarray(rows.T)
    arrays["up_gate"] = up(inputs["L0_ffn_shared_wg"], inputs["L0_ffn_exp_wg"])
    arrays["up"] = up(inputs["L0_ffn_shared_wu"], inputs["L0_ffn_exp_wu"])
    shared, experts = np.asarray(inputs["L0_ffn_shared_wd"]), np.asarray(inputs["L0_ffn_exp_wd"])
    rows = np.concatenate([shared.T, experts.transpose(0, 2, 1).reshape(-1, experts.shape[1])])
    half = experts.shape[2] // 2
    arrays["down"] = np.ascontiguousarray(rows.reshape(-1, half, rows.shape[1]).transpose(1, 0, 2))
    return arrays


def kernel(**inputs):
    import concourse.bacc as _bacc
    from concourse.bass_utils import run_bass_kernel_spmd as _run

    nc = _bacc.Bacc("TRN2", target_bir_lowering=False, num_devices=1)
    arrays = lay_out(inputs)
    args = {n: nc.dram_tensor(f"in_{n}", v.shape, mybir.dt.from_np(v.dtype), kind="ExternalInput").ap()
            for n, v in arrays.items()}
    out = nc.dram_tensor("out_0", arrays["x"].shape, F32, kind="ExternalOutput").ap()
    build(nc, args, out)
    r = _run(nc, [{f"in_{n}": v for n, v in arrays.items()}], core_ids=[0])
    return r.results[0]["out_0"]
```

```python
from contextlib import ExitStack

import numpy as np

import concourse.bass as bass
from concourse import mybir

F32 = mybir.dt.float32
BF16 = mybir.dt.bfloat16
U16 = mybir.dt.uint16
ACT = mybir.ActivationFunctionType
ALU = mybir.AluOpType
AX = mybir.AxisListType

P = 128
D = 256
DC = D // P
H = 16
HD = D // H
BANK = 512
ROUND = 12582912.0
LN255 = float(np.log(255.0))
EPS_STEP = 1e-8
LN_EPS = 1e-5


def build(nc, a, out):
    NT = a["x"].shape[0] * a["x"].shape[1]
    NK = a["ctx_T"].shape[1]
    QT, KT = NT // P, NK // P
    UNITS = H * QT
    CH = 2 * BANK
    NCH = NK // CH
    PARTS = 3
    KR = PARTS * HD
    CG = 4

    x_t = a["x"].rearrange("b t d -> (b t) d").rearrange("(n p) d -> p n d", p=P)
    out_t = out.rearrange("b t d -> (b t) d").rearrange("(n p) d -> p n d", p=P)

    kT_d = nc.dram_tensor("keys_transposed", [H * KR, NK], BF16, kind="Internal").ap()
    qT_d = nc.dram_tensor("queries_transposed", [D, NT], BF16, kind="Internal").ap()

    top = ExitStack()
    with top:
        def sb(name, shape, dt, ctx=top):
            return ctx.enter_context(nc.sbuf_tensor(name, shape, dt))

        def ps(name, shape, dt, ctx):
            per_bank = BANK * 4 // mybir.dt.size(dt)
            used = int(np.prod(shape[1:]))
            whole = ctx.enter_context(nc.psum_tensor(name, [P, -(-used // per_bank) * per_bank], dt))
            names = [f"d{i}" for i in range(len(shape) - 1)]
            return whole[:, 0:used].rearrange(f"p ({' '.join(names)}) -> p {' '.join(names)}",
                                              **dict(zip(names, shape[1:])))

        def sem(name, ctx=top):
            return ctx.enter_context(nc.semaphore(name))

        x_all = sb("x_all", [P, QT, D], F32)
        ident = sb("ident", [P, P], F32)
        ident_h = sb("ident_h", [P, P], BF16)
        ones = sb("ones", [P, P], F32)
        eps = sb("eps", [P, 1], F32)
        mean_var = sb("mean_var", [P, QT, 2], F32)
        rstd = sb("rstd", [P, QT], F32)
        std = sb("std", [P, QT], F32)

        mid = ExitStack()
        att = sb("att", [P, UNITS + 1, HD], F32, mid)
        wp_sb = sb("wp_sb", [P, DC, D], F32, mid)
        wps_sb = sb("wps_sb", [P, DC, D], F32, mid)
        q_step = sb("q_step", [P, UNITS + 2], F32, mid)
        v_int = sb("v_int", [P, KT, D], BF16, mid)

        pre = ExitStack()
        wkv_sb = sb("wkv_sb", [P, DC, 2 * D], F32, pre)
        bkv_sb = sb("bkv_sb", [P, 2 * D], F32, pre)
        wq_sb = sb("wq_sb", [P, DC, D], F32, pre)
        bq_sb = sb("bq_sb", [1, D], F32, pre)
        v_f = sb("v_f", [P, KT, D], F32, pre)

        s_w = sem("weights_loaded")
        s_x = sem("x_loaded")
        s_zero = sem("constants_filled")
        s_id = sem("constants_ready")
        with nc.Block() as block:
            @block.sync
            def _(sp):
                sp.dma_start(x_all[:], x_t).then_inc(s_x, 16)
                for dst, src in ((wkv_sb, a["L0_xattn_Wkv"]), (wq_sb, a["L0_xattn_Wq"]), (wp_sb, a["L0_xattn_Wp"])):
                    sp.dma_start(dst[:], src.rearrange("(c p) n -> p c n", p=P)).then_inc(s_w, 16)
                sp.dma_start(bq_sb[:], a["L0_xattn_bq"].rearrange("(a n) -> a n", a=1)).then_inc(s_w, 16)
                sp.wait_ge(s_zero, 4)
                for r in range(PARTS):
                    sp.dma_start(bkv_sb[32 * r:32 * r + 1, :],
                                 a["L0_xattn_bkv"].rearrange("(a n) -> a n", a=1)).then_inc(s_w, 16)
                sp.wait_ge(s_w, 7 * 16)
                sp.wait_ge(s_x, 16)

            @block.gpsimd
            def _(pool):
                nc.gpsimd.memset(ident[:], 0.0).then_inc(s_zero, 1)
                nc.gpsimd.memset(ident_h[:], 0.0).then_inc(s_zero, 1)
                nc.gpsimd.memset(ones[:], 1.0)
                nc.gpsimd.memset(eps[:], LN_EPS).then_inc(s_zero, 1)
                nc.gpsimd.memset(bkv_sb[:], 0.0).then_inc(s_zero, 1)
                pool.wait_ge(s_zero, 4)
                for m in (ident, ident_h):
                    nc.gpsimd.affine_select(out=m[:], in_=m[:], compare_op=ALU.not_equal, fill=1.0, base=0,
                                            pattern=[[-1, P]], channel_multiplier=1).then_inc(s_id, 1)
                pool.wait_ge(s_id, 2)

        def layer_norm(which):
            with ExitStack() as ln:
                stats = sb(f"stats_{which}", [P, QT, 6], F32, ln)
                s_st = sem(f"statistics_{which}", ln)
                s_sd = sem(f"deviation_{which}", ln)
                with nc.Block() as block:
                    @block.vector
                    def _(dve):
                        for t in range(QT):
                            last = nc.vector.bn_stats(stats[:, t, :], x_all[:, t, :])
                        last.then_inc(s_st, 1)
                        dve.wait_ge(s_st, 1)
                        for t in range(QT):
                            last = nc.vector.bn_aggr(mean_var[:, t, :], stats[:, t, :])
                        last.then_inc(s_st, 1)
                        dve.wait_ge(s_sd, 1)
                        nc.vector.reciprocal(rstd[:], std[:])

                    @block.scalar
                    def _(act):
                        act.wait_ge(s_st, 2)
                        nc.scalar.activation(std[:], mean_var[:, :, 1], ACT.Sqrt, bias=eps[:]).then_inc(s_sd, 1)

        layer_norm("query")

        G = 2
        NI = KT // G
        cs = ExitStack()
        cT = [sb(f"cT{i}", [P, DC, G * P], F32, cs) for i in range(2)]
        b_low = sb("b_low", [P, 2 * D], F32, cs)
        b_mid = sb("b_mid", [P, 2 * D], BF16, cs)
        b_parts = sb("b_parts", [P, 2 * D], BF16, cs)
        ones_h = sb("ones_h", [P, P], BF16, cs)
        k_f = [sb(f"k_f{i}", [P, G, D], F32, cs) for i in range(2)]
        k_amax = sb("k_amax", [P, G, H], F32, cs)
        k_st = sb("k_st", [P, G, H], F32, cs)
        k_rst = sb("k_rst", [P, G, H], F32, cs)
        k_a = sb("k_a", [P, G, D], F32, cs)
        k_b = sb("k_b", [P, G, D], F32, cs)
        k_parts = [sb(f"k_parts{i}", [P, G, H, PARTS, HD], BF16, cs) for i in range(2)]
        KC = H * KR // P
        kT_s = [sb(f"kT_s{i}", [P, KC, G, P], BF16, cs) for i in range(2)]
        pKV = [ps(f"pKV{i}", [P, G, 2 * D], F32, cs) for i in range(2)]
        pKT = [ps(f"pKT{i}", [P, G, 2 * BANK], BF16, cs) for i in range(2)]
        s_c = [sem(f"ctx_loaded{i}", cs) for i in range(2)]
        s_bp = sem("bias_parts", cs)
        s_kv = sem("kv_ready", cs)
        s_kc = sem("keys_copied", cs)
        s_vc = sem("values_copied", cs)
        s_kch = sem("key_steps", cs)
        s_kp = sem("key_parts_ready", cs)
        s_ktp = sem("keys_transposed", cs)
        s_kts = sem("keys_transposed_copied", cs)
        s_kst = [sem(f"keys_stored{i}", cs) for i in range(2)]
        START = 2

        def after(it):
            return it + START + 1

        def heads(ap):
            return ap.rearrange("p g (h d) -> p (g h) d", d=HD)

        def spread(ap):
            return ap.rearrange("p g h -> p (g h)").unsqueeze(2).to_broadcast([P, G * H, HD])

        with nc.Block() as block:
            cT_d = a["ctx_T"].rearrange("(c p) n -> p c n", p=P)

            @block.sync
            def _(sp):
                def load(it, i):
                    sp.dma_start(cT[i][:], cT_d[:, :, bass.ds(it * G * P, G * P)]).then_inc(s_c[i], 16)
                load(0, 0)
                load(1, 1)
                with sp.Fori(0, NI // 2 - 1) as k:
                    for i in range(2):
                        it = k * 2 + i
                        sp.wait_ge(s_kv, after(it))
                        load(it + 2, i)

            @block.gpsimd
            def _(pool):
                with pool.Fori(0, NI // 2) as k:
                    for i in range(2):
                        it = k * 2 + i
                        pool.wait_ge(s_kts, after(it))
                        pool.dma_start(kT_d.rearrange("(c p) n -> p c n", p=P)[:, :, bass.ds(it * G * P, G * P)],
                                       kT_s[i][:].rearrange("p c g n -> p c (g n)")).then_inc(s_kst[i], 16)
                for i in range(2):
                    pool.wait_ge(s_kst[i], 16 * (NI // 2))

            @block.tensor
            def _(pe):
                pe.sem_inc(s_kv, START)
                pe.sem_inc(s_ktp, START)

                def project(it, k, i):
                    pe.wait_ge(s_c[i], 16 * (k + 1))
                    pe.wait_ge(s_kc, after(it - 2))
                    pe.wait_ge(s_vc, after(it - 2))
                    for g in range(G):
                        nc.tensor.matmul(pKV[i][:, g, :], ones_h[:], b_parts[:], start=True, stop=False)
                        for c in range(DC):
                            mm = nc.tensor.matmul(pKV[i][:, g, :], cT[i][:, c, g * P:(g + 1) * P], wkv_sb[:, c, :],
                                                  start=False, stop=c == DC - 1)
                    mm.then_inc(s_kv, 1)

                def turn(it, i):
                    pe.wait_ge(s_kp, after(it))
                    pe.wait_ge(s_kts, after(it - 2))
                    for g in range(G):
                        flat = k_parts[i][:, g].rearrange("p h r d -> p (h r d)")
                        for c in range(KC):
                            mm = nc.tensor.transpose(pKT[i][:, g, c * P:(c + 1) * P], flat[:, c * P:(c + 1) * P],
                                                     ident_h[:])
                    mm.then_inc(s_ktp, 1)
                pe.wait_ge(s_bp, 8)
                project(0, 0, 0)
                project(1, 0, 1)
                with pe.Fori(0, NI // 2 - 1) as k:
                    for i in range(2):
                        turn(k * 2 + i, i)
                        project(k * 2 + i + 2, k + 1, i)
                turn(NI - 2, 0)
                turn(NI - 1, 1)

            @block.scalar
            def _(act):
                act.sem_inc(s_kc, START)
                act.sem_inc(s_vc, START)
                act.sem_inc(s_kts, START)

                def copies(it, i):
                    act.wait_ge(s_kv, after(it))
                    act.wait_ge(s_kp, after(it - 2))
                    nc.scalar.copy(k_f[i][:], pKV[i][:, :, 0:D]).then_inc(s_kc, 1)
                    nc.scalar.copy(v_f[:, bass.ds(it * G, G), :], pKV[i][:, :, D:2 * D]).then_inc(s_vc, 1)

                def evacuate(it, i, stores):
                    act.wait_ge(s_ktp, after(it))
                    if stores is not None:
                        act.wait_ge(s_kst[i], 16 * stores)
                    nc.scalar.copy(kT_s[i][:].rearrange("p c g n -> p g c n"),
                                   pKT[i][:, :, 0:KC * P].rearrange("p g (c n) -> p g c n", n=P)).then_inc(s_kts, 1)
                copies(0, 0)
                copies(1, 1)
                for i in range(2):
                    evacuate(i, i, None)
                    copies(i + 2, i)
                with act.Fori(1, NI // 2 - 1) as k:
                    for i in range(2):
                        evacuate(k * 2 + i, i, k)
                        copies(k * 2 + i + 2, i)
                evacuate(NI - 2, 0, NI // 2 - 1)
                evacuate(NI - 1, 1, NI // 2 - 1)

            @block.vector
            def _(dve):
                dve.sem_inc(s_kp, START)
                Q = 32
                nc.vector.memset(ones_h[:], 1.0).then_inc(s_bp, 1)
                nc.vector.memset(b_parts[:], 0.0).then_inc(s_bp, 1)
                nc.vector.tensor_copy(b_mid[:], bkv_sb[:]).then_inc(s_bp, 1)
                dve.wait_ge(s_bp, 3)
                nc.vector.tensor_copy(b_parts[0:Q, :], b_mid[0:Q, :]).then_inc(s_bp, 1)
                nc.vector.tensor_tensor(b_low[:], bkv_sb[:], b_mid[:], ALU.subtract).then_inc(s_bp, 1)
                dve.wait_ge(s_bp, 5)
                nc.vector.tensor_copy(b_mid[:], b_low[:]).then_inc(s_bp, 1)
                dve.wait_ge(s_bp, 6)
                nc.vector.tensor_copy(b_parts[Q:2 * Q, :], b_mid[Q:2 * Q, :]).then_inc(s_bp, 1)
                nc.vector.tensor_tensor(b_parts[2 * Q:3 * Q, :], b_low[2 * Q:3 * Q, :], b_mid[2 * Q:3 * Q, :],
                                        ALU.subtract).then_inc(s_bp, 1)

                def quantise(it, i):
                    LINKS = 9
                    done = [0]

                    def link(ins):
                        done[0] += 1
                        ins.then_inc(s_kch, 1)
                        dve.wait_ge(s_kch, it * LINKS + done[0])
                    dve.wait_ge(s_kc, after(it))
                    k = heads(k_f[i][:])
                    link(nc.vector.tensor_reduce(k_amax[:], k, AX.X, ALU.max, apply_absolute_value=True))
                    link(nc.vector.tensor_scalar(k_st[:], k_amax[:], 1.0 / 127.0, EPS_STEP, ALU.mult, ALU.max))
                    link(nc.vector.reciprocal(k_rst[:], k_st[:]))
                    link(nc.vector.tensor_tensor(heads(k_a[:]), k, spread(k_rst[:]), ALU.mult))
                    link(nc.vector.tensor_scalar(k_b[:], k_a[:], ROUND, ROUND, ALU.add, ALU.subtract))
                    link(nc.vector.tensor_tensor(heads(k_a[:]), heads(k_b[:]), spread(k_st[:]), ALU.mult))
                    dve.wait_ge(s_ktp, after(it - 2))
                    part = [k_parts[i][:, :, :, r, :].rearrange("p g h d -> p (g h) d") for r in range(PARTS)]
                    link(nc.vector.tensor_copy(part[0], heads(k_a[:])))
                    link(nc.vector.tensor_tensor(heads(k_b[:]), heads(k_a[:]), part[0], ALU.subtract))
                    link(nc.vector.tensor_copy(part[1], heads(k_b[:])))
                    nc.vector.tensor_tensor(part[2], heads(k_b[:]), part[1], ALU.subtract).then_inc(s_kp, 1)
                with dve.Fori(0, NI // 2) as k:
                    for i in range(2):
                        quantise(k * 2 + i, i)
        cs.close()

        NI_Q = QT // G
        qs = ExitStack()
        xn = sb("xn", [P, G, D], F32, qs)
        xT = sb("xT", [P, G, DC, P], F32, qs)
        q_f = sb("q_f", [P, G, D], F32, qs)
        q_amax = sb("q_amax", [P, G, H], F32, qs)
        q_st = sb("q_st", [P, G, H], F32, qs)
        q_rst = sb("q_rst", [P, G, H], F32, qs)
        q_a = sb("q_a", [P, G, D], F32, qs)
        q_int = sb("q_int", [P, G, D], BF16, qs)
        qT_s = sb("qT_s", [P, DC, G, P], BF16, qs)
        pX = ps("pX", [P, G, DC, P], F32, qs)
        pQ = ps("pQ", [P, G, D], F32, qs)
        pQT = ps("pQT", [P, G, DC, P], BF16, qs)
        s_xn = sem("x_normalised", qs)
        s_xt = sem("x_transposed", qs)
        s_xc = sem("x_transposed_copied", qs)
        s_q = sem("queries_ready", qs)
        s_qc = sem("queries_copied", qs)
        s_qch = sem("query_steps", qs)
        s_qi = sem("query_integers_ready", qs)
        s_qtp = sem("queries_transposed", qs)
        s_qts = sem("queries_transposed_copied", qs)
        s_qst = sem("queries_stored", qs)
        with nc.Block() as block:
            @block.gpsimd
            def _(pool):
                for it in range(NI_Q):
                    if it > 0:
                        pool.wait_ge(s_xt, it + 1)
                    for g in range(G):
                        t = it * G + g
                        last = nc.gpsimd.tensor_scalar(xn[:, g, :], x_all[:, t, :], mean_var[:, t, 0:1],
                                                       rstd[:, t:t + 1], ALU.subtract, ALU.mult)
                        last.then_inc(s_xn, 1)

            @block.tensor
            def _(pe):
                for s in (s_xt, s_q, s_qtp):
                    pe.sem_inc(s, 1)

                def project(it):
                    pe.wait_ge(s_xn, G * (it + 1))
                    pe.wait_ge(s_xc, it + 1)
                    for g in range(G):
                        for c in range(DC):
                            mm = nc.tensor.transpose(pX[:, g, c, :], xn[:, g, c * P:(c + 1) * P], ident[:])
                    mm.then_inc(s_xt, 1)
                    pe.wait_ge(s_xc, it + 2)
                    pe.wait_ge(s_qc, it + 1)
                    for g in range(G):
                        nc.tensor.matmul(pQ[:, g, :], ones[0:1, :], bq_sb[:], start=True, stop=False)
                        for c in range(DC):
                            mm = nc.tensor.matmul(pQ[:, g, :], xT[:, g, c, :], wq_sb[:, c, :],
                                                  start=False, stop=c == DC - 1)
                    mm.then_inc(s_q, 1)

                def turn(it):
                    pe.wait_ge(s_qi, it + 2)
                    pe.wait_ge(s_qts, it + 1)
                    for g in range(G):
                        for c in range(DC):
                            mm = nc.tensor.transpose(pQT[:, g, c, :], q_int[:, g, c * P:(c + 1) * P], ident_h[:])
                    mm.then_inc(s_qtp, 1)
                project(0)
                with pe.Fori(1, NI_Q) as it:
                    project(it)
                    turn(it - 1)
                turn(NI_Q - 1)

            @block.scalar
            def _(act):
                for s in (s_xc, s_qc, s_qts):
                    act.sem_inc(s, 1)

                def copies(it):
                    act.wait_ge(s_xt, it + 2)
                    act.wait_ge(s_q, it + 1)
                    nc.scalar.copy(xT[:].rearrange("p g c n -> p (g c n)"),
                                   pX[:].rearrange("p g c n -> p (g c n)")).then_inc(s_xc, 1)
                    act.wait_ge(s_q, it + 2)
                    act.wait_ge(s_qi, it + 1)
                    nc.scalar.mul(q_f[:], pQ[:], 1.0 / float(np.sqrt(HD))).then_inc(s_qc, 1)

                def evacuate(it):
                    act.wait_ge(s_qtp, it + 2)
                    act.wait_ge(s_qst, 16 * it)
                    nc.scalar.copy(qT_s[:].rearrange("p c g n -> p g c n"), pQT[:]).then_inc(s_qts, 1)
                copies(0)
                copies(1)
                evacuate(0)
                with act.Fori(2, NI_Q) as it:
                    copies(it)
                    evacuate(it - 1)
                evacuate(NI_Q - 1)

            @block.vector
            def _(dve):
                dve.sem_inc(s_qi, 1)
                with dve.Fori(0, NI_Q) as it:
                    LINKS = 5
                    done = [0]

                    def link(ins):
                        done[0] += 1
                        ins.then_inc(s_qch, 1)
                        dve.wait_ge(s_qch, it * LINKS + done[0])
                    dve.wait_ge(s_qc, it + 2)
                    link(nc.vector.tensor_reduce(q_amax[:], heads(q_f[:]), AX.X, ALU.max, apply_absolute_value=True))
                    link(nc.vector.tensor_scalar(q_st[:], q_amax[:], 1.0 / 127.0, EPS_STEP, ALU.mult, ALU.max))
                    link(nc.vector.tensor_copy(q_step[:, 0:UNITS].rearrange("p (h t) -> p t h", h=H)
                                               [:, bass.ds(it * G, G), :], q_st[:]))
                    link(nc.vector.reciprocal(q_rst[:], q_st[:]))
                    link(nc.vector.tensor_tensor(heads(q_a[:]), heads(q_f[:]), spread(q_rst[:]), ALU.mult))
                    dve.wait_ge(s_qtp, it + 1)
                    nc.vector.tensor_scalar(q_int[:], q_a[:], ROUND, ROUND, ALU.add, ALU.subtract).then_inc(s_qi, 1)

            @block.sync
            def _(sp):
                with sp.Fori(0, NI_Q) as it:
                    sp.wait_ge(s_qts, it + 2)
                    sp.dma_start(qT_d.rearrange("(c p) n -> p c n", p=P)[:, :, bass.ds(it * G * P, G * P)],
                                 qT_s[:].rearrange("p c g n -> p c (g n)")).then_inc(s_qst, 16)
                sp.wait_ge(s_qst, 16 * NI_Q)
        qs.close()

        k_area = x_all[:].rearrange("p t d -> p (t d)").bitcast(BF16)
        k_op = [k_area[:, i * NK:(i + 1) * NK] for i in range(2)]
        vs = ExitStack()
        v_amax = sb("v_amax", [P, D], F32, vs)
        v_col = sb("v_col", [P, DC], F32, vs)
        v_step = sb("v_step", [P, DC], F32, vs)
        v_diag = sb("v_diag", [P, DC, P], F32, vs)
        v_rst = sb("v_rst", [P, D], F32, vs)
        pV = ps("pV", [P, DC, P], F32, vs)
        pVB = ps("pVB", [P, D], F32, vs)
        s_v = sem("value_steps", vs)
        s_vp = sem("value_products", vs)
        s_vi = sem("value_integers", vs)
        VB = 8
        with nc.Block() as block:
            @block.gpsimd
            def _(pool):
                for i in range(2):
                    nc.gpsimd.memset(k_op[i].bitcast(F32), 0.0)

            @block.vector
            def _(dve):
                nc.vector.tensor_reduce(v_amax[:], v_f[:].rearrange("p t c -> p c t"), AX.X, ALU.max,
                                        apply_absolute_value=True).then_inc(s_v, 1)
                dve.wait_ge(s_vp, 1)
                nc.vector.tensor_reduce(v_col[:], pV[:], AX.X, ALU.max).then_inc(s_v, 1)
                dve.wait_ge(s_v, 2)
                nc.vector.tensor_scalar(v_step[:], v_col[:], 1.0 / 127.0, EPS_STEP, ALU.mult,
                                        ALU.max).then_inc(s_v, 1)
                dve.wait_ge(s_v, 3)
                for c in range(DC):
                    nc.vector.tensor_scalar(v_diag[:, c, :], ident[:], v_step[:, c:c + 1], None,
                                            ALU.mult).then_inc(s_v, 1)
                    nc.vector.tensor_scalar(wps_sb[:, c, :], wp_sb[:, c, :], v_step[:, c:c + 1], None, ALU.mult)
                dve.wait_ge(s_vp, 2)
                nc.vector.reciprocal(v_rst[:], pVB[:]).then_inc(s_v, 1)
                dve.wait_ge(s_v, 6)
                for b in range(KT // VB):
                    part = v_f[:, b * VB:(b + 1) * VB, :]
                    nc.vector.tensor_tensor(part, part, v_rst[:].unsqueeze(1).to_broadcast([P, VB, D]),
                                            ALU.mult).then_inc(s_vi, 1)
                    dve.wait_ge(s_vi, b + 1)
                    nc.vector.tensor_scalar(v_int[:, b * VB:(b + 1) * VB, :], part, ROUND, ROUND, ALU.add,
                                            ALU.subtract)

            @block.tensor
            def _(pe):
                pe.wait_ge(s_v, 1)
                for c in range(DC):
                    mm = nc.tensor.transpose(pV[:, c, :], v_amax[:, c * P:(c + 1) * P], ident[:])
                mm.then_inc(s_vp, 1)
                pe.wait_ge(s_v, 5)
                for c in range(DC):
                    mm = nc.tensor.matmul(pVB[:, c * P:(c + 1) * P], ones[:], v_diag[:, c, :], start=True, stop=True)
                mm.then_inc(s_vp, 1)
        vs.close()
        pre.close()

        RING = 3
        LAG = 2
        M = [(2 * j, 2 * j + 1) for j in range(6)] + [(b,) for b in range(12, 16)]
        NM = len(M)
        PE_STEPS = ("T6- E0 E1 M0 T7- T0 M1 E2 M2 T1 E3 M3 E4 T2 M4 T3 E5 M5 AV M6 M7 E6 FOLD T4 E7 M8 T5 "
                    "M9").split()
        DVE_STEPS = "M0 C7- M1 M2 C1 DEN M3 C2 INV M4 M5 M6 M7 FIN C4 M8 M9 MAX BIAS C5".split()
        ACT_STEPS = "C6- E0 E1 C0 E2 E3 E4 C3 E5 OC E6 E7".split()
        FILLS = [x for x in PE_STEPS if x[0] in "ME"]
        TURNS = [x for x in PE_STEPS if x[0] == "T" or x == "AV"]
        assert len(FILLS) == NM + NCH and len(FILLS) % RING == 0 and len(TURNS) % 2 == 1
        ON_ACT = sorted(int(x[1]) for x in ACT_STEPS if x[0] == "C")
        ON_DVE = sorted(int(x[1]) for x in DVE_STEPS if x[0] == "C")
        assert sorted(ON_ACT + ON_DVE) == list(range(NCH))
        TPC = CH // P
        LOADS_Q = 16 * 2 * PARTS
        STAGED0, STAGED = 6, 4

        xs = ExitStack()
        q_op = [sb(f"q_op{i}", [P, NT + 2 * P], BF16, xs) for i in range(2)]
        v_op = sb("v_op", [P, KT, 32], BF16, xs)
        q_m = [sb(f"q_m{i}", [P, P], BF16, xs) for i in range(2)]
        q_e = [sb(f"q_e{i}", [P, P], BF16, xs) for i in range(2)]
        step_m = [sb(f"step_m{i}", [P, 1], F32, xs) for i in range(2)]
        step_e = [sb(f"step_e{i}", [P, 1], F32, xs) for i in range(2)]
        n_op = sb("n_op", [P, NK], U16, xs)
        nT = [sb(f"nT{i}", [P, KT, P], BF16, xs) for i in range(2)]
        m_part = [sb(f"m_part{i}", [P, NM], F32, xs) for i in range(2)]
        m_un = [sb(f"m_un{i}", [P, 1], F32, xs) for i in range(2)]
        bias = [sb(f"bias{i}", [P, 1], F32, xs) for i in range(2)]
        e_sum = [sb(f"e_sum{i}", [P, NCH], F32, xs) for i in range(2)]
        den = sb("den", [P, 1], F32, xs)
        rden = sb("rden", [P, 1], F32, xs)
        oT = sb("oT", [P, P], F32, xs)
        fold = sb("fold", [P, HD], F32, xs)
        ring = [ps(f"ring{i}", [P, CH], F32, xs) for i in range(RING)]
        turns = [ps(f"turns{i}", [P, BANK], F32, xs) for i in range(2)]

        s_k = [sem(f"head_keys_loaded{i}", xs) for i in range(2)]
        s_qh = [sem(f"head_queries_loaded{i}", xs) for i in range(2)]
        s_init = sem("initialised", xs)
        s_pad = sem("queries_padded", xs)
        s_clear = sem("transposed_cleared", xs)
        s_fold = sem("fold_ready", xs)
        s_un = sem("unit_staged", xs)
        s_vo = sem("head_values_staged", xs)
        s_m = sem("max_scores_ready", xs)
        s_mu = sem("max_scores_used", xs)
        s_mg = sem("unit_max_ready", xs)
        s_b = sem("bias_ready", xs)
        s_e = sem("exp_scores_ready", xs)
        s_eu = sem("exp_done", xs)
        s_t = sem("chunk_transposed", xs)
        s_td = sem("chunk_copied_by_vector", xs)
        s_ta = sem("chunk_copied_by_scalar", xs)
        s_av = sem("value_product_done", xs)
        s_oc = sem("value_product_copied", xs)
        s_of = sem("value_product_folded", xs)
        s_den = sem("denominator_ready", xs)
        s_rd = sem("reciprocal_ready", xs)
        s_fin = sem("unit_finished", xs)

        def chunks(u, j):
            return (u + 1) * NCH + j + 1

        def maxes(u, i):
            return u * NM + i + 1

        def by(who, u, j):
            return (u + 1) * len(who) + who.index(j) + 1

        def wait_copied(e, u, j):
            if j in ON_ACT:
                e.wait_ge(s_ta, by(ON_ACT, u, j))
            else:
                e.wait_ge(s_td, by(ON_DVE, u, j))

        def slot(name):
            return ring[FILLS.index(name) % RING]

        def turn_bank(x, par):
            return turns[(TURNS.index(x) + par) % 2]

        def chunk_of(x, u):
            return (u - 1, int(x[1])) if x.endswith("-") else (u, int(x[1]))

        def each_unit(eng, period):
            with eng.Fori(0, H // 2) as pair:
                for hp in range(2):
                    h = pair * 2 + hp
                    period(h * QT, pair, h, 0, hp, 0, "first")
                    with eng.Fori(0, QT // 2 - 1) as i:
                        for k in (1, 2):
                            period(h * QT + i * 2 + k, pair, h, i * 2 + k, hp, k % 2, "inner")
                    period(h * QT + QT - 1, pair, h, QT - 1, hp, 1, "last")

        with nc.Block() as block:
            @block.sync
            def _(sp):
                def load(h, i, following):
                    sp.dma_start(k_op[i][0:KR, :], kT_d[bass.ds(h * KR, KR), :]).then_inc(s_k[i], 16)
                    for r in range(PARTS):
                        rows = slice(r * HD, (r + 1) * HD)
                        sp.dma_start(q_op[i][rows, 0:NT], qT_d[bass.ds(h * HD, HD), :]).then_inc(s_qh[i], 16)
                        sp.dma_start(q_op[i][rows, NT:NT + 2 * P],
                                     qT_d[bass.ds(following * HD, HD), 0:2 * P]).then_inc(s_qh[i], 16)

                def reload(h, i, following):
                    last = (h - 1) * QT - 1
                    sp.wait_ge(s_e, chunks(last, NCH - 1))
                    sp.wait_ge(s_un, STAGED0 + STAGED * (last + 1))
                    load(h, i, following)
                sp.wait_ge(s_pad, 2)
                load(0, 0, 1)
                load(1, 1, 2)
                with sp.Fori(1, H // 2 - 1) as pair:
                    reload(pair * 2, 0, pair * 2 + 1)
                    reload(pair * 2 + 1, 1, pair * 2 + 2)
                reload(H - 2, 0, H - 1)
                reload(H - 1, 1, 0)
                sp.wait_ge(s_e, chunks((H - 1) * QT - 1, NCH - 1))
                sp.dma_start(k_op[0][0:KR, :], kT_d[0:KR, :]).then_inc(s_k[0], 16)
                sp.wait_ge(s_k[0], 16 * (H // 2 + 1))
                sp.wait_ge(s_k[1], 16 * (H // 2))
                for i in range(2):
                    sp.wait_ge(s_qh[i], LOADS_Q * (H // 2))

            @block.gpsimd
            def _(pool):
                nc.gpsimd.memset(n_op[:, (NCH - LAG) * CH:NK], 0.0).then_inc(s_init, 1)
                nc.gpsimd.memset(e_sum[1][:], 1.0).then_inc(s_init, 1)
                nc.gpsimd.memset(q_step[:, UNITS:UNITS + 2], 0.0).then_inc(s_init, 1)
                nc.gpsimd.memset(v_op[:], 0.0).then_inc(s_init, 1)
                pool.wait_ge(s_init, 4)
                pool.sem_inc(s_vo, 1)

                def stage(u, t, hp, q_to, step_to):
                    nc.gpsimd.tensor_copy(step_to[:], q_step[:, bass.ds(u, 1)]).then_inc(s_un, 1)
                    nc.gpsimd.tensor_copy(q_to[:], q_op[hp][:, bass.ds(t * P, P)]).then_inc(s_un, 1)
                pool.wait_ge(s_qh[0], LOADS_Q)
                stage(0, 0, 0, q_m[0], step_m[0])
                stage(1, 1, 0, q_m[1], step_m[1])
                stage(0, 0, 0, q_e[0], step_e[0])

                def period(u, pair, h, t, hp, par, where):
                    if where == "first":
                        pool.wait_ge(s_qh[hp], LOADS_Q * (pair + 1))
                    pool.wait_ge(s_eu, chunks(u - 1, NCH - 1))
                    pool.wait_ge(s_b, u + 1)
                    stage(u + 2, t + 2, hp, q_m[par], step_m[par])
                    stage(u + 1, t + 1, hp, q_e[1 - par], step_e[1 - par])
                    if where == "first":
                        pool.wait_ge(s_av, u + 2)
                        nc.gpsimd.tensor_copy(v_op[:, :, 0:HD],
                                              v_int[:, :, bass.ds(h * HD, HD)]).then_inc(s_vo, 1)
                each_unit(pool, period)

            @block.tensor
            def _(pe):
                def scores(name, q_un, keys, ready):
                    j = int(name[1])
                    for n, b in enumerate(M[j] if name[0] == "M" else (2 * j, 2 * j + 1)):
                        mm = nc.tensor.matmul(slot(name)[:, n * BANK:(n + 1) * BANK], q_un[:],
                                              keys[:, b * BANK:(b + 1) * BANK], start=True, stop=True)
                    mm.then_inc(ready, 1)

                def fill(name, p, q_un, keys, ready):
                    at = FILLS.index(name)
                    before = FILLS[at - RING]
                    q = p if at >= RING else p - 1
                    if before[0] == "E":
                        pe.wait_ge(s_eu, chunks(q, int(before[1])))
                    else:
                        pe.wait_ge(s_mu, maxes(q + 1, int(before[1])))
                    scores(name, q_un, keys, ready)

                def wait_turn(x, p):
                    k = TURNS.index(x) - 2
                    before, q = TURNS[k], p if k >= 0 else p - 1
                    if before == "AV":
                        pe.wait_ge(s_fin, q + 2)
                    else:
                        wait_copied(pe, *chunk_of(before, q))

                def transposes(x, p, par):
                    u, j = chunk_of(x, p)
                    pe.wait_ge(s_eu, chunks(u, j))
                    wait_turn(x, p)
                    to = turn_bank(x, par).bitcast(BF16)
                    for b in range(TPC):
                        at = j * CH + b * P
                        mm = nc.tensor.transpose(to[:, b * P:(b + 1) * P], n_op[:, at:at + P].bitcast(BF16), ident_h[:])
                    mm.then_inc(s_t, 1)

                def value_product(u, par, buf):
                    pe.wait_ge(s_ta, by(ON_ACT, u, ON_ACT[-1]))
                    pe.wait_ge(s_td, by(ON_DVE, u, ON_DVE[-1]))
                    to = turn_bank("AV", par)
                    for b in range(KT):
                        mm = nc.tensor.matmul(to[32 * (b % CG):32 * (b % CG) + 32, 0:P], v_op[:, b, :],
                                              nT[buf][:, b, :], start=b < CG, stop=b >= KT - CG)
                    mm.then_inc(s_av, 1)

                def fold_groups(u, par):
                    pe.wait_ge(s_oc, u + 2)
                    nc.tensor.matmul(turn_bank("AV", par)[:, P:P + HD], oT[:], fold[:], start=True,
                                     stop=True).then_inc(s_of, 1)

                def period(u, pair, h, t, hp, par, where):
                    pe.wait_ge(s_un, STAGED0 + STAGED * u)
                    if where == "last":
                        pe.wait_ge(s_k[1 - hp], 16 * (pair + 1 + hp))
                    for x in PE_STEPS:
                        if x[0] == "M":
                            fill(x, u, q_m[1 - par], k_op[1 - hp if where == "last" else hp], s_m)
                        elif x[0] == "E":
                            fill(x, u, q_e[par], k_op[hp], s_e)
                        elif x[0] == "T":
                            transposes(x, u, par)
                        elif x == "AV":
                            pe.wait_ge(s_vo, h + 1 if where == "first" else h + 2)
                            wait_turn(x, u)
                            value_product(u - 1, par, 1 - par)
                        else:
                            fold_groups(u - 1, par)
                pe.sem_inc(s_e, NCH)
                pe.sem_inc(s_t, NCH - LAG)
                pe.sem_inc(s_av, 1)
                pe.sem_inc(s_of, 1)
                pe.wait_ge(s_init, 4)
                pe.wait_ge(s_clear, 1)
                pe.wait_ge(s_fold, CG)
                pe.wait_ge(s_un, STAGED0)
                pe.wait_ge(s_k[0], 16)
                for i in range(NM):
                    same = [m for m in range(i) if slot(f"M{m}") is slot(f"M{i}")]
                    if same:
                        pe.wait_ge(s_mu, same[-1] + 1)
                    scores(f"M{i}", q_m[0], k_op[0], s_m)
                each_unit(pe, period)
                for x in PE_STEPS:
                    if x.endswith("-"):
                        transposes(x, UNITS, 0)
                value_product(UNITS - 1, 0, 1)
                fold_groups(UNITS - 1, 0)

            @block.vector
            def _(dve):
                def chunk_max(u, i, par):
                    dve.wait_ge(s_m, maxes(u, i))
                    nc.vector.tensor_reduce(m_part[par][:, i:i + 1], slot(f"M{i}")[:, 0:len(M[i]) * BANK],
                                            AX.X, ALU.max).then_inc(s_mu, 1)

                def unit_max(u, par):
                    dve.wait_ge(s_mu, maxes(u, NM - 1))
                    nc.vector.tensor_reduce(m_un[par][:], m_part[par][:], AX.X, ALU.max, negate=True).then_inc(s_mg, 1)

                def make_bias(u, par):
                    dve.wait_ge(s_mg, u + 1)
                    nc.vector.tensor_scalar(bias[par][:], m_un[par][:], step_m[par][:], LN255, ALU.mult,
                                            ALU.add).then_inc(s_b, 1)

                def copy_chunk(x, p, par):
                    u, j = chunk_of(x, p)
                    buf = 1 - par if x.endswith("-") else par
                    if j == ON_DVE[0]:
                        dve.wait_ge(s_av, u + 1)
                    dve.wait_ge(s_t, chunks(u, j))
                    nc.vector.tensor_copy(nT[buf][:, j * TPC:(j + 1) * TPC, :].rearrange("p a b -> p (a b)"),
                                          turn_bank("T" + x[1:], par).bitcast(U16)).then_inc(s_td, 1)

                def denominator(u, buf):
                    dve.wait_ge(s_eu, chunks(u, NCH - 1))
                    dve.wait_ge(s_rd, u + 2)
                    nc.vector.tensor_reduce(den[:], e_sum[buf][:], AX.X, ALU.add).then_inc(s_den, 1)

                def invert(u):
                    dve.wait_ge(s_den, u + 3)
                    dve.wait_ge(s_fin, u + 2)
                    nc.vector.reciprocal(rden[:], den[:]).then_inc(s_rd, 1)

                def finish(u, par):
                    dve.wait_ge(s_of, u + 3)
                    dve.wait_ge(s_rd, u + 3)
                    nc.vector.tensor_scalar(att[:, bass.ds(u + 1, 1), :].rearrange("p a d -> p (a d)"),
                                            turn_bank("AV", par)[:, P:P + HD],
                                            rden[:], None, ALU.mult).then_inc(s_fin, 1)

                def period(u, pair, h, t, hp, par, where):
                    dve.wait_ge(s_un, STAGED0 + STAGED * u)
                    for x in DVE_STEPS:
                        if x == "MAX":
                            unit_max(u + 1, 1 - par)
                        elif x == "INV":
                            invert(u - 1)
                        elif x[0] == "M":
                            chunk_max(u + 1, int(x[1]), 1 - par)
                        elif x[0] == "C":
                            copy_chunk(x, u, par)
                        elif x == "DEN":
                            denominator(u - 1, 1 - par)
                        elif x == "FIN":
                            finish(u - 1, par)
                        else:
                            make_bias(u + 1, 1 - par)
                for s in (s_den, s_rd, s_fin):
                    dve.sem_inc(s, 1)
                dve.sem_inc(s_td, sum(j < NCH - LAG for j in ON_DVE))
                for i in range(2):
                    nc.vector.memset(q_op[i][:].bitcast(F32), 0.0).then_inc(s_pad, 1)
                nc.vector.memset(nT[1][:, 0:(NCH - LAG) * TPC, :], 0.0).then_inc(s_clear, 1)
                for g in range(CG):
                    nc.vector.tensor_copy(fold[32 * g:32 * g + 32, :],
                                          ident[32 * g:32 * g + 32, 32 * g:32 * g + HD]).then_inc(s_fold, 1)
                dve.wait_ge(s_un, STAGED0)
                for i in range(NM):
                    chunk_max(0, i, 0)
                unit_max(0, 0)
                make_bias(0, 0)
                each_unit(dve, period)
                for x in DVE_STEPS:
                    if x.endswith("-"):
                        copy_chunk(x, UNITS, 0)
                denominator(UNITS - 1, 1)
                invert(UNITS - 1)
                finish(UNITS - 1, 0)

            @block.scalar
            def _(act):
                def exponential(u, j, par):
                    if j == 0:
                        act.wait_ge(s_b, u + 1)
                        act.wait_ge(s_un, STAGED0 + STAGED * u)
                        act.wait_ge(s_den, u + 1)
                    act.wait_ge(s_e, chunks(u, j))
                    act.wait_ge(s_t, chunks(u - 1, j))
                    nc.scalar.activation(n_op[:, j * CH:(j + 1) * CH], slot(f"E{j}")[:], ACT.Exp, bias=bias[par][:],
                                         scale=step_e[par][:], accum_out=e_sum[par][:, j:j + 1]).then_inc(s_eu, 1)

                def copy_chunk(x, p, par):
                    u, j = chunk_of(x, p)
                    buf = 1 - par if x.endswith("-") else par
                    if j == ON_ACT[0]:
                        act.wait_ge(s_av, u + 1)
                    act.wait_ge(s_t, chunks(u, j))
                    nc.scalar.copy(nT[buf][:, j * TPC:(j + 1) * TPC, :].rearrange("p a b -> p (a b)"),
                                   turn_bank("T" + x[1:], par).bitcast(U16)).then_inc(s_ta, 1)

                def copy_product(u, par):
                    act.wait_ge(s_av, u + 3)
                    act.wait_ge(s_of, u + 2)
                    nc.scalar.copy(oT[:], turn_bank("AV", par)[:, 0:P]).then_inc(s_oc, 1)

                def period(u, pair, h, t, hp, par, where):
                    for x in ACT_STEPS:
                        if x[0] == "E":
                            exponential(u, int(x[1]), par)
                        elif x[0] == "C":
                            copy_chunk(x, u, par)
                        else:
                            copy_product(u - 1, par)
                act.sem_inc(s_eu, NCH)
                act.sem_inc(s_ta, sum(j < NCH - LAG for j in ON_ACT))
                each_unit(act, period)
                for x in ACT_STEPS:
                    if x.endswith("-"):
                        copy_chunk(x, UNITS, 0)
                copy_product(UNITS - 1, 0)
        xs.close()

        pj = ExitStack()
        a_o = [sb(f"a_o{i}", [P, D], F32, pj) for i in range(2)]
        aT = [sb(f"aT{i}", [P, DC, P], F32, pj) for i in range(2)]
        bp_all = sb("bp_all", [P, D], F32, pj)
        pA = [ps(f"pA{i}", [P, DC, P], F32, pj) for i in range(2)]
        pY = [ps(f"pY{i}", [P, D], F32, pj) for i in range(2)]
        s_g = sem("heads_gathered", pj)
        s_at = sem("heads_transposed", pj)
        s_ac = sem("heads_transposed_copied", pj)
        s_y = sem("projected", pj)
        s_r = sem("projection_added", pj)
        s_xb = sem("bias_added", pj)
        s_xa = sem("x_and_bias_loaded", pj)
        with nc.Block() as block:
            @block.sync
            def _(sp):
                sp.dma_start(x_all[:], x_t).then_inc(s_xa, 16)
                sp.dma_start(bp_all[:], a["L0_xattn_bp"].rearrange("(a n) -> a n", a=1).to_broadcast([P, D])
                             ).then_inc(s_xa, 16)

            @block.gpsimd
            def _(pool):
                pool.sem_inc(s_g, START)
                with pool.Fori(0, QT // 2) as k:
                    for i in range(2):
                        t = k * 2 + i
                        pool.wait_ge(s_at, after(t - 2))
                        nc.gpsimd.tensor_copy(a_o[i][:].rearrange("p (h d) -> p h d", d=HD),
                                              att[:, 1:UNITS + 1, :].rearrange("p (h t) d -> p h t d", h=H)
                                              [:, :, bass.ds(t, 1), :].rearrange("p h a d -> p h (a d)")
                                              ).then_inc(s_g, 1)

            @block.tensor
            def _(pe):
                pe.sem_inc(s_at, START)
                pe.sem_inc(s_y, START)

                def turn(t, i):
                    pe.wait_ge(s_g, after(t))
                    pe.wait_ge(s_ac, after(t - 2))
                    for c in range(DC):
                        mm = nc.tensor.transpose(pA[i][:, c, :], a_o[i][:, c * P:(c + 1) * P], ident[:])
                    mm.then_inc(s_at, 1)

                def project(t, i):
                    pe.wait_ge(s_ac, after(t))
                    pe.wait_ge(s_r, after(t - 2))
                    for c in range(DC):
                        mm = nc.tensor.matmul(pY[i], aT[i][:, c, :], wps_sb[:, c, :], start=c == 0, stop=c == DC - 1)
                    mm.then_inc(s_y, 1)
                turn(0, 0)
                with pe.Fori(0, QT // 2 - 1) as k:
                    for i in range(2):
                        turn(k * 2 + i + 1, 1 - i)
                        project(k * 2 + i, i)
                turn(QT - 1, 1)
                project(QT - 2, 0)
                project(QT - 1, 1)

            @block.scalar
            def _(act):
                act.sem_inc(s_ac, START)
                with act.Fori(0, QT // 2) as k:
                    for i in range(2):
                        t = k * 2 + i
                        act.wait_ge(s_at, after(t))
                        act.wait_ge(s_y, after(t - 2))
                        nc.scalar.copy(aT[i][:], pA[i]).then_inc(s_ac, 1)

            @block.vector
            def _(dve):
                dve.sem_inc(s_r, START)
                dve.wait_ge(s_xa, 2 * 16)
                nc.vector.tensor_tensor(x_all[:], x_all[:], bp_all[:].unsqueeze(1).to_broadcast([P, QT, D]),
                                        ALU.add).then_inc(s_xb, 1)
                dve.wait_ge(s_xb, 1)
                with dve.Fori(0, QT // 2) as k:
                    for i in range(2):
                        t = k * 2 + i
                        row = x_all[:, bass.ds(t, 1), :].rearrange("p a d -> p (a d)")
                        dve.wait_ge(s_y, after(t))
                        nc.vector.tensor_tensor(row, row, pY[i], ALU.add).then_inc(s_r, 1)
        pj.close()
        mid.close()

        B = 64
        NB = P // B
        KH = 4
        GH = H // KH
        KD = KH * HD
        QK = D + KD
        HC = P // HD
        RMS_EPS = 1e-6
        layer_norm("first")

        sa = ExitStack()
        wqkv_sb = sb("wqkv_sb", [P, DC, QK + KD], F32, sa)
        wo_sb = sb("wo_sb", [P, DC, D], F32, sa)
        rope = sb("rope", [P, 2, HD], F32, sa)
        qkv = sb("qkv", [P, QT, QK + KD], F32, sa)
        v_sw = sb("v_sw", [P, QT, KD], F32, sa)
        squares = sb("squares", [P, QT, 2], F32, sa)
        rms = sb("rms", [P, QT, 2], F32, sa)
        rms_r = sb("rms_r", [P, QT, 2], F32, sa)
        rms_eps = sb("rms_eps", [P, 1], F32, sa)
        head_mask = sb("head_mask", [P, HC], F32, sa)

        s1 = ExitStack()
        y_n = [sb(f"y_n{i}", [P, D], F32, s1) for i in range(2)]
        yT = [sb(f"yT{i}", [P, DC, P], F32, s1) for i in range(2)]
        sq_out = sb("sq_out", [P, D], F32, s1)
        pB = [ps(f"pB{i}", [P, DC, P], F32, s1) for i in range(2)]
        pC = [ps(f"pC{i}", [P, BANK], F32, s1) for i in range(2)]
        pS = [ps(f"pS{i}", [P, KD], F32, s1) for i in range(2)]
        s_sw = sem("self_weights_loaded", s1)
        s_yn = sem("self_normalised", s1)
        s_yt = sem("self_transposed", s1)
        s_yc = sem("self_transposed_copied", s1)
        s_pr = sem("self_projected", s1)
        s_sq = sem("self_squares", s1)
        s_cp = sem("self_projections_copied", s1)
        s_rm = sem("self_rms", s1)
        s_rs = sem("self_rms_root", s1)
        s_ep = sem("self_rms_eps_filled", s1)
        with nc.Block() as block:
            @block.sync
            def _(sp):
                at = 0
                for src in (a["L0_attn_Wq"], a["L0_attn_Wk"], a["L0_attn_Wv"]):
                    n = src.shape[1]
                    sp.dma_start(wqkv_sb[:, :, at:at + n], src.rearrange("(c p) n -> p c n", p=P)).then_inc(s_sw, 16)
                    at += n
                sp.dma_start(wo_sb[:], a["L0_attn_Wout"].rearrange("(c p) n -> p c n", p=P)).then_inc(s_sw, 16)
                sp.dma_start(rope[:], a["rope"]).then_inc(s_sw, 16)
                sp.wait_ge(s_sw, 5 * 16)

            @block.gpsimd
            def _(pool):
                nc.gpsimd.memset(rms_eps[:], RMS_EPS).then_inc(s_ep, 1)
                for t in range(QT):
                    if t >= 2:
                        pool.wait_ge(s_yt, t - 1)
                    nc.gpsimd.tensor_scalar(y_n[t % 2][:], x_all[:, t, :], mean_var[:, t, 0:1], rstd[:, t:t + 1],
                                            ALU.subtract, ALU.mult).then_inc(s_yn, 1)

            @block.tensor
            def _(pe):
                def turn(t, i):
                    pe.wait_ge(s_yn, t + 1)
                    for c in range(DC):
                        mm = nc.tensor.transpose(pB[i][:, c, :], y_n[i][:, c * P:(c + 1) * P], ident[:])
                    mm.then_inc(s_yt, 1)

                def project(t, i):
                    pe.wait_ge(s_yc, t + 2)
                    for c in range(DC):
                        nc.tensor.matmul(pC[i][:, 0:QK + KD], yT[i][:, c, :], wqkv_sb[:, c, :],
                                         start=c == 0, stop=c == DC - 1)
                    for b in range(NB):
                        for c in range(DC):
                            mm = nc.tensor.matmul(pS[i][b * B:(b + 1) * B, :],
                                                  yT[i][:, c, (1 - b) * B:(2 - b) * B],
                                                  wqkv_sb[:, c, QK:QK + KD], start=c == 0, stop=c == DC - 1)
                    mm.then_inc(s_pr, 1)
                pe.wait_ge(s_sw, 5 * 16)
                turn(0, 0)
                with pe.Fori(0, QT // 2 - 1) as k:
                    for i in range(2):
                        t = k * 2 + i
                        pe.wait_ge(s_yc, t + 1)
                        turn(t + 1, 1 - i)
                        pe.wait_ge(s_cp, 2 * after(t - 2))
                        project(t, i)
                pe.wait_ge(s_yc, QT - 1)
                turn(QT - 1, 1)
                for i in range(2):
                    pe.wait_ge(s_cp, 2 * after(QT - 4 + i))
                    project(QT - 2 + i, i)

            @block.scalar
            def _(act):
                act.sem_inc(s_yc, 1)
                act.sem_inc(s_sq, 1)

                def copy_tokens(t, i):
                    act.wait_ge(s_yt, t + 1)
                    nc.scalar.copy(yT[i][:], pB[i][:]).then_inc(s_yc, 1)

                def square(t, i):
                    act.wait_ge(s_pr, t + 1)
                    for n, (lo, hi) in enumerate(((0, D), (D, QK))):
                        act.wait_ge(s_sq, 2 * t + n + 1)
                        nc.scalar.activation(sq_out[:, 0:hi - lo], pC[i][:, lo:hi], ACT.Square,
                                             accum_out=squares[:, bass.ds(t, 1), n:n + 1].rearrange("p a b -> p (a b)")
                                             ).then_inc(s_sq, 1)
                copy_tokens(0, 0)
                with act.Fori(0, QT // 2 - 1) as k:
                    for i in range(2):
                        copy_tokens(k * 2 + i + 1, 1 - i)
                        square(k * 2 + i, i)
                copy_tokens(QT - 1, 1)
                square(QT - 2, 0)
                square(QT - 1, 1)
                act.wait_ge(s_rm, 1)
                nc.scalar.activation(rms[:], squares[:], ACT.Sqrt, bias=rms_eps[:]).then_inc(s_rs, 1)

            @block.vector
            def _(dve):
                dve.sem_inc(s_cp, 2 * START)
                with dve.Fori(0, QT // 2) as k:
                    for i in range(2):
                        t = k * 2 + i
                        dve.wait_ge(s_pr, t + 1)
                        dve.wait_ge(s_sq, 2 * t + 3)
                        nc.vector.tensor_copy(qkv[:, bass.ds(t, 1), :].rearrange("p a n -> p (a n)"),
                                              pC[i][:, 0:QK + KD]).then_inc(s_cp, 1)
                        nc.vector.tensor_copy(v_sw[:, bass.ds(t, 1), :].rearrange("p a n -> p (a n)"),
                                              pS[i][:]).then_inc(s_cp, 1)
                for n, width in enumerate((D, KD)):
                    last = nc.vector.tensor_scalar(squares[:, :, n], squares[:, :, n], 1.0 / width, None, ALU.mult)
                last.then_inc(s_rm, 1)
                nc.vector.tensor_reduce(head_mask[:], ident[:].rearrange("p (h d) -> p h d", d=HD), AX.X, ALU.add)
                dve.wait_ge(s_rs, 1)
                nc.vector.reciprocal(rms_r[:], rms[:]).then_inc(s_rm, 1)
                dve.wait_ge(s_rm, 2)
                nc.vector.tensor_scalar(rms_r[:, :, 0], rms_r[:, :, 0], 1.0 / float(np.sqrt(HD)), None, ALU.mult)
                nc.vector.tensor_tensor(qkv[:, :, D:QK], qkv[:, :, D:QK],
                                        rms_r[:, :, 1:2].to_broadcast([P, QT, KD]), ALU.mult)
        s1.close()

        RT = 4
        s2 = ExitStack()
        rot = [sb(f"rot{i}", [P, RT, QK], F32, s2) for i in range(2)]
        s_ro = sem("rotated_half", s2)
        s_rc = sem("rotated_cosine", s2)
        with nc.Block() as block:
            cos, sin = rope[:, 0, :], rope[:, 1, :]
            HH = HD // 2

            @block.vector
            def _(dve):
                for n in range(QT // RT):
                    qk = qkv[:, n * RT:(n + 1) * RT, 0:QK].rearrange("p t (h d) -> p t h d", d=HD)
                    r = rot[n % 2][:].rearrange("p t (h d) -> p t h d", d=HD)
                    for half in range(2):
                        to, frm = slice(half * HH, (half + 1) * HH), slice((1 - half) * HH, (2 - half) * HH)
                        nc.vector.tensor_tensor(r[:, :, :, to], qk[:, :, :, frm],
                                                sin[:, to].unsqueeze(1).unsqueeze(1).to_broadcast(
                                                    [P, RT, QK // HD, HH]), ALU.mult).then_inc(s_ro, 1)
                    dve.wait_ge(s_ro, 2 * n + 2)
                    nc.vector.tensor_tensor(qk, qk, cos.unsqueeze(1).unsqueeze(1).to_broadcast([P, RT, QK // HD, HD]),
                                            ALU.mult).then_inc(s_rc, 1)
                    dve.wait_ge(s_rc, n + 1)
                    nc.vector.tensor_tensor(qk, qk, r, ALU.add)
        s2.close()

        s3 = ExitStack()
        k_rep = [sb(f"k_rep{i}", [P, H, HD], F32, s3) for i in range(2)]
        q_s = [sb(f"q_s{i}", [P, D], F32, s3) for i in range(2)]
        qT = [sb(f"qT{i}", [P, DC, P], F32, s3) for i in range(2)]
        kT = [sb(f"kT{i}", [P, DC, P], F32, s3) for i in range(2)]
        k_bd = [sb(f"k_bd{i}", [P, DC, NB, HC, B], F32, s3) for i in range(2)]
        v_bd = [sb(f"v_bd{i}", [P, NB, KH, 2, HD], F32, s3) for i in range(2)]
        l_max = sb("l_max", [P, H], F32, s3)
        l_sub = [sb(f"l_sub{i}", [P, H, B], F32, s3) for i in range(2)]
        prob = [sb(f"prob{i}", [P, H, B], F32, s3) for i in range(2)]
        p_sum = sb("p_sum", [P, H], F32, s3)
        p_rec = sb("p_rec", [P, H], F32, s3)
        pT_s = sb("pT_s", [P, H // 2, P], F32, s3)
        enc = sb("enc", [P, H, HD], F32, s3)
        eT = sb("eT", [P, DC, P], F32, s3)
        pK = ps("pK", [P, 2, DC, P], F32, s3)
        pL = [ps(f"pL{i}", [P, H, B], F32, s3) for i in range(2)]
        pP = ps("pP", [P, H // 2, P], F32, s3)
        p_last = ps("p_last", [P, 2, D], F32, s3)
        pE, pF, pG = p_last[:, 0, :], p_last[:, 1, :].rearrange("p (c n) -> p c n", n=P), p_last[:, 0, :]
        s_kr = sem("tile_queries_and_keys_staged", s3)
        s_qk = sem("qk_transposed", s3)
        s_qkc = sem("qk_transposed_copied", s3)
        s_bd = sem("keys_placed", s3)
        s_vz = sem("values_cleared", s3)
        s_vb = sem("values_placed", s3)
        s_l = sem("logits_ready", s3)
        s_lc = sem("softmax_steps", s3)
        s_lm = sem("logit_maximum", s3)
        s_ls = sem("logits_shifted", s3)
        s_p = sem("probabilities_ready", s3)
        s_pt = sem("probabilities_transposed", s3)
        s_pc = sem("probabilities_copied", s3)
        s_en = sem("values_mixed", s3)
        s_ec = sem("mixed_normalised", s3)
        s_et = sem("mixed_transposed", s3)
        s_ect = sem("mixed_transposed_copied", s3)
        s_o = sem("self_output_ready", s3)
        s_x2 = sem("self_residual_added", s3)
        with nc.Block() as block:
            def pipelined(eng, step):
                with eng.Fori(0, QT // 2 - 2) as k:
                    for i in range(2):
                        step(k * 2 + i, i, 3)
                for t in range(QT - 4, QT):
                    step(t, t % 2, QT - 1 - t)

            @block.gpsimd
            def _(pool):
                pool.sem_inc(s_bd, DC * NB * START)
                for i in range(2):
                    nc.gpsimd.memset(v_bd[i][:], 0.0).then_inc(s_vz, 1)

                def place_keys(t, i):
                    pool.wait_ge(s_qkc, after(t))
                    pool.wait_ge(s_l, after(t - 2))
                    for c in range(DC):
                        for b in range(NB):
                            nc.gpsimd.tensor_tensor(
                                k_bd[i][:, c, b], kT[i][:, c, b * B:(b + 1) * B].unsqueeze(1).to_broadcast([P, HC, B]),
                                head_mask[:].unsqueeze(2).to_broadcast([P, HC, B]), ALU.mult).then_inc(s_bd, 1)

                def step(t, i, left):
                    if left >= 2:
                        place_keys(t + 2, i)
                place_keys(0, 0)
                place_keys(1, 1)
                pipelined(pool, step)

            @block.tensor
            def _(pe):
                for s in (s_qk, s_l, s_pt, s_en, s_et, s_o):
                    pe.sem_inc(s, START)

                def keys(t, i):
                    pe.wait_ge(s_kr, after(t))
                    pe.wait_ge(s_qkc, after(t - 1))
                    for c in range(DC):
                        nc.tensor.transpose(pK[:, 0, c, :], q_s[i][:, c * P:(c + 1) * P], ident[:])
                        mm = nc.tensor.transpose(pK[:, 1, c, :], k_rep[i][:].rearrange("p h d -> p (h d)")
                                                 [:, c * P:(c + 1) * P], ident[:])
                    mm.then_inc(s_qk, 1)

                def logits(t, i):
                    pe.wait_ge(s_bd, DC * NB * after(t))
                    pe.wait_ge(s_ls, after(t - 2))
                    for c in range(DC):
                        for b in range(NB):
                            mm = nc.tensor.matmul(pL[i][b * B:(b + 1) * B, c * HC:(c + 1) * HC, :],
                                                  qT[i][:, c, b * B:(b + 1) * B], k_bd[i][:, c, b],
                                                  start=True, stop=True)
                    mm.then_inc(s_l, 1)

                def turn_probabilities(t, i):
                    pe.wait_ge(s_p, after(t))
                    pe.wait_ge(s_pc, after(t - 1))
                    for h in range(H // 2):
                        mm = nc.tensor.transpose(pP[:, h, :], prob[i][:, 2 * h:2 * h + 2, :]
                                                 .rearrange("p h s -> p (h s)"), ident[:])
                    mm.then_inc(s_pt, 1)

                def mix(t, i):
                    pe.wait_ge(s_pc, after(t))
                    pe.wait_ge(s_vb, 2 * NB * after(t))
                    pe.wait_ge(s_x2, after(t - 1))
                    for b in range(NB):
                        for h in range(H // 2):
                            mm = nc.tensor.matmul(pE[b * B:(b + 1) * B, 2 * h * HD:(2 * h + 2) * HD],
                                                  pT_s[:, h, b * B:(b + 1) * B],
                                                  v_bd[i][:, b, 2 * h // GH].rearrange("p a d -> p (a d)"),
                                                  start=True, stop=True)
                    mm.then_inc(s_en, 1)

                def turn_mixed(t):
                    pe.wait_ge(s_ec, after(t))
                    for c in range(DC):
                        mm = nc.tensor.transpose(pF[:, c, :], enc[:].rearrange("p h d -> p (h d)")
                                                 [:, c * P:(c + 1) * P], ident[:])
                    mm.then_inc(s_et, 1)

                def output(t):
                    pe.wait_ge(s_ect, after(t))
                    for c in range(DC):
                        mm = nc.tensor.matmul(pG, eT[:, c, :], wo_sb[:, c, :], start=c == 0, stop=c == DC - 1)
                    mm.then_inc(s_o, 1)

                def step(t, i, left):
                    turn_probabilities(t, i)
                    if left >= 1:
                        logits(t + 1, 1 - i)
                    mix(t, i)
                    if left >= 2:
                        keys(t + 2, i)
                    turn_mixed(t)
                    output(t)
                keys(0, 0)
                keys(1, 1)
                logits(0, 0)
                pipelined(pe, step)

            @block.scalar
            def _(act):
                for s in (s_kr, s_qkc, s_p, s_pc, s_ect):
                    act.sem_inc(s, START)

                def gather(t, i):
                    act.wait_ge(s_qk, after(t - 2))
                    nc.scalar.copy(q_s[i][:], qkv[:, bass.ds(t, 1), 0:D].rearrange("p a n -> p (a n)"))
                    k_src = qkv[:, bass.ds(t, 1), D:QK].rearrange("p a (k d) -> p (a k) d", d=HD)
                    nc.scalar.copy(k_rep[i][:].rearrange("p (k g) d -> p k g d", g=GH),
                                   k_src.unsqueeze(2).to_broadcast([P, KH, GH, HD])).then_inc(s_kr, 1)

                def copy_keys(t, i):
                    act.wait_ge(s_qk, after(t))
                    act.wait_ge(s_l, after(t - 2))
                    act.wait_ge(s_bd, DC * NB * after(t - 2))
                    nc.scalar.copy(qT[i][:], pK[:, 0])
                    nc.scalar.copy(kT[i][:], pK[:, 1]).then_inc(s_qkc, 1)

                def exponential(t, i):
                    act.wait_ge(s_ls, after(t))
                    act.wait_ge(s_pt, after(t - 2))
                    act.wait_ge(s_lc, 2 * after(t - 2))
                    nc.scalar.activation(prob[i][:], l_sub[i][:], ACT.Exp,
                                         scale=rms_r[:, bass.ds(t, 1), 0:1].rearrange("p a b -> p (a b)")
                                         ).then_inc(s_p, 1)

                def step(t, i, left):
                    act.wait_ge(s_pt, after(t))
                    act.wait_ge(s_en, after(t - 1))
                    nc.scalar.copy(pT_s[:], pP[:]).then_inc(s_pc, 1)
                    if left >= 3:
                        gather(t + 3, 1 - i)
                    if left >= 2:
                        copy_keys(t + 2, i)
                    act.wait_ge(s_et, after(t))
                    act.wait_ge(s_o, after(t - 1))
                    nc.scalar.copy(eT[:], pF).then_inc(s_ect, 1)
                    if left >= 1:
                        exponential(t + 1, 1 - i)
                gather(0, 0)
                gather(1, 1)
                copy_keys(0, 0)
                gather(2, 0)
                copy_keys(1, 1)
                exponential(0, 0)
                pipelined(act, step)

            @block.vector
            def _(dve):
                for s, n in ((s_vb, 2 * NB), (s_lm, 1), (s_ls, 1), (s_lc, 2), (s_ec, 1), (s_x2, 1)):
                    dve.sem_inc(s, n * START)
                dve.wait_ge(s_vz, 2)

                def place_values(t, i):
                    own = qkv[:, bass.ds(t, 1), QK:QK + KD].rearrange("p a (k d) -> p (a k) d", d=HD)
                    other = v_sw[:, bass.ds(t, 1), :].rearrange("p a (k d) -> p (a k) d", d=HD)
                    dve.wait_ge(s_en, after(t - 2))
                    for b in range(NB):
                        for half in range(2):
                            rows = slice(half * B, (half + 1) * B)
                            src = own if b == half else other
                            nc.vector.tensor_copy(v_bd[i][rows, b, :, half, :], src[rows]).then_inc(s_vb, 1)

                def maximum(t, i):
                    dve.wait_ge(s_l, after(t))
                    nc.vector.tensor_reduce(l_max[:], pL[i][:], AX.X, ALU.max).then_inc(s_lm, 1)

                def shift(t, i):
                    dve.wait_ge(s_lm, after(t))
                    dve.wait_ge(s_p, after(t - 2))
                    nc.vector.tensor_tensor(l_sub[i][:], pL[i][:], l_max[:].unsqueeze(2).to_broadcast([P, H, B]),
                                            ALU.subtract).then_inc(s_ls, 1)

                def step(t, i, left):
                    dve.wait_ge(s_p, after(t))
                    nc.vector.tensor_reduce(p_sum[:], prob[i][:], AX.X, ALU.add).then_inc(s_lc, 1)
                    dve.wait_ge(s_lc, 2 * after(t - 1) + 1)
                    nc.vector.reciprocal(p_rec[:], p_sum[:]).then_inc(s_lc, 1)
                    if left >= 1:
                        maximum(t + 1, 1 - i)
                    dve.wait_ge(s_en, after(t))
                    dve.wait_ge(s_lc, 2 * after(t))
                    dve.wait_ge(s_et, after(t - 1))
                    nc.vector.tensor_tensor(enc[:], pE.rearrange("p (h d) -> p h d", d=HD),
                                            p_rec[:].unsqueeze(2).to_broadcast([P, H, HD]), ALU.mult).then_inc(s_ec, 1)
                    if left >= 1:
                        shift(t + 1, 1 - i)
                    if left >= 2:
                        place_values(t + 2, i)
                    row = x_all[:, bass.ds(t, 1), :].rearrange("p a d -> p (a d)")
                    dve.wait_ge(s_o, after(t))
                    nc.vector.tensor_tensor(row, row, pG, ALU.add).then_inc(s_x2, 1)
                place_values(0, 0)
                place_values(1, 1)
                maximum(0, 0)
                shift(0, 0)
                pipelined(dve, step)
        s3.close()
        sa.close()
        layer_norm("second")

        E = a["gate"].shape[1]
        F = a["down"].shape[0]
        NE = a["member"].shape[0] // PARTS
        SH = NE - E
        NF = -(-F // P)
        rows = [min(P, F - f * P) for f in range(NF)]
        TB = 4
        NBLK = QT // TB
        SCALE = 2.5
        assert NF % 2 == 0
        mo = ExitStack()
        wg_sb = sb("wg_sb", [P, DC, F], F32, mo)
        wu_sb = sb("wu_sb", [P, DC, F], F32, mo)
        wd_sb = sb("wd_sb", [P, NF, D], F32, mo)
        member = sb("member", [PARTS * NE, F], BF16, mo)
        wT = sb("wT", [PARTS * NE, QT * P], BF16, mo)
        gate_sb = sb("gate_sb", [P, DC, E], F32, mo)
        zT = sb("zT", [P, DC, QT, P], F32, mo)
        score = sb("score", [P, QT, E], F32, mo)
        weight = sb("weight", [P, QT, NE], F32, mo)

        r1 = ExitStack()
        z_n = [sb(f"z_n{i}", [P, D], F32, r1) for i in range(2)]
        before = sb("before", [P, E, E], F32, r1)
        gt = sb("gt", [P, QT, E, E], F32, r1)
        eq = sb("eq", [P, QT, E, E], F32, r1)
        rank = sb("rank", [P, QT, E], F32, r1)
        chosen = sb("chosen", [P, QT, E], F32, r1)
        total = sb("total", [P, QT], F32, r1)
        total_r = sb("total_r", [P, QT], F32, r1)
        pZ = [ps(f"pZ{i}", [P, DC, P], F32, r1) for i in range(2)]
        member_f = sb("member_f", [PARTS * NE, F], F32, r1)
        w_low = sb("w_low", [P, QT, NE], F32, r1)
        w_parts = sb("w_parts", [P, QT, PARTS, NE], BF16, r1)
        pR = ps("pR", [P, QT, E], F32, r1)
        pW = ps("pW", [P, QT * P], BF16, r1)
        s_gw = sem("router_weights_loaded", mo)
        s_mw = sem("moe_weights_loaded", mo)
        s_zn = sem("moe_normalised", r1)
        s_zt = sem("moe_transposed", r1)
        s_zc = sem("moe_transposed_copied", r1)
        s_r = sem("router_logits_ready", r1)
        s_sc = sem("router_scores_ready", r1)
        s_rt = sem("router_steps", r1)
        s_bf = sem("order_mask", r1)
        s_wp = sem("weight_parts_ready", r1)
        s_wt = sem("weights_transposed", r1)
        with nc.Block() as block:
            @block.sync
            def _(sp):
                sp.dma_start(gate_sb[:], a["gate"].rearrange("(c p) n -> p c n", p=P)).then_inc(s_gw, 16)
                for dst, src in ((wg_sb, a["up_gate"]), (wu_sb, a["up"])):
                    sp.dma_start(dst[:], src.rearrange("(c p) n -> p c n", p=P)).then_inc(s_mw, 16)
                sp.dma_start(member_f[:], a["member"]).then_inc(s_mw, 16)
                whole = F // P
                sp.dma_start(wd_sb[:, 0:whole, :], a["down"][0:whole * P, :].rearrange("(c p) n -> p c n", p=P)
                             ).then_inc(s_mw, 16)
                sp.dma_start(wd_sb[0:rows[-1], NF - 1, :], a["down"][(NF - 1) * P:F, :]).then_inc(s_mw, 16)

            @block.gpsimd
            def _(pool):
                nc.gpsimd.memset(before[:], 1.0).then_inc(s_bf, 1)
                pool.wait_ge(s_bf, 1)
                nc.gpsimd.affine_select(out=before[:], in_=before[:], compare_op=ALU.is_ge, fill=0.0, base=-1,
                                        pattern=[[1, E], [-1, E]], channel_multiplier=0).then_inc(s_bf, 1)

            @block.tensor
            def _(pe):
                def turn(t, i):
                    pe.wait_ge(s_zn, t + 1)
                    for c in range(DC):
                        mm = nc.tensor.transpose(pZ[i][:, c, :], z_n[i][:, c * P:(c + 1) * P], ident[:])
                    mm.then_inc(s_zt, 1)
                pe.wait_ge(s_gw, 16)
                for t in range(QT):
                    if t >= 2:
                        pe.wait_ge(s_zc, t - 1)
                    turn(t, t % 2)
                    if t >= 1:
                        pe.wait_ge(s_zc, t)
                        for c in range(DC):
                            nc.tensor.matmul(pR[:, t - 1, :], zT[:, c, t - 1, :], gate_sb[:, c, :],
                                             start=c == 0, stop=c == DC - 1)
                pe.wait_ge(s_zc, QT)
                for c in range(DC):
                    mm = nc.tensor.matmul(pR[:, QT - 1, :], zT[:, c, QT - 1, :], gate_sb[:, c, :],
                                          start=c == 0, stop=c == DC - 1)
                mm.then_inc(s_r, 1)
                pe.wait_ge(s_wp, 1)
                for t in range(QT):
                    mm = nc.tensor.transpose(pW[0:PARTS * NE, t * P:(t + 1) * P],
                                             w_parts[:, t].rearrange("p r e -> p (r e)"), ident_h[:])
                mm.then_inc(s_wt, 1)

            @block.scalar
            def _(act):
                for t in range(QT):
                    act.wait_ge(s_zt, t + 1)
                    nc.scalar.copy(zT[:, :, t, :], pZ[t % 2][:]).then_inc(s_zc, 1)
                act.wait_ge(s_r, 1)
                nc.scalar.activation(score[:], pR[:], ACT.Sigmoid).then_inc(s_sc, 1)
                act.wait_ge(s_mw, 5 * 16)
                nc.scalar.copy(member[:], member_f[:])
                act.wait_ge(s_wt, 1)
                nc.scalar.copy(wT[:, 0:QT * P // 2], pW[0:PARTS * NE, 0:QT * P // 2])

            @block.vector
            def _(dve):
                done = [0]

                def link(ins):
                    done[0] += 1
                    ins.then_inc(s_rt, 1)
                    dve.wait_ge(s_rt, done[0])
                for t in range(QT):
                    if t >= 2:
                        dve.wait_ge(s_zt, t - 1)
                    nc.vector.tensor_scalar(z_n[t % 2][:], x_all[:, t, :], mean_var[:, t, 0:1], rstd[:, t:t + 1],
                                            ALU.subtract, ALU.mult).then_inc(s_zn, 1)
                mine = score[:].unsqueeze(3).to_broadcast([P, QT, E, E])
                other = score[:].unsqueeze(2).to_broadcast([P, QT, E, E])
                dve.wait_ge(s_sc, 1)
                dve.wait_ge(s_bf, 2)
                link(nc.vector.tensor_tensor(gt[:], other, mine, ALU.is_gt))
                link(nc.vector.tensor_tensor(eq[:], other, mine, ALU.is_equal))
                link(nc.vector.tensor_tensor(eq[:], eq[:], before[:].unsqueeze(1).to_broadcast([P, QT, E, E]),
                                             ALU.mult))
                link(nc.vector.tensor_tensor(gt[:], gt[:], eq[:], ALU.add))
                link(nc.vector.tensor_reduce(rank[:], gt[:], AX.X, ALU.add))
                link(nc.vector.tensor_scalar(rank[:], rank[:], 1.5, None, ALU.is_lt))
                link(nc.vector.tensor_tensor(chosen[:], score[:], rank[:], ALU.mult))
                link(nc.vector.tensor_reduce(total[:], chosen[:], AX.X, ALU.add))
                link(nc.vector.tensor_scalar(total[:], total[:], 1e-20, None, ALU.add))
                link(nc.vector.reciprocal(total_r[:], total[:]))
                link(nc.vector.tensor_tensor(chosen[:], chosen[:], total_r[:].unsqueeze(2).to_broadcast([P, QT, E]),
                                             ALU.mult))
                nc.vector.memset(weight[:, :, 0:SH], 1.0)
                link(nc.vector.tensor_scalar(weight[:, :, SH:NE], chosen[:], SCALE, None, ALU.mult))
                link(nc.vector.tensor_copy(w_parts[:, :, 0, :], weight[:]))
                link(nc.vector.tensor_tensor(w_low[:], weight[:], w_parts[:, :, 0, :], ALU.subtract))
                link(nc.vector.tensor_copy(w_parts[:, :, 1, :], w_low[:]))
                nc.vector.tensor_tensor(w_parts[:, :, 2, :], w_low[:], w_parts[:, :, 1, :],
                                        ALU.subtract).then_inc(s_wp, 1)
                dve.wait_ge(s_wt, 1)
                nc.vector.tensor_copy(wT[:, QT * P // 2:QT * P], pW[0:PARTS * NE, QT * P // 2:QT * P])
        r1.close()

        m2 = ExitStack()
        h_gate = [sb(f"h_gate{i}", [P, TB * P], F32, m2) for i in range(2)]
        h_up = [sb(f"h_up{i}", [P, TB * P], F32, m2) for i in range(2)]
        hidden = sb("hidden", [P, NF, TB * P], F32, m2)
        pGt = [ps(f"pGt{i}", [P, TB * P], F32, m2) for i in range(2)]
        pUp = [ps(f"pUp{i}", [P, TB * P], F32, m2) for i in range(2)]
        pWt = [ps(f"pWt{i}", [P, TB * P], F32, m2) for i in range(2)]
        pDn = [ps(f"pDn{i}", [P, D], F32, m2) for i in range(2)]
        s_up = sem("up_products_ready", m2)
        s_si = sem("gate_activated", m2)
        s_hu = sem("gated_ready", m2)
        s_h = sem("hidden_ready", m2)
        s_d = sem("down_product_ready", m2)
        s_a = sem("experts_added", m2)
        s_out = sem("output_stored", m2)
        with nc.Block() as block:
            @block.tensor
            def _(pe):
                for s in (s_up, s_d):
                    pe.sem_inc(s, START)

                def up(blk, f, i):
                    n = blk * NF + f
                    cols, r = slice(f * P, f * P + rows[f]), rows[f]
                    pe.wait_ge(s_h, after(n - 2))
                    for dst, w in ((pGt[i], wg_sb), (pUp[i], wu_sb)):
                        for c in range(DC):
                            nc.tensor.matmul(dst[0:r, :], w[:, c, cols],
                                             zT[:, c, bass.ds(blk * TB, TB), :].rearrange("p t n -> p (t n)"),
                                             start=c == 0, stop=c == DC - 1)
                    nc.tensor.matmul(pWt[i][0:r, :], member[:, cols], wT[:, bass.ds(blk * TB * P, TB * P)],
                                     start=True, stop=True).then_inc(s_up, 1)

                def down(blk, t):
                    m = blk * TB + t
                    pe.wait_ge(s_a, after(m - 2))
                    for f in range(NF):
                        if t == 0 and f >= NF - 2:
                            pe.wait_ge(s_h, after(blk * NF + f))
                        mm = nc.tensor.matmul(pDn[t % 2], hidden[0:rows[f], f, t * P:(t + 1) * P],
                                              wd_sb[0:rows[f], f, :], start=f == 0, stop=f == NF - 1)
                    mm.then_inc(s_d, 1)
                with pe.Fori(0, NBLK) as blk:
                    for f in range(NF):
                        up(blk, f, f % 2)
                    for t in range(TB):
                        down(blk, t)

            @block.scalar
            def _(act):
                act.sem_inc(s_si, START)
                with act.Fori(0, NBLK) as blk:
                    for f in range(NF):
                        n = blk * NF + f
                        act.wait_ge(s_up, after(n))
                        act.wait_ge(s_hu, after(n - 2))
                        nc.scalar.activation(h_gate[f % 2][0:rows[f], :], pGt[f % 2][0:rows[f], :],
                                             ACT.Silu).then_inc(s_si, 1)

            @block.vector
            def _(dve):
                for s in (s_hu, s_h, s_a):
                    dve.sem_inc(s, START)

                def gated(blk, f, i):
                    dve.wait_ge(s_si, after(blk * NF + f))
                    dve.wait_ge(s_h, after(blk * NF + f - 2))
                    nc.vector.tensor_tensor(h_up[i][0:rows[f], :], h_gate[i][0:rows[f], :], pUp[i][0:rows[f], :],
                                            ALU.mult).then_inc(s_hu, 1)

                def weighted(blk, f, i):
                    dve.wait_ge(s_hu, after(blk * NF + f))
                    dve.wait_ge(s_d, after(blk * TB - 1))
                    nc.vector.tensor_tensor(hidden[0:rows[f], f, :], h_up[i][0:rows[f], :], pWt[i][0:rows[f], :],
                                            ALU.mult).then_inc(s_h, 1)
                with dve.Fori(0, NBLK) as blk:
                    for f in range(NF):
                        gated(blk, f, f % 2)
                        weighted(blk, f, f % 2)
                    for t in range(TB):
                        m = blk * TB + t
                        row = x_all[:, bass.ds(m, 1), :].rearrange("p a d -> p (a d)")
                        dve.wait_ge(s_d, after(m))
                        nc.vector.tensor_tensor(row, row, pDn[t % 2], ALU.add).then_inc(s_a, 1)

            @block.sync
            def _(sp):
                with sp.Fori(0, NBLK) as blk:
                    sp.wait_ge(s_a, after(TB * (blk + 1) - 1))
                    sp.dma_start(out_t[:, bass.ds(blk * TB, TB), :], x_all[:, bass.ds(blk * TB, TB), :]
                                 ).then_inc(s_out, 16)
                sp.wait_ge(s_out, 16 * NBLK)
        m2.close()
        mo.close()


_INS = ["x", "L0_xattn_Wq", "L0_xattn_bq", "L0_xattn_Wkv", "L0_xattn_bkv", "L0_xattn_Wp", "L0_xattn_bp",
        "L0_attn_Wq", "L0_attn_Wk", "L0_attn_Wv", "L0_attn_Wout"]


def rope_table(batch=64):
    fraction = np.arange(0, HD, 2, dtype=np.float32) / np.float32(HD)
    timescale = (np.float32(10000.0) ** fraction).astype(np.float32)
    position = (np.arange(P) % batch).astype(np.float32)
    angle = position[:, None] * (np.float32(1.0) / timescale)[None, :]
    cos, sin = np.cos(angle), np.sin(angle)
    return np.stack([np.concatenate([cos, cos], 1), np.concatenate([-sin, sin], 1)], 1).astype(np.float32)


def lay_out(inputs):
    arrays = {name: np.ascontiguousarray(inputs[name]) for name in _INS}
    ctx = np.asarray(inputs["ctx_2048"])
    arrays["ctx_T"] = np.ascontiguousarray(ctx.reshape(-1, ctx.shape[-1]).T)
    arrays["rope"] = rope_table()
    arrays["gate"] = np.ascontiguousarray(np.asarray(inputs["L0_ffn_gate_w"]).T)

    def up(shared, experts):
        shared, experts = np.asarray(shared), np.asarray(experts)
        rows = np.concatenate([shared, experts.reshape(-1, experts.shape[-1])])
        return np.ascontiguousarray(rows.T)
    arrays["up_gate"] = up(inputs["L0_ffn_shared_wg"], inputs["L0_ffn_exp_wg"])
    arrays["up"] = up(inputs["L0_ffn_shared_wu"], inputs["L0_ffn_exp_wu"])
    shared, experts = np.asarray(inputs["L0_ffn_shared_wd"]), np.asarray(inputs["L0_ffn_exp_wd"])
    arrays["down"] = np.concatenate([shared.T, experts.transpose(0, 2, 1).reshape(-1, experts.shape[1])])
    hidden, width = arrays["down"].shape[0], experts.shape[2]
    of = np.arange(hidden) // width
    arrays["member"] = np.tile(of[None, :] == np.arange(hidden // width)[:, None], (3, 1)).astype(np.float32)
    return arrays


def kernel(**inputs):
    import concourse.bacc as _bacc
    from concourse.bass_utils import run_bass_kernel_spmd as _run

    nc = _bacc.Bacc("TRN2", target_bir_lowering=False, num_devices=1)
    arrays = lay_out(inputs)
    args = {n: nc.dram_tensor(f"in_{n}", v.shape, mybir.dt.from_np(v.dtype), kind="ExternalInput").ap()
            for n, v in arrays.items()}
    out = nc.dram_tensor("out_0", arrays["x"].shape, F32, kind="ExternalOutput").ap()
    build(nc, args, out)
    r = _run(nc, [{f"in_{n}": v for n, v in arrays.items()}], core_ids=[0])
    return r.results[0]["out_0"]
```
